# Optimizing a Trainium2 kernel written in Bass

```python
import numpy as np
import jax
import jax.numpy as jnp

def _softmax(x, axis=-1):
    return jax.nn.softmax(x, axis=axis)

def _gelu(x):
    return jax.nn.gelu(x, approximate=True)

def _silu(x):
    return jax.nn.silu(x)

def _sigmoid(x):
    return jax.nn.sigmoid(x)

def _layernorm(x, axis=-1, eps=1e-05):
    m = jnp.mean(x, axis=axis, keepdims=True)
    v = jnp.var(x, axis=axis, keepdims=True)
    return (x - m) / jnp.sqrt(v + eps)

def _scatter_add(tgt, idx, src, axis=0):
    return tgt.at[idx].add(src)

def _segment_sum(src, seg, n):
    return jax.ops.segment_sum(src, seg, n)
kernel_name = 'mk_adaln_d2_jaxref_r8_ebb0d4'

def setup_inputs(seed: int=0):
    np.random.seed(seed)
    _w = jnp.asarray

    def _L0_attn_setup():
        import jax, jax.numpy as jnp
        import numpy as np
        B, N, D, H = (2, 256, 128, 16)
        DH = D // H
        EPS = 1e-05

        def _lrpe(t, theta, n):
            idx = jnp.arange(n, dtype=t.dtype).reshape(1, n, 1)
            th = theta * idx
            return jnp.concatenate([t * jnp.cos(th), t * jnp.sin(th)], axis=-1)
        key = jax.random.key(seed)
        ks = jax.random.split(key, 8)
        x = jax.random.normal(ks[0], (B, N, D), dtype=jnp.float32)
        context = jax.random.normal(ks[1], (B, N, D), dtype=jnp.float32)
        Wqkvu = jax.random.normal(ks[2], (4 * D, D), dtype=jnp.float32) * 0.02
        bqkvu = jax.random.normal(ks[3], (4 * D,), dtype=jnp.float32) * 0.02
        Wout = jax.random.normal(ks[4], (D, D), dtype=jnp.float32) * 0.02
        bout = jax.random.normal(ks[5], (D,), dtype=jnp.float32) * 0.02
        theta = (10000.0 ** (-2.0 / D * jnp.arange(D, dtype=jnp.float32))).reshape(H, 1, DH)
        ln_w = jnp.ones((D,), dtype=jnp.float32)
        ln_b = jnp.zeros((D,), dtype=jnp.float32)
        return {'x': x, 'context': context, 'Wqkvu': Wqkvu, 'bqkvu': bqkvu, 'Wout': Wout, 'bout': bout, 'theta': theta, 'ln_w': ln_w, 'ln_b': ln_b}
    _L0_attn_in = _L0_attn_setup()

    def _L0_ffn_setup():
        import jax, jax.numpy as jnp
        import numpy as np
        D = 128
        H = 512
        E = 8
        TOPK = 2
        CAP_F = 1.25
        key = jax.random.key(seed)
        ks = jax.random.split(key, 6)
        sc = 0.02
        return {'x': jax.random.normal(ks[0], (4, 256, D), jnp.float32), 'Wg': jax.random.normal(ks[1], (D, E), jnp.float32) * sc, 'bg': jnp.zeros((E,), jnp.float32), 'W1': jax.random.normal(ks[2], (E, D, H), jnp.float32) * sc, 'W2': jax.random.normal(ks[3], (E, D, H), jnp.float32) * sc, 'W3': jax.random.normal(ks[4], (E, H, D), jnp.float32) * sc}
    _L0_ffn_in = _L0_ffn_setup()
    _L0_c = _w((lambda *s: np.random.randn(*s).astype(np.float32) * 0.05)(4, 128))
    _L0_wmod = _w((lambda *s: np.random.randn(*s).astype(np.float32) * 0.05)(128, 6 * 128) * 128 ** (-0.5))

    def _L1_attn_setup():
        import math
        import jax, jax.numpy as jnp
        import numpy as np
        NHEAD = 16
        HEAD_DIM = 64
        D_MODEL = 128
        B, T = (2, 512)

        def _cosformer(x, Wq, bq, Wk, bk, Wv, bv, Wo, bo):
            Bsz, Tlen, _ = x.shape
            H, dh = (NHEAD, HEAD_DIM)
            Q = (x @ Wq + bq).reshape(Bsz, Tlen, H, dh)
            K = (x @ Wk + bk).reshape(Bsz, Tlen, H, dh)
            V = (x @ Wv + bv).reshape(Bsz, Tlen, H, dh)
            Qp = jax.nn.relu(Q)
            Kp = jax.nn.relu(K)
            angles = math.pi / (2.0 * Tlen) * jnp.arange(Tlen, dtype=jnp.float32)
            cosw = jnp.cos(angles)[None, :, None, None]
            sinw = jnp.sin(angles)[None, :, None, None]
            Qc, Qs = (Qp * cosw, Qp * sinw)
            Kc, Ks = (Kp * cosw, Kp * sinw)
            tm = lambda a: jnp.moveaxis(a, 1, 0)
            Qc, Qs, Kc, Ks, Vt = (tm(Qc), tm(Qs), tm(Kc), tm(Ks), tm(V))
            S0 = jnp.zeros((Bsz, H, dh, dh), dtype=x.dtype)
            z0 = jnp.zeros((Bsz, H, dh), dtype=x.dtype)

            def step(carry, inp):
                S_cos, S_sin, z_cos, z_sin = carry
                qc, qs, kc, ks_, v = inp
                S_cos = S_cos + kc[..., :, None] * v[..., None, :]
                S_sin = S_sin + ks_[..., :, None] * v[..., None, :]
                z_cos = z_cos + kc
                z_sin = z_sin + ks_
                num = jnp.einsum('bhi,bhij->bhj', qc, S_cos) + jnp.einsum('bhi,bhij->bhj', qs, S_sin)
                den = jnp.sum(qc * z_cos + qs * z_sin, axis=-1)
                den = jnp.maximum(den, 1e-06)[..., None]
                return ((S_cos, S_sin, z_cos, z_sin), num / den)
            _, out = jax.lax.scan(step, (S0, S0, z0, z0), (Qc, Qs, Kc, Ks, Vt))
            out = jnp.moveaxis(out, 0, 1).reshape(Bsz, Tlen, H * dh)
            return out @ Wo + bo
        key = jax.random.key(seed)
        ks = jax.random.split(key, 9)
        HD = NHEAD * HEAD_DIM
        s_in = 1.0 / math.sqrt(D_MODEL)
        s_out = 1.0 / math.sqrt(HD)
        return {'x': jax.random.normal(ks[0], (B, T, D_MODEL), dtype=jnp.float32), 'Wq': jax.random.normal(ks[1], (D_MODEL, HD), dtype=jnp.float32) * s_in, 'bq': jnp.zeros((HD,), dtype=jnp.float32), 'Wk': jax.random.normal(ks[2], (D_MODEL, HD), dtype=jnp.float32) * s_in, 'bk': jnp.zeros((HD,), dtype=jnp.float32), 'Wv': jax.random.normal(ks[3], (D_MODEL, HD), dtype=jnp.float32) * s_in, 'bv': jnp.zeros((HD,), dtype=jnp.float32), 'Wo': jax.random.normal(ks[4], (HD, D_MODEL), dtype=jnp.float32) * s_out, 'bo': jnp.zeros((D_MODEL,), dtype=jnp.float32)}
    _L1_attn_in = _L1_attn_setup()

    def _L1_ffn_setup():
        import jax, jax.numpy as jnp
        import numpy as np
        HIDDEN = 128
        N_ROUTED = 16
        N_SHARED = 2
        TOP_K = 2
        MID_R = HIDDEN // 4
        MID_S = HIDDEN // 2
        key = jax.random.key(seed)
        ks = jax.random.split(key, 8)
        s = 0.02
        return {'x': jax.random.normal(ks[0], (2, 128, HIDDEN), dtype=jnp.float32), 'router_w': jax.random.normal(ks[1], (HIDDEN, N_ROUTED), dtype=jnp.float32) * s, 'wg_r': jax.random.normal(ks[2], (N_ROUTED, HIDDEN, MID_R), dtype=jnp.float32) * s, 'wu_r': jax.random.normal(ks[3], (N_ROUTED, HIDDEN, MID_R), dtype=jnp.float32) * s, 'wd_r': jax.random.normal(ks[4], (N_ROUTED, MID_R, HIDDEN), dtype=jnp.float32) * s, 'wg_s': jax.random.normal(ks[5], (N_SHARED, HIDDEN, MID_S), dtype=jnp.float32) * s, 'wu_s': jax.random.normal(ks[6], (N_SHARED, HIDDEN, MID_S), dtype=jnp.float32) * s, 'wd_s': jax.random.normal(ks[7], (N_SHARED, MID_S, HIDDEN), dtype=jnp.float32) * s}
    _L1_ffn_in = _L1_ffn_setup()
    _L1_c = _w((lambda *s: np.random.randn(*s).astype(np.float32) * 0.05)(4, 128))
    _L1_wmod = _w((lambda *s: np.random.randn(*s).astype(np.float32) * 0.05)(128, 6 * 128) * 128 ** (-0.5))
    _d = {'L0_attn_x': _L0_attn_in['x'], 'L0_attn_context': _L0_attn_in['context'], 'L0_attn_Wqkvu': _L0_attn_in['Wqkvu'], 'L0_attn_bqkvu': _L0_attn_in['bqkvu'], 'L0_attn_Wout': _L0_attn_in['Wout'], 'L0_attn_bout': _L0_attn_in['bout'], 'L0_attn_theta': _L0_attn_in['theta'], 'L0_attn_ln_w': _L0_attn_in['ln_w'], 'L0_attn_ln_b': _L0_attn_in['ln_b'], 'L0_ffn_Wg': _L0_ffn_in['Wg'], 'L0_ffn_bg': _L0_ffn_in['bg'], 'L0_ffn_W1': _L0_ffn_in['W1'], 'L0_ffn_W2': _L0_ffn_in['W2'], 'L0_ffn_W3': _L0_ffn_in['W3'], 'L0_c': _L0_c, 'L0_wmod': _L0_wmod, 'L1_attn_Wq': _L1_attn_in['Wq'], 'L1_attn_bq': _L1_attn_in['bq'], 'L1_attn_Wk': _L1_attn_in['Wk'], 'L1_attn_bk': _L1_attn_in['bk'], 'L1_attn_Wv': _L1_attn_in['Wv'], 'L1_attn_bv': _L1_attn_in['bv'], 'L1_attn_Wo': _L1_attn_in['Wo'], 'L1_attn_bo': _L1_attn_in['bo'], 'L1_ffn_router_w': _L1_ffn_in['router_w'], 'L1_ffn_wg_r': _L1_ffn_in['wg_r'], 'L1_ffn_wu_r': _L1_ffn_in['wu_r'], 'L1_ffn_wd_r': _L1_ffn_in['wd_r'], 'L1_ffn_wg_s': _L1_ffn_in['wg_s'], 'L1_ffn_wu_s': _L1_ffn_in['wu_s'], 'L1_ffn_wd_s': _L1_ffn_in['wd_s'], 'L1_c': _L1_c, 'L1_wmod': _L1_wmod}
    _x0 = _d['L0_attn_x']
    _d['L0_attn_x'] = jax.random.normal(jax.random.fold_in(jax.random.key(seed), 1), (4, 1024, 128), dtype=_x0.dtype)
    del _x0
    return _d

def reference(L0_attn_x, L0_attn_context, L0_attn_Wqkvu, L0_attn_bqkvu, L0_attn_Wout, L0_attn_bout, L0_attn_theta, L0_attn_ln_w, L0_attn_ln_b, L0_ffn_Wg, L0_ffn_bg, L0_ffn_W1, L0_ffn_W2, L0_ffn_W3, L0_c, L0_wmod, L1_attn_Wq, L1_attn_bq, L1_attn_Wk, L1_attn_bk, L1_attn_Wv, L1_attn_bv, L1_attn_Wo, L1_attn_bo, L1_ffn_router_w, L1_ffn_wg_r, L1_ffn_wu_r, L1_ffn_wd_r, L1_ffn_wg_s, L1_ffn_wu_s, L1_ffn_wd_s, L1_c, L1_wmod):

    def _L0_attn_ref(x, context, Wqkvu, bqkvu, Wout, bout, theta, ln_w, ln_b):
        import jax, jax.numpy as jnp
        import numpy as np
        B, N, D, H = (2, 256, 128, 16)
        DH = D // H
        EPS = 1e-05

        def _lrpe(t, theta, n):
            idx = jnp.arange(n, dtype=t.dtype).reshape(1, n, 1)
            th = theta * idx
            return jnp.concatenate([t * jnp.cos(th), t * jnp.sin(th)], axis=-1)
        b, n, d = x.shape
        qkvu = x @ Wqkvu.T + bqkvu
        q, k, v, u = jnp.split(qkvu, 4, axis=-1)
        tohead = lambda t: t.reshape(b, n, H, DH).transpose(0, 2, 1, 3)
        q, k, v = (tohead(q), tohead(k), tohead(v))
        q = jax.nn.silu(q)
        k = jax.nn.silu(k)
        q = _lrpe(q, theta, n)
        k = _lrpe(k, theta, n)
        qk = jnp.einsum('bhmd,bhnd->bhmn', q, k)
        out = jnp.einsum('bhmn,bhne->bhme', qk, v)
        out = out.transpose(0, 2, 1, 3).reshape(b, n, d)
        mu = jnp.mean(out, axis=-1, keepdims=True)
        var = jnp.var(out, axis=-1, keepdims=True)
        out = (out - mu) * jax.lax.rsqrt(var + EPS) * ln_w + ln_b
        out = u * out
        return out @ Wout.T + bout

    def _L0_ffn_ref(x, Wg, bg, W1, W2, W3):
        import jax, jax.numpy as jnp
        import numpy as np
        D = 128
        H = 512
        E = 8
        TOPK = 2
        CAP_F = 1.25
        b, s, d = x.shape
        xt = x.reshape(-1, d)
        T = xt.shape[0]
        capacity = int(T / E * CAP_F)
        gate_logits = xt @ Wg + bg
        top_v, top_i = jax.lax.top_k(gate_logits, TOPK)
        expert_label = jax.nn.one_hot(top_i, E, dtype=xt.dtype).sum(axis=1)
        seq = jnp.cumsum(expert_label, axis=0) * expert_label
        valid = (seq > 0) & (seq <= capacity)
        slot = (seq - 1.0).astype(jnp.int32)
        flat_idx = jnp.where(valid, jnp.arange(E, dtype=jnp.int32)[None, :] * capacity + slot, E * capacity)
        src = jnp.broadcast_to(xt[:, None, :], (T, E, d)).reshape(-1, d)
        buf = jnp.zeros((E * capacity + 1, d), xt.dtype).at[flat_idx.reshape(-1)].set(src)
        disp = buf[:-1].reshape(E, capacity, d)
        h = jax.nn.silu(jnp.einsum('ecd,edh->ech', disp, W1)) * jnp.einsum('ecd,edh->ech', disp, W2)
        out = jnp.einsum('ech,ehd->ecd', h, W3)
        out_flat = jnp.concatenate([out.reshape(E * capacity, d), jnp.zeros((1, d), xt.dtype)], axis=0)
        all_expert_output = out_flat[flat_idx]
        sel = jnp.take_along_axis(all_expert_output, top_i[:, :, None], axis=1)
        routing_w = jax.nn.softmax(top_v, axis=-1)
        y = (routing_w[:, :, None] * sel).sum(axis=1)
        return y.reshape(b, s, d)

    def _L1_attn_ref(x, Wq, bq, Wk, bk, Wv, bv, Wo, bo):
        import math
        import jax, jax.numpy as jnp
        import numpy as np
        NHEAD = 16
        HEAD_DIM = 64
        D_MODEL = 128
        B, T = (2, 512)

        def _cosformer(x, Wq, bq, Wk, bk, Wv, bv, Wo, bo):
            Bsz, Tlen, _ = x.shape
            H, dh = (NHEAD, HEAD_DIM)
            Q = (x @ Wq + bq).reshape(Bsz, Tlen, H, dh)
            K = (x @ Wk + bk).reshape(Bsz, Tlen, H, dh)
            V = (x @ Wv + bv).reshape(Bsz, Tlen, H, dh)
            Qp = jax.nn.relu(Q)
            Kp = jax.nn.relu(K)
            angles = math.pi / (2.0 * Tlen) * jnp.arange(Tlen, dtype=jnp.float32)
            cosw = jnp.cos(angles)[None, :, None, None]
            sinw = jnp.sin(angles)[None, :, None, None]
            Qc, Qs = (Qp * cosw, Qp * sinw)
            Kc, Ks = (Kp * cosw, Kp * sinw)
            tm = lambda a: jnp.moveaxis(a, 1, 0)
            Qc, Qs, Kc, Ks, Vt = (tm(Qc), tm(Qs), tm(Kc), tm(Ks), tm(V))
            S0 = jnp.zeros((Bsz, H, dh, dh), dtype=x.dtype)
            z0 = jnp.zeros((Bsz, H, dh), dtype=x.dtype)

            def step(carry, inp):
                S_cos, S_sin, z_cos, z_sin = carry
                qc, qs, kc, ks_, v = inp
                S_cos = S_cos + kc[..., :, None] * v[..., None, :]
                S_sin = S_sin + ks_[..., :, None] * v[..., None, :]
                z_cos = z_cos + kc
                z_sin = z_sin + ks_
                num = jnp.einsum('bhi,bhij->bhj', qc, S_cos) + jnp.einsum('bhi,bhij->bhj', qs, S_sin)
                den = jnp.sum(qc * z_cos + qs * z_sin, axis=-1)
                den = jnp.maximum(den, 1e-06)[..., None]
                return ((S_cos, S_sin, z_cos, z_sin), num / den)
            _, out = jax.lax.scan(step, (S0, S0, z0, z0), (Qc, Qs, Kc, Ks, Vt))
            out = jnp.moveaxis(out, 0, 1).reshape(Bsz, Tlen, H * dh)
            return out @ Wo + bo
        return _cosformer(x, Wq, bq, Wk, bk, Wv, bv, Wo, bo)

    def _L1_ffn_ref(x, router_w, wg_r, wu_r, wd_r, wg_s, wu_s, wd_s):
        import jax, jax.numpy as jnp
        import numpy as np
        HIDDEN = 128
        N_ROUTED = 16
        N_SHARED = 2
        TOP_K = 2
        MID_R = HIDDEN // 4
        MID_S = HIDDEN // 2
        orig_shape = x.shape
        flat = x.reshape(-1, orig_shape[-1])
        gs = jnp.einsum('td,ndm->tnm', flat, wg_s)
        us = jnp.einsum('td,ndm->tnm', flat, wu_s)
        out = jnp.einsum('tnm,nmd->td', jax.nn.silu(gs) * us, wd_s)
        logits = (flat @ router_w).astype(jnp.float32)
        probs = jax.nn.softmax(logits, axis=-1)
        weights, indices = jax.lax.top_k(probs, TOP_K)
        weights = weights / (weights.sum(axis=-1, keepdims=True) + 1e-09)
        weights = weights.astype(x.dtype)
        comb = jnp.sum(jax.nn.one_hot(indices, N_ROUTED, dtype=x.dtype) * weights[..., None], axis=1)
        g = jnp.einsum('td,edm->tem', flat, wg_r)
        u = jnp.einsum('td,edm->tem', flat, wu_r)
        h = jax.nn.silu(g) * u
        h = h * comb[:, :, None]
        out = out + jnp.einsum('tem,emd->td', h, wd_r)
        return out.reshape(orig_shape)
    x = L0_attn_x
    mod = (_silu(L0_c) @ L0_wmod).reshape(L0_c.shape[0], 6, 1, -1)
    sa, ca, ga, sb, cb, gb = (mod[:, 0], mod[:, 1], mod[:, 2], mod[:, 3], mod[:, 4], mod[:, 5])
    ga = (2 * (ga >= 0) - 1) * jnp.maximum(jnp.abs(ga), 0.25)
    gb = (2 * (gb >= 0) - 1) * jnp.maximum(jnp.abs(gb), 0.25)
    h = _layernorm(x, axis=-1) * (1 + ca) + sa
    x = x + ga * _L0_attn_ref(h, L0_attn_context, L0_attn_Wqkvu, L0_attn_bqkvu, L0_attn_Wout, L0_attn_bout, L0_attn_theta, L0_attn_ln_w, L0_attn_ln_b)
    h = _layernorm(x, axis=-1) * (1 + cb) + sb
    x = x + gb * _L0_ffn_ref(h, L0_ffn_Wg, L0_ffn_bg, L0_ffn_W1, L0_ffn_W2, L0_ffn_W3)
    mod = (_silu(L1_c) @ L1_wmod).reshape(L1_c.shape[0], 6, 1, -1)
    sa, ca, ga, sb, cb, gb = (mod[:, 0], mod[:, 1], mod[:, 2], mod[:, 3], mod[:, 4], mod[:, 5])
    ga = (2 * (ga >= 0) - 1) * jnp.maximum(jnp.abs(ga), 0.25)
    gb = (2 * (gb >= 0) - 1) * jnp.maximum(jnp.abs(gb), 0.25)
    h = _layernorm(x, axis=-1) * (1 + ca) + sa
    x = x + ga * _L1_attn_ref(h, L1_attn_Wq, L1_attn_bq, L1_attn_Wk, L1_attn_bk, L1_attn_Wv, L1_attn_bv, L1_attn_Wo, L1_attn_bo)
    h = _layernorm(x, axis=-1) * (1 + cb) + sb
    x = x + gb * _L1_ffn_ref(h, L1_ffn_router_w, L1_ffn_wg_r, L1_ffn_wu_r, L1_ffn_wd_r, L1_ffn_wg_s, L1_ffn_wu_s, L1_ffn_wd_s)
    return x

_drawn_inputs = setup_inputs


def setup_inputs(seed=0):
    import zlib

    import numpy as np

    out = dict(_drawn_inputs(seed))
    spreads = {'L0_attn_ln_w': (1.0, 0.6),
     'L0_attn_ln_b': (0.0, 0.8),
     'L0_ffn_bg': (0.0, 0.8),
     'L1_attn_bq': (0.0, 0.8),
     'L1_attn_bk': (0.0, 0.8),
     'L1_attn_bv': (0.0, 0.295),
     'L1_attn_bo': (0.0, 0.342)}
    factors = {'L0_attn_Wqkvu': 4.146,
     'L0_attn_bqkvu': 8.0,
     'L0_attn_Wout': 4.102,
     'L0_attn_bout': 8.0,
     'L0_attn_theta': 5.881,
     'L0_ffn_Wg': 8.0,
     'L0_ffn_W1': 8.0,
     'L0_ffn_W2': 8.0,
     'L0_ffn_W3': 8.0,
     'L0_c': 3.776,
     'L0_wmod': 3.918,
     'L1_attn_Wq': 7.808,
     'L1_attn_Wk': 6.658,
     'L1_ffn_router_w': 8.0,
     'L1_ffn_wg_r': 8.0,
     'L1_ffn_wu_r': 8.0,
     'L1_ffn_wd_r': 8.0,
     'L1_ffn_wg_s': 8.0,
     'L1_ffn_wu_s': 8.0,
     'L1_ffn_wd_s': 8.0}
    for name, (base, spread) in spreads.items():
        noise = np.random.default_rng([zlib.crc32(name.encode()), seed]).standard_normal(out[name].shape)
        drawn = base * np.exp(spread * noise) if base else spread * noise
        out[name] = jnp.asarray(drawn.astype(out[name].dtype))
    for name, factor in factors.items():
        out[name] = (out[name] * factor).astype(out[name].dtype)
    return out
```

```python
from contextlib import ExitStack

import numpy as np

import concourse.bass as bass
from concourse import mybir
from concourse.alu_op_type import AluOpType as ALU

ACT = mybir.ActivationFunctionType
F32 = mybir.dt.float32
F32R = mybir.dt.float32r
I32 = mybir.dt.int32
AX = mybir.AxisListType

P = 128
B, T, D = 4, 1024, 128
TB = T // P
NT = B * TB
G4 = 4
EPS = 1e-5
E0, H0 = 8, 512
CAP = int(B * T / E0 * 1.25)
ST = CAP // P
NSLOT = E0 * CAP
NH, DH = 16, 64
HD = NH * DH
HG = 4
NG = NH // HG
E1, MR = 16, 32
NS, MS = 2, 64
MB = E1 * MR // P
TWO_PI = 6.283185307179586
C1 = 6.28125
C2 = float(np.float32(round((TWO_PI - C1) * 2.0**20) / 2.0**20))
C3 = float(TWO_PI - C1 - C2)
ROUND = 12582912.0
PI32 = 3.1415925


class Engine:

    def __init__(self, name, eng, sem):
        self.name, self.eng, self.sem = name, eng, sem
        self.base, self.k, self.per = 0, 0, 0

    def inc(self, ins):
        ins.then_inc(self.sem, 1)
        self.k += 1
        return self


class Sync:

    def __init__(self, nc, ctx):
        self.nc = nc
        mk = lambda n, e: Engine(n, e, ctx.enter_context(nc.semaphore(f"done_{n}")))
        self.pe, self.act = mk("pe", nc.tensor), mk("act", nc.scalar)
        self.dve, self.pool = mk("dve", nc.vector), mk("pool", nc.gpsimd)
        self.all = [self.pe, self.act, self.dve, self.pool]
        self.marks, self.waited = {}, {}
        self.turn = 0

    def mark(self, name, e):
        self.marks[name] = (e, self.turn, e.k, e.base if isinstance(e.base, int) else None)

    def did(self, name, e, ins):
        e.inc(ins)
        self.mark(name, e)

    def value(self, name):
        e, turn, k, base = self.marks[name]
        rolled = not isinstance(e.base, int)
        if turn == self.turn:
            return e, ((1, k) if rolled else (0, e.base + k))
        if rolled and turn == self.turn - 1:
            return e, (1, k - e.per)
        return e, (0, base + k)

    def need(self, waiter, *names, apart=False):
        latest = {}
        for name in names:
            if name in self.marks:
                e, v = self.value(name)
                latest[e.name] = max(latest.get(e.name, (e, v)), (e, v), key=lambda x: x[1])
        waits = []
        for e, v in latest.values():
            key = (id(waiter), e.name)
            turn, done = self.waited.get(key, (-1, (0, 0)))
            if turn == self.turn and done >= v:
                continue
            self.waited[key] = (self.turn, v)
            waits.append((e.sem, e.base + v[1] if v[0] else v[1]))
        if apart and any(not isinstance(value, int) for _, value in waits):
            waits = [(sem, value if isinstance(value, int) else waiter.to_reg(value)) for sem, value in waits]
            waiter.wait_ge(next(e.sem for e in self.all if e.eng is waiter), 1)
        for sem, value in waits:
            waiter.wait_ge(sem, value)

    def need_apart(self, waiter, *names):
        self.need(waiter, *names, apart=True)

    def loop(self, first, last, body):
        def counted(n):
            self.turn += 1
            before = [e.k for e in self.all]
            body(n)
            return [e.k - b for e, b in zip(self.all, before)]
        for e in self.all:
            e.base += e.k
            e.k = 0
        got = counted(first)
        for e, g in zip(self.all, got):
            e.per = g
        start = [e.base + g for e, g in zip(self.all, got)]
        with self.nc.Fori(first + 1, last) as n:
            for e, s in zip(self.all, start):
                e.base, e.k = n * e.per + (s - (first + 1) * e.per), 0
            again = counted(n)
            assert again == got, (got, again)
        for e, s in zip(self.all, start):
            e.base, e.k = s + (last - first - 1) * e.per, 0
        self.turn += 1
        for m, (e, turn, k, base) in list(self.marks.items()):
            if turn == self.turn - 1 and base is None:
                self.marks[m] = (e, turn, k - e.per, e.base)


def rows(ap, count):
    p, w = ap.shape
    return ap.unsqueeze(1).to_broadcast([p, count, w])


class Kernel:

    def __init__(self, nc, ctx, io):
        self.nc, self.ctx, self.io = nc, ctx, io
        self.mem, self.outer, self.scratch = ctx, [], {}
        self.s = Sync(nc, ctx)
        self.pe, self.act, self.dve, self.pool, self.sp = nc.tensor, nc.scalar, nc.vector, nc.gpsimd, nc.sync
        self.bank = [ctx.enter_context(nc.psum_tensor(f"bank{i}", [P, 512], F32)) for i in range(8)]
        self.dma_sems, self.dma_total = {}, {}

    def sb(self, name, shape, dt=F32):
        return self.mem.enter_context(self.nc.sbuf_tensor(f"sb_{name}", shape, dt))

    def phase(self):
        self.outer.append(self.mem)
        self.mem = ExitStack()
        self.scratch = {}

    def end_phase(self):
        for waiter in (self.pe, self.act, self.dve, self.pool, self.sp):
            for e in self.s.all:
                waiter.wait_ge(e.sem, e.base + e.k)
        self.mem.close()
        self.mem = self.outer.pop()
        self.scratch = {}

    def V(self, name, ins):
        self.s.did(name, self.s.dve, ins)

    def S(self, name, ins):
        self.s.did(name, self.s.act, ins)

    def M(self, name, ins):
        self.s.did(name, self.s.pe, ins)

    def GP(self, name, ins):
        self.s.did(name, self.s.pool, ins)

    def load(self, name, out, in_, queue=None):
        sem = self.ctx.enter_context(self.nc.semaphore(f"dma_{name}"))
        self.dma_sems[name] = sem
        self.dma_total[name] = 16
        (queue or self.sp).dma_start(out, in_).then_inc(sem, 16)

    def loaded(self, waiter, *names):
        for name in names:
            waiter.wait_ge(self.dma_sems[name], self.dma_total[name])

    def stats(self, tag, tiles, buf):
        v, need, V = self.dve, self.s.need, self.V
        st, mv, y, h, t = buf
        n = len(tiles)
        for i, x in enumerate(tiles):
            ins = v.bn_stats(st[:, i, :], x)
        V(f"{tag}.st", ins)
        self.s.need_apart(v, f"{tag}.st")
        for i in range(n):
            ins = v.bn_aggr(mv[:, i, :], st[:, i, :])
        V(f"{tag}.mv", ins)
        need(v, f"{tag}.mv")
        V(f"{tag}.v", v.tensor_scalar(t[:, 0:n], mv[:, 0:n, 1], EPS, None, ALU.add))
        V(f"{tag}.h", v.tensor_scalar(h[:, 0:n], mv[:, 0:n, 1], EPS, -0.5, ALU.add, ALU.mult))
        need(v, f"{tag}.v")
        V(f"{tag}.y0", v.tensor_scalar(y[:, 0:n].bitcast(I32), t[:, 0:n].bitcast(I32), -0.5, 1597463007.0,
                                       ALU.mult, ALU.add))
        for _ in range(4):
            need(v, f"{tag}.y0")
            V(f"{tag}.t", v.tensor_tensor(t[:, 0:n], y[:, 0:n], y[:, 0:n], ALU.mult))
            need(v, f"{tag}.t")
            V(f"{tag}.t", v.tensor_tensor(t[:, 0:n], t[:, 0:n], h[:, 0:n], ALU.mult))
            need(v, f"{tag}.t")
            V(f"{tag}.y0", v.scalar_tensor_tensor(y[:, 0:n], t[:, 0:n], 1.5, y[:, 0:n], ALU.add, ALU.mult))
        need(v, f"{tag}.y0")

    def normed(self, name, out, x, i, buf):
        _, mv, y, _, _ = buf
        self.V(name, self.dve.tensor_scalar(out, x, mv[:, i, 0:1], y[:, i:i + 1], ALU.subtract, ALU.mult))

    def stat_buffers(self, tag, n):
        return (self.sb(f"{tag}_st", [P, n, 6]), self.sb(f"{tag}_mv", [P, n, 2]), self.sb(f"{tag}_y", [P, n]),
                self.sb(f"{tag}_h", [P, n]), self.sb(f"{tag}_t", [P, n]))

    def setup(self):
        nc, io, v, s, pe = self.nc, self.io, self.dve, self.s, self.pe
        need, V, S, M = s.need, self.V, self.S, self.M
        sb = self.sb
        self.X = sb("x", [P, NT, D])
        self.cols = sb("cols", [P, io["cols"].shape[1]])
        self.consts = sb("consts", [P, io["consts"].shape[1]])
        self.rowsb = sb("rows", [P, io["rows"].shape[1]])
        self.mT = [sb(f"mt{i}", [P, 6, B]) for i in range(2)]
        self.mB = [sb(f"mb{i}", [P, B, 6, D]) for i in range(2)]
        self.w0 = [sb(f"w0_{k}", [P, NT]) for k in range(2)]
        self.slot = [sb(f"slot{k}", [P, NT], I32) for k in range(2)]
        self.e_w12 = sb("e_w12", [P, 2, 2, H0])
        self.e_w3 = sb("e_w3", [P, 2, H0 // P, D])
        self.phase()
        self.H2 = sb("h2", [P, NT, D])
        self.LG = sb("lg", [P, NT, E0])
        self.phase()
        self.wmod = [sb(f"wmod{i}", [P, 6 * D]) for i in range(2)]
        self.W0 = sb("w0", [P, 4 * D])
        self.WoT = sb("wo0", [P, D])
        self.load("cols", self.cols[:], io["cols"])
        self.load("consts", self.consts[:], io["consts"])
        self.load("wmod0", self.wmod[0][:], io["wmod0"], self.act)
        for b in range(B):
            self.load(f"x{b}", self.X[:, b * TB:(b + 1) * TB, :],
                      io["x"][b].rearrange("(c p) d -> p c d", p=P), self.act if b % 2 else self.sp)
            if b == 0:
                self.load("rows", self.rowsb[:], io["rows"].to_broadcast([P, io["rows"].shape[1]]))
                self.load("w0", self.W0[:], io["w0"], self.act)
        self.load("wo0", self.WoT[:], io["wo0"])
        self.load("wmod1", self.wmod[1][:], io["wmod1"], self.act)
        at = 0
        self.c = {}
        for name, w in CONSTS:
            self.c[name] = self.consts[:, at:at + w]
            at += w
        at = 0
        for name, w in COLS:
            self.c[name] = self.cols[:, at:at + w]
            at += w
        at = 0
        for name, w in ROWS:
            self.c[name] = self.rowsb[:, at:at + w]
            at += w
        self.zero = sb("zero", [P, 10 * D])
        self.GP("zero", self.pool.memset(self.zero[:], 0.0))
        self.disp = nc.dram_tensor("disp", [NSLOT, D], F32).ap()
        self.eout = nc.dram_tensor("eout", [NSLOT + 1, D], F32).ap()
        need(self.sp, "zero")
        sem = self.ctx.enter_context(nc.semaphore("dma_zeroed"))
        self.dma_sems["zeroed"] = sem
        self.dma_total["zeroed"] = 5 * 16
        part = NSLOT // 4
        for i in range(4):
            self.sp.dma_start(self.disp[i * part:(i + 1) * part, :].rearrange("(p a) d -> p (a d)", p=P),
                              self.zero[:]).then_inc(sem, 16)
        self.sp.dma_start(self.eout[NSLOT:NSLOT + 1, :], self.zero[0:1, 0:D]).then_inc(sem, 16)

        self.sc = sb("sc", [P, 2, B])
        self.scB = sb("scb", [P, B, P])
        self.loaded(self.act, "cols")
        S("sc", self.act.activation(self.sc[:], self.c["cT"].rearrange("p (l b) -> p l b", l=2), ACT.Silu))
        for lay in range(2):
            self.modulations(lay)

    def modulations(self, lay):
        v, s, pe, act = self.dve, self.s, self.pe, self.act
        need, V, S, M = s.need, self.V, self.S, self.M
        w, mT, mB = self.wmod[lay], self.mT[lay], self.mB[lay]
        need(v, "sc", "mod.mm")
        V("mod.scB", v.tensor_copy(self.scB[:], self.sc[:, lay, :].unsqueeze(2).to_broadcast([P, B, P])))
        self.loaded(pe, f"wmod{lay}")
        need(pe, "sc", "mod.evT")
        for j in range(6):
            ins = pe.matmul(self.bank[0][:, j * B:(j + 1) * B], w[:, j * D:(j + 1) * D], self.sc[:, lay, :],
                            start=True, stop=True)
        M("mod.T", ins)
        need(act, "mod.T")
        S("mod.evT", act.copy(mT[:], self.bank[0][:, 0:6 * B].rearrange("p (j b) -> p j b", j=6)))
        need(pe, "mod.scB")
        for b in range(B):
            k = 1 + 2 * (b % 2)
            need(pe, f"mod.evB{b % 2}")
            pe.matmul(self.bank[k][:, :], self.scB[:, b, :], w[:, 0:512], start=True, stop=True)
            M("mod.mm", pe.matmul(self.bank[k + 1][:, 0:256], self.scB[:, b, :], w[:, 512:768],
                                  start=True, stop=True))
            need(act, "mod.mm")
            act.copy(mB[:, b, 0:4, :].rearrange("p j d -> p (j d)"), self.bank[k][:, :])
            S(f"mod.evB{b % 2}", act.copy(mB[:, b, 4:6, :].rearrange("p j d -> p (j d)"),
                                          self.bank[k + 1][:, 0:256]))
        need(v, "mod.evT", "mod.evB0", "mod.evB1")
        for j in (1, 4):
            v.tensor_scalar(mT[:, j, :], mT[:, j, :], 1.0, None, ALU.add)
        V("mod.one", v.tensor_scalar(mB[:, :, 4, :], mB[:, :, 4, :], 1.0, None, ALU.add))
        for j in (2, 5):
            g = mB[:, :, j, :]
            t = self.scr(f"gate{j}", [P, B, D])
            V("mod.sg", v.tensor_scalar(t[:], g, 0.0, 2.0, ALU.is_ge, ALU.mult))
            V("mod.ab", v.scalar_tensor_tensor(g, g, -1.0, g, ALU.mult, ALU.max))
            need(v, "mod.ab")
            V("mod.sg", v.tensor_scalar(t[:], t[:], -1.0, None, ALU.add))
            need(v, "mod.sg")
            V("mod.g", v.scalar_tensor_tensor(g, g, 0.25, t[:], ALU.max, ALU.mult))
        s.mark(f"mod{lay}", s.dve)

    def scr(self, name, shape):
        if name not in self.scratch:
            self.scratch[name] = self.sb(name, shape)
        return self.scratch[name]

    def rotation(self):
        v, s, pe, act = self.dve, self.s, self.pe, self.act
        need, V, S, M = s.need, self.V, self.S, self.M
        th = self.sb("th", [P, TB, D])
        cnt = self.sb("cnt", [P, TB, D])
        self.tokT = [self.sb(f"tokt{k}", [P, TB, D]) for k in range(2)]
        self.dimT = [self.sb(f"dimt{k}", [P, T]) for k in range(2)]
        self.loaded(v, "rows")
        self.loaded(v, "consts")
        for c in range(TB):
            ins = v.tensor_scalar(th[:, c, :], self.c["theta"], self.c["pos"][:, c:c + 1], None, ALU.mult)
        V("th", ins)
        for k, (turn, shift) in enumerate(((0.25, TWO_PI / 4), (0.0, 0.0))):
            r = self.tokT[k]
            need(v, "th", "rot.r")
            V("rot.n", v.tensor_scalar(cnt[:], th[:], 1.0 / TWO_PI, turn, ALU.mult, ALU.add))
            need(v, "rot.n")
            V("rot.n", v.tensor_scalar(cnt[:], cnt[:], ROUND, None, ALU.add))
            need(v, "rot.n")
            V("rot.n", v.tensor_scalar(cnt[:], cnt[:], ROUND, None, ALU.subtract))
            need(v, "rot.n")
            V("rot.r", v.scalar_tensor_tensor(r[:], cnt[:], -C1, th[:], ALU.mult, ALU.add))
            for cc in (C2, C3):
                need(v, "rot.r")
                V("rot.r", v.scalar_tensor_tensor(r[:], cnt[:], -cc, r[:], ALU.mult, ALU.add))
            need(v, "rot.r")
            V("rot.r", v.tensor_scalar(r[:], r[:], shift, None, ALU.add))
            need(v, "rot.r")
            V("rot.n", v.tensor_scalar(cnt[:], r[:], 1.0 / TWO_PI, ROUND, ALU.mult, ALU.add))
            need(v, "rot.n")
            V("rot.n", v.tensor_scalar(cnt[:], cnt[:], ROUND, None, ALU.subtract))
            need(v, "rot.n")
            V("rot.r", v.scalar_tensor_tensor(r[:], cnt[:], -TWO_PI, r[:], ALU.mult, ALU.add))
            need(v, "rot.r")
            V("rot.r", v.tensor_scalar(r[:], r[:], -PI32, PI32, ALU.max, ALU.min))
            need(act, "rot.r")
            S(f"tok{k}", act.activation(r[:], r[:], ACT.Sin))
            for half in range(2):
                bk = self.bank[5 + half]
                need(pe, f"tok{k}", f"rot.ev{half}")
                for i in range(4):
                    ins = pe.transpose(bk[:, i * P:(i + 1) * P], r[:, 4 * half + i, :], self.c["ident"])
                M("rot.tr", ins)
                need(v, "rot.tr")
                V(f"rot.ev{half}", v.tensor_copy(self.dimT[k][:, half * 512:(half + 1) * 512], bk[:, :]))
        s.mark("rotation", s.dve)

    def l0_buffers(self):
        sb = self.sb
        self.qT = sb("q_t", [P, NT * P])
        self.uT = sb("u_t", [P, NT * P])
        self.xn = sb("xn", [P, G4, D])
        self.hT = sb("h_t", [P, G4 * P])
        self.kv = sb("kv", [P, G4, 2 * D])
        self.kr = [sb(f"kr{k}", [P, G4, D]) for k in range(2)]
        self.KVa = sb("kva", [P, 2, D])
        self.KVm = sb("kvm", [P, 2, D])
        self.qr = [sb(f"qr{k}", [P, G4 * P]) for k in range(2)]
        self.on = sb("on", [P, G4, D])
        self.oT = sb("o_t", [P, G4 * P])
        self.hm = sb("hm", [P, G4, D])
        self.h2T = sb("h2_t", [P, G4 * P])
        self.wog = sb("wog", [P, D])
        self.gbo = sb("gbo", [P, D])
        self.stA, self.stB, self.stC = (self.stat_buffers(f"s{x}", G4) for x in "abc")
        self.Wg = sb("wg0", [P, E0])
        self.load("wg0", self.Wg[:], self.io["wg0"])

    def l0_keys(self, b, half):
        v, s, pe, act, bank = self.dve, self.s, self.pe, self.act, self.bank
        need, V, S, M = s.need, self.V, self.S, self.M
        n0 = b * TB + half * G4
        tiles = [self.X[:, n0 + i, :] for i in range(G4)]
        self.stats("ln1", tiles, self.stA)
        need(v, "l0.xT")
        for i in range(G4):
            ins_name = "l0.xn"
            self.normed(ins_name, self.xn[:, i, :], tiles[i], i, self.stA)
        need(pe, "l0.xn", "l0.hT")
        for i in range(G4):
            ins = pe.transpose(bank[0][:, i * P:(i + 1) * P], self.xn[:, i, :], self.c["ident"])
        M("l0.xT", ins)
        self.s.need_apart(act, "l0.xT", "l0.kvmm")
        S("l0.hT", act.activation(self.hT[:], bank[0][:, :], ACT.Identity, scale=at1(self.mT[0][:, 1, :], b),
                                  bias=at1(self.mT[0][:, 0, :], b)))
        need(pe, "l0.hT", "l0.q", "l0.u")
        M("l0.qmm", pe.matmul(bank[1][:, :], self.W0[:, 0:D], self.hT[:], start=True, stop=True))
        M("l0.umm", pe.matmul(bank[2][:, :], self.W0[:, 3 * D:4 * D], self.hT[:], start=True, stop=True))
        sl = tokens(n0, G4)
        self.s.need_apart(act, "l0.qmm")
        S("l0.q", act.activation(self.qT[:, sl], bank[1][:, :], ACT.Silu, bias=self.c["bq"]))
        self.s.need_apart(act, "l0.umm")
        S("l0.u", act.activation(self.uT[:, sl], bank[2][:, :], ACT.Identity, bias=self.c["bu"]))
        for j in range(2):
            need(pe, f"l0.kv{j}")
            for i in range(2):
                t = 2 * j + i
                ins = pe.matmul(bank[3 + j][:, i * 256:(i + 1) * 256], self.hT[:, t * P:(t + 1) * P],
                                self.W0[:, D:3 * D], start=True, stop=True)
            M("l0.kvmm", ins)
            need(v, "l0.kvmm", "l0.state", "l0.ks")
            V(f"l0.kv{j}", v.tensor_tensor(self.kv[:, 2 * j:2 * j + 2, :],
                                           bank[3 + j][:, :].rearrange("p (a b) -> p a b", a=2),
                                           rows(self.c["bkv"], 2), ALU.add))
        need(act, "l0.kv1", "l0.kr")
        S("l0.ks", act.activation(self.kv[:, :, 0:D], self.kv[:, :, 0:D], ACT.Silu))
        need(v, "l0.ks", "l0.state")
        for k in range(2):
            V("l0.kr", v.tensor_tensor(self.kr[k][:], self.kv[:, :, 0:D], self.tokT[k][:, 4 * half:4 * half + 4, :],
                                       ALU.mult))
        need(pe, "l0.kr", "l0.kva")
        for k in range(2):
            for i in range(G4):
                ins = pe.matmul(bank[5][:, k * D:(k + 1) * D], self.kr[k][:, i, :], self.kv[:, i, D:2 * D],
                                start=(i == 0), stop=(i == G4 - 1))
        M("l0.state", ins)
        need(v, "l0.state", "l0.kvm")
        both = bank[5][:, 0:2 * D].rearrange("p (k d) -> p k d", k=2)
        if half == 0:
            V("l0.kva", v.tensor_copy(self.KVa[:], both))
        else:
            V("l0.kva", v.tensor_tensor(self.KVa[:], self.KVa[:], both, ALU.add))

    def l0_close_state(self):
        need, v = self.s.need, self.dve
        need(v, "l0.kva", "l0.omm")
        self.V("l0.kvm", v.tensor_tensor(self.KVm[:], self.KVa[:], rows(self.c["headmask"], 2), ALU.mult))

    def l0_out_weights(self, b):
        need, v = self.s.need, self.dve
        g = self.mB[0][:, b, 2, :]
        need(v, "l0.ymm", "l0.x")
        v.tensor_tensor(self.wog[:], self.WoT[:], g, ALU.mult)
        self.V("l0.wog", v.tensor_tensor(self.gbo[:], self.c["bout"], g, ALU.mult))

    def l0_queries(self, b, half):
        v, s, pe, act, bank = self.dve, self.s, self.pe, self.act, self.bank
        need, V, S, M = s.need, self.V, self.S, self.M
        n0 = b * TB + half * G4
        sl = tokens(n0, G4)
        need(v, "l0.q", "l0.omm")
        for k in range(2):
            V("l0.qr", v.tensor_tensor(self.qr[k][:], self.qT[:, sl], self.dimT[k][:, half * 512:half * 512 + 512],
                                       ALU.mult))
        need(pe, "l0.qr", "l0.kvm", "l0.x")
        for i in range(G4):
            for k in range(2):
                ins = pe.matmul(bank[6][:, i * P:(i + 1) * P], self.qr[k][:, i * P:(i + 1) * P], self.KVm[:, k, :],
                                start=(k == 0), stop=(k == 1))
        M("l0.omm", ins)
        need(v, "l0.omm")
        self.stats("ln2", [bank[6][:, i * P:(i + 1) * P] for i in range(G4)], self.stB)
        need(v, "l0.onT")
        for i in range(G4):
            self.normed("l0.on", self.on[:, i, :], bank[6][:, i * P:(i + 1) * P], i, self.stB)
        need(pe, "l0.on", "l0.h2T")
        for i in range(G4):
            ins = pe.transpose(bank[7][:, i * P:(i + 1) * P], self.on[:, i, :], self.c["ident"])
        M("l0.onT", ins)
        need(act, "l0.onT", "l0.ymm")
        S("l0.oT", act.activation(self.oT[:], bank[7][:, :], ACT.Identity, scale=self.c["lnw"], bias=self.c["lnb"]))
        need(v, "l0.oT", "l0.u")
        V("l0.ou", v.tensor_tensor(self.oT[:], self.oT[:], self.uT[:, sl], ALU.mult))
        need(pe, "l0.ou", "l0.wog")
        for i in range(G4):
            ins = pe.matmul(bank[6][:, i * P:(i + 1) * P], self.oT[:, i * P:(i + 1) * P], self.wog[:],
                            start=True, stop=True)
        M("l0.ymm", ins)
        xs = self.X[:, bass.ds(n0, G4), :]
        need(v, "l0.ymm")
        V("l0.xa", v.tensor_tensor(xs, bank[6][:, :].rearrange("p (a b) -> p a b", a=G4), xs, ALU.add))
        need(v, "l0.xa", "l0.wog")
        V("l0.x", v.tensor_tensor(xs, xs, rows(self.gbo[:], G4), ALU.add))
        self.s.need_apart(v, "l0.x", "l0.H2", "l0.h2mm")
        tiles = [self.X[:, n0 + i, :] for i in range(G4)]
        self.stats("ln3", tiles, self.stC)
        for i in range(G4):
            self.normed("l0.hn", self.hm[:, i, :], tiles[i], i, self.stC)
        need(v, "l0.hn")
        V("l0.hc", v.tensor_tensor(self.hm[:], self.hm[:], rows(self.mB[0][:, b, 4, :], G4), ALU.mult))
        need(v, "l0.hc")
        V("l0.h2", v.tensor_tensor(self.hm[:], self.hm[:], rows(self.mB[0][:, b, 3, :], G4), ALU.add))
        need(act, "l0.h2")
        S("l0.H2", act.copy(self.H2[:, bass.ds(n0, G4), :], self.hm[:]))
        need(pe, "l0.h2", "l0.oT")
        for i in range(G4):
            ins = pe.transpose(bank[7][:, i * P:(i + 1) * P], self.hm[:, i, :], self.c["ident"])
        M("l0.h2mm", ins)
        need(act, "l0.h2mm", "l0.lgmm")
        S("l0.h2T", act.copy(self.h2T[:], bank[7][:, :]))
        need(pe, "l0.h2T", "l0.lg")
        for i in range(G4):
            ins = pe.matmul(bank[6][:, i * E0:(i + 1) * E0], self.h2T[:, i * P:(i + 1) * P], self.Wg[:],
                            start=True, stop=True)
        M("l0.lgmm", ins)
        need(v, "l0.lgmm")
        V("l0.lg", v.tensor_tensor(self.LG[:, bass.ds(n0, G4), :],
                                   bank[6][:, 0:G4 * E0].rearrange("p (a b) -> p a b", a=G4),
                                   rows(self.c["bg"], G4), ALU.add))
        s.mark("l0.x", s.dve)

    def layer0_attention(self):
        s = self.s
        self.l0_buffers()
        for b in range(B):
            self.loaded(self.dve, f"x{b}")
        self.loaded(self.pe, "w0", "consts", "wg0", "wo0")
        self.loaded(self.dve, "wo0")
        s.need(self.pe, "rotation")
        s.need(self.act, "mod0", "rotation")

        self.l0_keys(0, 0)
        self.l0_keys(0, 1)
        self.l0_close_state()

        def body(b):
            self.l0_out_weights(b)
            for half in range(2):
                self.l0_keys(b + 1, half)
                self.l0_queries(b, half)
            self.l0_close_state()

        s.loop(0, B - 1, body)
        self.l0_out_weights(B - 1)
        for half in range(2):
            self.l0_queries(B - 1, half)
        self.end_phase()

    def top2(self, tag, lg, oh, n, e, iota, top):
        v, need, V = self.dve, self.s.need, self.V
        wk = self.scr(f"{tag}_wk", [P, n, e])
        rest = self.scr(f"{tag}_rest", [P, n, e])
        idx = self.scr(f"{tag}_idx", [P, n])
        src = lg
        for k in range(2):
            V(f"{tag}.a", v.tensor_reduce(top[k], src, AX.X, ALU.max))
            need(v, f"{tag}.a")
            V(f"{tag}.a", v.tensor_tensor(wk[:], src, top[k].unsqueeze(2).to_broadcast([P, n, e]), ALU.is_equal))
            need(v, f"{tag}.a")
            V(f"{tag}.a", v.scalar_tensor_tensor(wk[:], wk[:], -64.0, rows(iota, n), ALU.mult, ALU.add))
            need(v, f"{tag}.a")
            V(f"{tag}.a", v.tensor_reduce(idx[:], wk[:], AX.X, ALU.min))
            need(v, f"{tag}.a")
            V(f"{tag}.a", v.tensor_scalar(idx[:], idx[:], 64.0, None, ALU.add))
            need(v, f"{tag}.a")
            V(f"{tag}.a", v.tensor_tensor(oh[k], rows(iota, n), idx[:].unsqueeze(2).to_broadcast([P, n, e]),
                                          ALU.is_equal))
            need(v, f"{tag}.a")
            if k == 0:
                V(f"{tag}.a", v.scalar_tensor_tensor(rest[:], oh[0], -3.0e38, lg, ALU.mult, ALU.add))
                need(v, f"{tag}.a")
                src = rest[:]

    def l0_routing(self):
        v, s, pe, act, bank = self.dve, self.s, self.pe, self.act, self.bank
        need, V, S, M, sb = s.need, self.V, self.S, self.M, self.sb
        oh = [sb(f"oh{k}", [P, NT, E0]) for k in range(2)]
        top = [sb(f"top{k}", [P, NT]) for k in range(2)]
        label, seq, pre, wk = (sb(f"rt_{x}", [P, NT, E0]) for x in ("label", "seq", "pre", "wk"))
        sf, sv = sb("rt_sf", [P, NT]), sb("rt_sv", [P, NT])
        need(v, "l0.lg")
        self.top2("t0", self.LG[:], [o[:] for o in oh], NT, E0, self.c["iota8"], [t[:] for t in top])
        V("r0.d", v.tensor_tensor(self.w0[1][:], top[1][:], top[0][:], ALU.subtract))
        V("r0.label", v.tensor_tensor(label[:], oh[0][:], oh[1][:], ALU.add))
        need(act, "r0.d")
        S("r0.e", act.activation(self.w0[1][:], self.w0[1][:], ACT.Exp))
        need(pe, "r0.label")
        flat = label[:].rearrange("p n e -> p (n e)")
        pe.matmul(bank[0][:, 0:NT * E0], self.c["upto"], flat, start=True, stop=True)
        M("r0.cum", pe.matmul(bank[1][:, 0:NT * E0], self.c["ones"], flat, start=True, stop=True))
        need(v, "r0.cum")
        tot = bank[1][:, 0:NT * E0].rearrange("p (n e) -> p n e", e=E0)
        V("r0.a", v.tensor_copy(pre[:], tot))
        need(v, "r0.a")
        a, b = pre, wk
        step = 1
        while step < NT:
            V("r0.a", v.tensor_copy(b[:, 0:step, :], a[:, 0:step, :]))
            V("r0.a", v.tensor_tensor(b[:, step:, :], a[:, step:, :], a[:, 0:NT - step, :], ALU.add))
            need(v, "r0.a")
            a, b = b, a
            step *= 2
        V("r0.a", v.tensor_tensor(seq[:], a[:], tot, ALU.subtract))
        need(v, "r0.a")
        V("r0.seq", v.tensor_tensor(seq[:], seq[:], bank[0][:, 0:NT * E0].rearrange("p (n e) -> p n e", e=E0),
                                    ALU.add))
        need(v, "r0.seq", "r0.e")
        V("r0.w", v.tensor_scalar(self.w0[0][:], self.w0[1][:], 1.0, None, ALU.add))
        need(v, "r0.w")
        V("r0.w", v.reciprocal(self.w0[0][:], self.w0[0][:]))
        need(v, "r0.w")
        V("r0.w", v.tensor_tensor(self.w0[1][:], self.w0[1][:], self.w0[0][:], ALU.mult))
        for k in range(2):
            V("r0.a", v.tensor_tensor(wk[:], seq[:], oh[k][:], ALU.mult))
            need(v, "r0.a")
            V("r0.a", v.tensor_reduce(sv[:], wk[:], AX.X, ALU.add))
            need(v, "r0.a")
            V("r0.a", v.tensor_tensor(wk[:], rows(self.c["iota8"], NT), oh[k][:], ALU.mult))
            need(v, "r0.a")
            V("r0.a", v.tensor_reduce(sf[:], wk[:], AX.X, ALU.add))
            need(v, "r0.a")
            V("r0.a", v.tensor_scalar(sf[:], sf[:], float(CAP), -1.0, ALU.mult, ALU.add))
            need(v, "r0.a")
            V("r0.a", v.tensor_tensor(sf[:], sf[:], sv[:], ALU.add))
            V("r0.b", v.tensor_scalar(sv[:], sv[:], float(CAP), None, ALU.is_le))
            need(v, "r0.a", "r0.b")
            V("r0.a", v.scalar_tensor_tensor(sf[:], sf[:], -float(NSLOT), sv[:], ALU.add, ALU.mult))
            need(v, "r0.a")
            V("r0.a", v.tensor_scalar(sf[:], sf[:], float(NSLOT), None, ALU.add))
            need(v, "r0.a")
            V(f"r0.slot{k}", v.tensor_copy(self.slot[k][:], sf[:]))
        g = self.pool
        need(g, "r0.slot0", "r0.slot1", "l0.H2")
        self.loaded(g, "zeroed")
        sem = self.ctx.enter_context(self.nc.semaphore("dma_dispatched"))
        self.dma_sems["dispatched"], self.dma_total["dispatched"] = sem, 2 * NT * 16
        for n in range(NT):
            for k in range(2):
                g.indirect_dma_start(out=self.disp, out_offset=bass.IndirectOffsetOnAxis(
                    ap=self.slot[k][:, n:n + 1], axis=0), in_=self.H2[:, n, :], in_offset=None,
                    bounds_check=NSLOT - 1, oob_is_err=False).then_inc(sem, 16)

    def l0_experts(self):
        nc, v, s, pe, act, bank, sp = self.nc, self.dve, self.s, self.pe, self.act, self.bank, self.sp
        need, V, S, M, sb, io = s.need, self.V, self.S, self.M, self.sb, self.io
        w12, w3 = self.e_w12, self.e_w3
        self.phase()
        xe = sb("e_x", [P, 2, ST, D])
        xT = sb("e_xt", [P, CAP])
        hs = sb("e_hs", [P, H0 // P, CAP])
        sg = sb("e_sg", [P, CAP])
        y = sb("e_y", [P, ST, D])
        sem = lambda n: self.ctx.enter_context(nc.semaphore(n))
        s_w = [sem(f"dma_expert_w{i}") for i in range(2)]
        s_x = [sem(f"dma_expert_x{i}") for i in range(2)]
        s_y = sem("dma_expert_y")
        HC = CAP // 2
        PAIRS = E0 // 2

        def load_weights(e, i):
            act.dma_start(w12[:, i, 0, :], io["w1"][e]).then_inc(s_w[i], 16)
            act.dma_start(w12[:, i, 1, :], io["w2"][e]).then_inc(s_w[i], 16)
            act.dma_start(w3[:, i, :, :], io["w3"][e].rearrange("(m p) d -> p m d", p=P)).then_inc(s_w[i], 16)

        def load_slots(e, i):
            sp.dma_start(xe[:, i, :, :], self.disp[bass.ds(e * CAP, CAP), :].rearrange("(a p) d -> p a d", p=P)
                         ).then_inc(s_x[i], 16)

        for i in range(2):
            load_weights(i, i)
        self.loaded(sp, "dispatched")
        for i in range(2):
            load_slots(i, i)

        def body(pair, last=False):
            for i in range(2):
                e = 2 * pair + i
                pe.wait_ge(s_x[i], (pair + 1) * 16)
                need(pe, "e.xT")
                for a in range(ST):
                    bk, col = (6, a) if a < 4 else (7, 0)
                    ins = pe.transpose(bank[bk][:, col * P:(col + 1) * P], xe[:, i, a, :], self.c["ident"])
                M("e.tr", ins)
                s.mark(f"e.tr{i}", s.pe)
                need(v, "e.tr", "e.mm")
                v.tensor_copy(xT[:, 0:512], bank[6][:, :])
                V("e.xT", v.tensor_copy(xT[:, 512:CAP], bank[7][:, 0:P]))
                pe.wait_ge(s_w[i], (pair + 1) * 48)
                need(pe, "e.xT")
                for m in range(H0 // P):
                    for half in range(2):
                        need(pe, f"e.h{half}")
                        cols = slice(half * HC, (half + 1) * HC)
                        pe.matmul(bank[2 * half][:, 0:HC], w12[:, i, 0, m * P:(m + 1) * P], xT[:, cols],
                                  start=True, stop=True)
                        M("e.mm", pe.matmul(bank[2 * half + 1][:, 0:HC], w12[:, i, 1, m * P:(m + 1) * P],
                                            xT[:, cols], start=True, stop=True))
                        need(act, "e.mm", f"e.h{half}")
                        S(f"e.sg{half}", act.activation(sg[:, cols], bank[2 * half][:, 0:HC], ACT.Silu))
                        need(v, f"e.sg{half}", "e.down")
                        V(f"e.h{half}", v.tensor_tensor(hs[:, m, cols], bank[2 * half + 1][:, 0:HC], sg[:, cols],
                                                        ALU.mult))
                need(pe, "e.h0", "e.h1")
                for a in range(ST):
                    bk, col = (4, a) if a < 4 else (5, 0)
                    need(pe, f"e.y{min(a, 4) // 4}")
                    for m in range(H0 // P):
                        ins = pe.matmul(bank[bk][:, col * P:(col + 1) * P], hs[:, m, a * P:(a + 1) * P],
                                        w3[:, i, m, :], start=(m == 0), stop=(m == H0 // P - 1))
                M("e.down", ins)
                s.mark(f"e.down{i}", s.pe)
                need(act, "e.down")
                if not isinstance(e, int) or e > 0:
                    act.wait_ge(s_y, e * 16)
                S("e.y0", act.copy(y[:, 0:4, :], bank[4][:, :].rearrange("p (a d) -> p a d", d=D)))
                S("e.y1", act.copy(y[:, 4, :], bank[5][:, 0:P]))
                need(sp, "e.y1")
                sp.dma_start(self.eout[bass.ds(e * CAP, CAP), :].rearrange("(a p) d -> p a d", p=P),
                             y[:]).then_inc(s_y, 16)
                if not last:
                    need(act, f"e.down{i}")
                    load_weights(e + 2, i)
                    need(sp, f"e.tr{i}")
                    load_slots(e + 2, i)

        s.loop(0, PAIRS - 1, body)
        body(PAIRS - 1, last=True)
        self.dma_sems["experts"], self.dma_total["experts"] = s_y, E0 * 16
        s.mark("experts", s.act)
        self.sp.wait_ge(s_y, E0 * 16)
        self.act.wait_ge(s_y, E0 * 16)
        self.end_phase()

    def l1_attention_setup(self):
        sb, io, g = self.sb, self.io, self.pool
        self.phase()
        self.WqD = sb("a_wq", [P, NH * P])
        self.Wk = sb("a_wk", [P, HD])
        self.Wv = sb("a_wv", [P, HD])
        self.Wo = sb("a_wo", [P, HD // P, D])
        self.csT = sb("a_cst", [P, NT * P])
        self.G = [sb(f"a_g{k}", [P, NT, D]) for k in range(2)]
        self.state = sb("a_state", [P, NH, DH + 1])
        self.load("wq1", self.WqD[:], io["wq1"], self.act)
        self.load("wk1", self.Wk[:], io["wk1"])
        self.load("wv1", self.Wv[:], io["wv1"], self.act)
        self.load("wo1", self.Wo[:], io["wo1"].rearrange("(m p) d -> p m d", p=P))
        self.load("cst", self.csT[:].rearrange("p (b t) -> p b t", b=B),
                  io["cst"].unsqueeze(1).to_broadcast([P, B, T]), self.act)
        ring = [self.ctx.enter_context(self.nc.semaphore(f"dma_gather{k}")) for k in range(4)]
        self.gathered = self.ctx.enter_context(self.nc.semaphore("gathered_tiles"))
        self.loaded(g, "experts")
        for n in range(NT + len(ring)):
            done = n - len(ring)
            if done >= 0:
                g.wait_ge(ring[done % len(ring)], 32 * (done // len(ring) + 1))
                g.sem_inc(self.gathered, 1)
            if n < NT:
                for k in range(2):
                    g.indirect_dma_start(out=self.G[k][:, n, :], out_offset=None, in_=self.eout,
                                         in_offset=bass.IndirectOffsetOnAxis(ap=self.slot[k][:, n:n + 1], axis=0)
                                         ).then_inc(ring[n % len(ring)], 16)
        self.Qp = sb("a_qp", [P, HG, P])
        self.Qr = [sb(f"a_qr{k}", [P, HG, P]) for k in range(2)]
        self.Kb = sb("a_kb", [P, HG, DH])
        self.Kr = [sb(f"a_kr{k}", [P, HG, P]) for k in range(2)]
        self.Va = [sb(f"a_va{k}", [P, HG, DH + 1]) for k in range(2)]
        self.KrT = [sb(f"a_krt{k}", [P, HG, P]) for k in range(2)]
        self.Sm = [sb(f"a_sm{k}", [P, HG, P]) for k in range(2)]
        self.den = sb("a_den", [P, HG])
        self.O = sb("a_o", [P, NH, DH])
        self.oT1 = sb("a_ot", [P, HD // P, P])
        self.hT1 = sb("a_ht", [P, P])
        self.xn1 = sb("a_xn", [P, D])
        self.mt1 = sb("a_mt", [P, D])
        self.yt1 = sb("a_yt", [P, D])
        self.st1 = self.stat_buffers("s1", 1)
        v = self.dve
        v.memset(self.Va[0][:], 1.0)
        v.memset(self.Va[1][:], 1.0)
        self.V("a.init", v.memset(self.state[:], 0.0))

    def a_pre(self, n):
        v, s, pe, act, bank = self.dve, self.s, self.pe, self.act, self.bank
        need, V, S, M = s.need, self.V, self.S, self.M
        x, b = self.X[:, n, :], n // TB
        v.wait_ge(self.gathered, n + 1)
        V("a.m", v.tensor_scalar(self.mt1[:], self.G[0][:, n, :], self.w0[0][:, bass.ds(n, 1)], None, ALU.mult))
        need(v, "a.m")
        V("a.m", v.scalar_tensor_tensor(self.mt1[:], self.G[1][:, n, :], self.w0[1][:, bass.ds(n, 1)], self.mt1[:],
                                        ALU.mult, ALU.add))
        need(v, "a.m")
        V("a.m", v.tensor_tensor(self.mt1[:], self.mt1[:], self.mB[0][:, b, 5, :], ALU.mult))
        need(v, "a.m")
        V("a.m", v.tensor_tensor(x, x, self.mt1[:], ALU.add))
        self.s.need_apart(v, "a.m")
        self.stats("lna", [x], self.st1)
        need(v, "a.xT")
        self.normed("a.xn", self.xn1[:], x, 0, self.st1)
        need(pe, "a.xn", "a.Yread")
        M("a.xT", pe.transpose(bank[6][:, 0:P], self.xn1[:], self.c["ident"]))

    def a_ready(self, n):
        act, b = self.act, n // TB
        self.s.need_apart(act, "a.xT", "a.kvmm")
        self.S("a.hT", act.activation(self.hT1[:], self.bank[6][:, 0:P], ACT.Identity,
                                      scale=at1(self.mT[1][:, 1, :], b), bias=at1(self.mT[1][:, 0, :], b)))

    def a_project(self, n, g):
        v, s, pe, act, bank = self.dve, self.s, self.pe, self.act, self.bank
        need, V, S, M = s.need, self.V, self.S, self.M
        i = g % 2
        need(pe, "a.hT", "a.Qp")
        for h in range(HG):
            ins = pe.matmul(bank[0][:, h * P:(h + 1) * P], self.WqD[:, (HG * g + h) * P:(HG * g + h + 1) * P],
                            self.hT1[:], start=True, stop=True)
        M("a.qmm", ins)
        need(pe, "a.Va0", "a.Va1")
        w = HG * DH
        pe.matmul(bank[1][:, 0:w], self.hT1[:], self.Wk[:, g * w:(g + 1) * w], start=True, stop=True)
        M("a.kvmm", pe.matmul(bank[1][:, w:2 * w], self.hT1[:], self.Wv[:, g * w:(g + 1) * w],
                              start=True, stop=True))
        need(act, "a.qmm", "a.Qr0", "a.Qr1")
        for h in range(HG):
            ins = act.activation(self.Qp[:, h, :], bank[0][:, h * P:(h + 1) * P], ACT.Relu,
                                 bias=self.c["bq1"][:, HG * g + h:HG * g + h + 1])
        S("a.Qp", ins)
        need(v, "a.kvmm", "a.Kr0", "a.Kr1")
        V("a.Kb", v.tensor_tensor(self.Kb[:].rearrange("p h d -> p (h d)"), bank[1][:, 0:w],
                                  self.c["bk1"][:, g * w:(g + 1) * w], ALU.add))
        need(v, f"a.U{i}", f"a.I{i}")
        V(f"a.Va{i}", v.tensor_tensor(self.Va[i][:, :, 0:DH],
                                      bank[1][:, w:2 * w].rearrange("p (h d) -> p h d", d=DH),
                                      self.c["bv1"][:, g * w:(g + 1) * w].rearrange("p (h d) -> p h d", d=DH),
                                      ALU.add))
        need(v, "a.Qp")
        V(f"a.Qr{i}", v.tensor_tensor(self.Qr[i][:], self.Qp[:], rows(self.csT[:, tokens(n, 1)], HG), ALU.mult))
        self.s.need_apart(act, "a.Kb", f"a.U{i}", f"a.KT{i}")
        for k in range(2):
            ins = act.activation(self.Kr[i][:, :, k * DH:(k + 1) * DH], self.Kb[:], ACT.Relu,
                                 scale=self.c[("cos1", "sin1")[k]][:, bass.ds(n, 1)])
        S(f"a.Kr{i}", ins)

    def a_keys_turned(self, n, g):
        pe, act, i = self.pe, self.act, g % 2
        need = self.s.need
        need(pe, f"a.Kr{i}", "a.KrT0", "a.KrT1")
        for h in range(HG):
            ins = pe.transpose(self.bank[2][:, h * P:(h + 1) * P], self.Kr[i][:, h, :], self.c["ident"])
        self.M(f"a.KT{i}", ins)
        need(act, f"a.KT{i}", f"a.S{i}")
        self.S(f"a.KrT{i}", act.copy(self.KrT[i][:], self.bank[2][:, :].rearrange("p (h t) -> p h t", h=HG)))

    def a_scores(self, n, g):
        v, s, pe, bank, i = self.dve, self.s, self.pe, self.bank, g % 2
        need, V, M = s.need, self.V, self.M
        need(pe, f"a.KrT{i}", f"a.Qr{i}", "a.Sm0", "a.Sm1")
        for h in range(HG):
            ins = pe.matmul(bank[3][:, h * P:(h + 1) * P], self.KrT[i][:, h, :], self.Qr[i][:, h, :],
                            start=True, stop=True)
        M(f"a.S{i}", ins)
        need(v, f"a.S{i}", f"a.I{i}")
        V(f"a.Sm{i}", v.tensor_tensor(self.Sm[i][:], bank[3][:, :].rearrange("p (h t) -> p h t", h=HG),
                                      rows(self.c["upto"], HG), ALU.mult))
        need(pe, f"a.Va{i}", f"a.Kr{i}", "a.state")
        for h in range(HG):
            ins = pe.matmul(bank[5][:, h * 65:(h + 1) * 65], self.Kr[i][:, h, :], self.Va[i][:, h, :],
                            start=True, stop=True)
        M(f"a.U{i}", ins)

    def a_values(self, n, g):
        v, s, pe, bank, i = self.dve, self.s, self.pe, self.bank, g % 2
        need, V, M = s.need, self.V, self.M
        need(pe, f"a.Sm{i}", "a.On", "a.state", "a.init")
        for h in range(HG):
            o = bank[4][:, h * 65:(h + 1) * 65]
            pe.matmul(o, self.Qr[i][:, h, :], self.state[:, HG * g + h, :], start=True, stop=False)
            ins = pe.matmul(o, self.Sm[i][:, h, :], self.Va[i][:, h, :], start=False, stop=True)
        M(f"a.I{i}", ins)
        need(v, f"a.I{i}")
        o4 = bank[4][:, 0:HG * 65].rearrange("p (h d) -> p h d", d=65)
        V("a.den", v.tensor_scalar(self.den[:], o4[:, :, DH], 1e-6, None, ALU.max))
        need(v, "a.den")
        V("a.den", v.reciprocal(self.den[:], self.den[:]))
        need(v, "a.den", f"a.oT{g % 2}")
        V("a.On", v.tensor_tensor(self.O[:, HG * g:HG * (g + 1), :], o4[:, :, 0:DH],
                                  self.den[:].unsqueeze(2).to_broadcast([P, HG, DH]), ALU.mult))
        st = self.state[:, HG * g:HG * (g + 1), :]
        V("a.stw", v.tensor_tensor(st, st, bank[5][:, 0:HG * 65].rearrange("p (h d) -> p h d", d=65), ALU.add))
        need(v, "a.stw")
        V("a.state", v.tensor_scalar(st, st, self.c["keep"][:, bass.ds(n, 1)], None, ALU.mult))

    def a_turned(self, g):
        pe, act, need = self.pe, self.act, self.s.need
        need(pe, "a.On", "a.oTc")
        for j in range(2):
            blk = 2 * g + j
            ins = pe.transpose(self.bank[7][:, j * P:(j + 1) * P],
                               self.O[:, 2 * blk:2 * blk + 2, :].rearrange("p h d -> p (h d)"), self.c["ident"])
        self.M(f"a.oT{g % 2}", ins)
        need(act, f"a.oT{g % 2}", "a.Y")
        self.S("a.oTc", act.copy(self.oT1[:, 2 * g:2 * g + 2, :],
                                 self.bank[7][:, 0:2 * P].rearrange("p (j t) -> p j t", j=2)))

    def a_output(self, n):
        v, s, pe, bank = self.dve, self.s, self.pe, self.bank
        need, V, M = s.need, self.V, self.M
        need(pe, "a.oTc", "a.hT", "a.Yread")
        for m in range(HD // P):
            ins = pe.matmul(bank[6][:, 0:D], self.oT1[:, m, :], self.Wo[:, m, :], start=(m == 0),
                            stop=(m == HD // P - 1))
        M("a.Y", ins)
        need(v, "a.Y")
        V("a.Yread", v.tensor_tensor(self.yt1[:], bank[6][:, 0:D], self.c["bo1"], ALU.add))
        need(v, "a.Yread")
        V("a.y", v.tensor_tensor(self.yt1[:], self.yt1[:], self.mB[1][:, n // TB, 2, :], ALU.mult))
        need(v, "a.y")
        x = self.X[:, n, :]
        V("a.x", v.tensor_tensor(x, x, self.yt1[:], ALU.add))

    def l1_attention(self):
        s = self.s
        self.l1_attention_setup()
        self.loaded(self.pe, "wq1", "wk1", "wv1", "wo1")
        self.loaded(self.dve, "cst")
        s.need(self.act, "mod1")

        def body(n, first=False, last=False):
            for g in range(NG):
                more = not (last and g == NG - 1)
                if more:
                    nn, gg = (n, g + 1) if g < NG - 1 else (n + 1, 0)
                    self.a_project(nn, gg)
                if not (first and g == 0):
                    self.a_turned((g - 1) % NG)
                self.a_scores(n, g)
                if more:
                    self.a_keys_turned(nn, gg)
                self.a_values(n, g)
                if g == 0 and not first:
                    self.a_output(n - 1)
                if g == 1 and not last:
                    self.a_pre(n + 1)
                if g == 2 and not last:
                    self.a_ready(n + 1)

        self.a_pre(0)
        self.a_ready(0)
        self.a_project(0, 0)
        self.a_keys_turned(0, 0)
        body(0, first=True)
        s.loop(1, NT - 1, body)
        body(NT - 1, last=True)
        self.a_turned(NG - 1)
        self.a_output(NT - 1)
        self.end_phase()

    def l1_moe(self):
        s = self.s
        io, sb = self.io, self.sb
        self.phase()
        self.Wgu = sb("m_wgu", [P, 2, (MB + 1) * P])
        self.Wd = sb("m_wd", [P, MB + 1, D])
        self.Wr = sb("m_wr", [P, E1])
        self.load("wgu", self.Wgu[:], io["wgu"], self.act)
        self.load("wr", self.Wr[:], io["wr"])
        self.load("wd", self.Wd[:], io["wd"].rearrange("(m p) d -> p m d", p=P))
        self.ex_in = sb("m_ex0", [2 * E1, MB * P])
        self.load("expand", self.ex_in[:], io["expand"], self.act)
        self.ex = sb("m_ex", [2 * E1, MB * P], F32R)
        self.h3T = sb("m_h3t", [P, NT * P])
        self.lg1 = sb("m_lg", [P, NT, E1])
        self.xn3 = sb("m_xn", [P, G4, D])
        self.hl3 = sb("m_hl", [P, G4, P])
        self.st3 = self.stat_buffers("s3", G4)
        self.sg3 = [sb(f"m_sg{k}", [P, G4 * P]) for k in range(2)]
        self.hd3 = [sb(f"m_hd{k}", [P, G4 * P]) for k in range(MB + 1)]
        self.comb = sb("m_comb", [P, NT, 2, E1], F32R)
        self.combT = sb("m_combt", [2 * E1, NT * P], F32R)
        self.yo = sb("m_yo", [P, G4, D])
        self.loaded(self.pe, "wr", "wgu", "wd")
        s.loop(0, NT // G4, self.m_logits)
        self.m_routing()
        self.stored = self.ctx.enter_context(self.nc.semaphore("dma_stored"))
        s.loop(0, NT // G4, self.m_experts)
        self.sp.wait_ge(self.stored, NT // G4 * 16)
        self.end_phase()

    def m_logits(self, gi):
        v, s, pe, act, bank = self.dve, self.s, self.pe, self.act, self.bank
        need, V, S, M = s.need, self.V, self.S, self.M
        b, n0 = gi // (TB // G4), gi * G4
        tiles = [self.X[:, n0 + i, :] for i in range(G4)]
        self.stats("ln5", tiles, self.st3)
        need(v, "m.xT")
        for i in range(G4):
            self.normed("m.xn", self.xn3[:, i, :], tiles[i], i, self.st3)
        need(pe, "m.xn", "m.hT")
        for i in range(G4):
            ins = pe.transpose(bank[0][:, i * P:(i + 1) * P], self.xn3[:, i, :], self.c["ident"])
        M("m.xT", ins)
        self.s.need_apart(act, "m.xT", "m.lgmm")
        flat = self.hl3[:].rearrange("p n t -> p (n t)")
        S("m.hT", act.activation(flat, bank[0][:, :], ACT.Identity, scale=at1(self.mT[1][:, 4, :], b),
                                 bias=at1(self.mT[1][:, 3, :], b)))
        need(self.pool, "m.hT")
        self.GP("m.h3", self.pool.tensor_copy(self.h3T[:, tokens(n0, G4)], flat))
        need(pe, "m.hT", "m.lg")
        for i in range(G4):
            ins = pe.matmul(bank[1][:, i * E1:(i + 1) * E1], self.hl3[:, i, :], self.Wr[:], start=True, stop=True)
        M("m.lgmm", ins)
        need(v, "m.lgmm")
        V("m.lg", v.tensor_copy(self.lg1[:, bass.ds(n0, G4), :],
                                bank[1][:, 0:G4 * E1].rearrange("p (n e) -> p n e", e=E1)))
        need(act, "m.h3")

    def m_routing(self):
        v, s, pe, act, bank = self.dve, self.s, self.pe, self.act, self.bank
        need, V, S, M, sb = s.need, self.V, self.S, self.M, self.sb
        oh = [sb(f"m_oh{k}", [P, NT, E1]) for k in range(2)]
        top = [sb(f"m_top{k}", [P, NT]) for k in range(2)]
        z, w1, w2 = (sb(f"m_{x}", [P, NT]) for x in ("z", "w1", "w2"))
        dl, cm = sb("m_dl", [P, NT, E1]), sb("m_cm", [P, NT, E1])
        self.loaded(v, "expand")
        V("m.ex", v.tensor_copy(self.ex[:], self.ex_in[:]))
        need(v, "m.lg")
        self.top2("t1", self.lg1[:], [o[:] for o in oh], NT, E1, self.c["iota16"], [t[:] for t in top])
        V("m.dl", v.tensor_tensor(dl[:], self.lg1[:], top[0][:].unsqueeze(2).to_broadcast([P, NT, E1]), ALU.subtract))
        V("m.d2", v.tensor_tensor(w2[:], top[1][:], top[0][:], ALU.subtract))
        need(act, "m.d2")
        act.activation(dl[:], dl[:], ACT.Exp)
        S("m.exp", act.activation(w2[:], w2[:], ACT.Exp))
        need(v, "m.exp")
        V("m.z", v.tensor_reduce(z[:], dl[:], AX.X, ALU.add))
        need(v, "m.z")
        V("m.z", v.scalar_tensor_tensor(z[:], z[:], 1e-9, w2[:], ALU.mult, ALU.add))
        need(v, "m.z")
        V("m.z", v.tensor_scalar(z[:], z[:], 1.0, None, ALU.add))
        need(v, "m.z")
        V("m.w1", v.reciprocal(w1[:], z[:]))
        need(v, "m.w1")
        V("m.w2", v.tensor_tensor(w2[:], w2[:], w1[:], ALU.mult))
        need(v, "m.w2")
        for k, w in enumerate((w1, w2)):
            V(f"m.oh{k}", v.tensor_tensor(oh[k][:], oh[k][:], w[:].unsqueeze(2).to_broadcast([P, NT, E1]), ALU.mult))
        need(v, "m.oh1")
        V("m.cm", v.tensor_tensor(cm[:], oh[0][:], oh[1][:], ALU.add))
        need(v, "m.cm")
        V("m.hi", v.tensor_copy(self.comb[:, :, 0, :], cm[:]))
        need(v, "m.hi")
        V("m.lo", v.tensor_tensor(self.comb[:, :, 1, :], cm[:], self.comb[:, :, 0, :].bitcast(F32), ALU.subtract))
        need(pe, "m.lo")
        for q in range(NT // G4):
            bk = bank[2 + q % 2]
            need(pe, f"m.ct{q % 2}")
            for i in range(G4):
                ins = pe.transpose(bk[0:2 * E1, i * P:(i + 1) * P],
                                   self.comb[:, q * G4 + i, :, :].rearrange("p k e -> p (k e)").bitcast(F32),
                                   self.c["ident"])
            M("m.ctT", ins)
            need(act, "m.ctT")
            S(f"m.ct{q % 2}", act.copy(self.combT[:, q * G4 * P:(q + 1) * G4 * P], bk[0:2 * E1, :]))

    def m_experts(self, gi):
        v, s, pe, act, bank = self.dve, self.s, self.pe, self.act, self.bank
        need, V, S, M = s.need, self.V, self.S, self.M
        b, n0 = gi // (TB // G4), gi * G4
        sl = tokens(n0, G4)
        need(pe, "m.h3", "m.ct0", "m.ct1", "m.ex")
        order = [MB] + list(range(MB))
        for j, blk in enumerate(order):
            i = j % 2
            need(pe, f"m.h{i}")
            pe.matmul(bank[2 * i][:, :], self.Wgu[:, 0, blk * P:(blk + 1) * P], self.h3T[:, sl], start=True, stop=True)
            M(f"m.gu{i}", pe.matmul(bank[2 * i + 1][:, :], self.Wgu[:, 1, blk * P:(blk + 1) * P], self.h3T[:, sl],
                                    start=True, stop=True))
            if blk < MB:
                self.s.need_apart(pe, f"m.hc{i}")
                M(f"m.ce{i}", pe.matmul(bank[4 + i][:, :], self.ex[:, blk * P:(blk + 1) * P], self.combT[:, sl],
                                        start=True, stop=True))
            need(act, f"m.gu{i}", f"m.h{i}")
            S(f"m.sg{i}", act.activation(self.sg3[i][:], bank[2 * i][:, :], ACT.Silu))
            hd = self.hd3[blk]
            need(v, f"m.sg{i}", "m.down")
            V(f"m.h{i}", v.tensor_tensor(hd[:], bank[2 * i + 1][:, :], self.sg3[i][:], ALU.mult))
            if blk < MB:
                need(v, f"m.h{i}", f"m.ce{i}")
                V(f"m.hc{i}", v.tensor_tensor(hd[:], bank[4 + i][:, :], hd[:], ALU.mult))
        need(pe, "m.hc0", "m.hc1", "m.y")
        for i in range(G4):
            for j, blk in enumerate(order):
                ins = pe.matmul(bank[6][:, i * P:(i + 1) * P], self.hd3[blk][:, i * P:(i + 1) * P], self.Wd[:, blk, :],
                                start=(j == 0), stop=(j == MB))
        M("m.down", ins)
        need(v, "m.down", "m.x")
        V("m.y", v.tensor_tensor(self.yo[:], bank[6][:, :].rearrange("p (n d) -> p n d", d=D),
                                 rows(self.mB[1][:, b, 5, :], G4), ALU.mult))
        need(v, "m.y")
        x = self.X[:, bass.ds(n0, G4), :]
        V("m.x", v.tensor_tensor(x, x, self.yo[:], ALU.add))
        need(self.sp, "m.x")
        self.sp.dma_start(self.io["out"].rearrange("b (c p) d -> p (b c) d", p=P)[:, bass.ds(n0, G4), :],
                          x).then_inc(self.stored, 16)

    def build(self):
        self.setup()
        self.rotation()
        self.layer0_attention()
        self.l0_routing()
        self.l0_experts()
        self.end_phase()
        self.l1_attention()
        self.l1_moe()


def build(nc, io):
    with ExitStack() as ctx:
        Kernel(nc, ctx, io).build()


def at1(ap, b):
    return ap[:, bass.ds(b, 1)]


def tokens(n0, count):
    return bass.ds(n0 * P, count * P)


CONSTS = [("ident", P), ("headmask", P), ("upto", P), ("ones", P), ("pos", TB), ("iota8", E0), ("iota16", E1),
          ("cos1", NT), ("sin1", NT), ("keep", NT)]
COLS = [("cT", 2 * B), ("bq", 1), ("bu", 1), ("lnw", 1), ("lnb", 1), ("bq1", NH)]
ROWS = [("theta", D), ("bkv", 2 * D), ("bout", D), ("bg", E0), ("bk1", HD), ("bv1", HD), ("bo1", D)]


def layout(i):
    f = {k: np.asarray(a) for k, a in i.items()}
    j = np.arange(P)
    angle = np.float32(np.pi / (2.0 * T)) * np.arange(T, dtype=np.float32)
    cs, sn = np.cos(angle).astype(np.float32), np.sin(angle).astype(np.float32)
    consts = np.concatenate([
        np.eye(P), (j[:, None] // 8 == j[None, :] // 8), (j[:, None] <= j[None, :]), np.ones((P, P)),
        j[:, None] + P * np.arange(TB)[None, :],
        np.broadcast_to(np.arange(E0)[None, :], (P, E0)), np.broadcast_to(np.arange(E1)[None, :], (P, E1)),
        np.tile(cs.reshape(TB, P).T, (1, B)), np.tile(sn.reshape(TB, P).T, (1, B)),
        np.broadcast_to((np.arange(NT) % TB != TB - 1)[None, :], (P, NT)),
    ], axis=1).astype(np.float32)
    bqkvu = f["L0_attn_bqkvu"]
    bq1 = f["L1_attn_bq"].reshape(NH, DH)
    cols = np.concatenate([
        f["L0_c"].T, f["L1_c"].T, bqkvu[0:D, None], bqkvu[3 * D:, None], f["L0_attn_ln_w"][:, None],
        f["L0_attn_ln_b"][:, None], np.concatenate([bq1, bq1], axis=1).T,
    ], axis=1)
    rws = np.concatenate([f["L0_attn_theta"].reshape(-1), bqkvu[D:3 * D], f["L0_attn_bout"], f["L0_ffn_bg"],
                          f["L1_attn_bk"], f["L1_attn_bv"], f["L1_attn_bo"]])[None, :]
    wq = f["L1_attn_Wq"].reshape(D, NH, DH)
    return {
        "x": f["L0_attn_x"], "cols": cols, "consts": consts, "rows": rws,
        "wmod0": f["L0_wmod"], "wmod1": f["L1_wmod"], "w0": f["L0_attn_Wqkvu"].T, "wo0": f["L0_attn_Wout"].T,
        "cst": np.concatenate([np.tile(cs, (DH, 1)), np.tile(sn, (DH, 1))]),
        "wq1": np.concatenate([wq, wq], axis=2).reshape(D, NH * P), "wk1": f["L1_attn_Wk"], "wv1": f["L1_attn_Wv"],
        "wo1": f["L1_attn_Wo"],
        "wgu": np.stack([np.concatenate([f[f"L1_ffn_w{k}_r"].transpose(1, 0, 2).reshape(D, E1 * MR),
                                         f[f"L1_ffn_w{k}_s"].transpose(1, 0, 2).reshape(D, NS * MS)], axis=1)
                         for k in "gu"], axis=1),
        "wd": np.concatenate([f["L1_ffn_wd_r"].reshape(E1 * MR, D), f["L1_ffn_wd_s"].reshape(NS * MS, D)]),
        "wr": f["L1_ffn_router_w"],
        "expand": (np.arange(2 * E1)[:, None] % E1 == np.arange(E1 * MR)[None, :] // MR).astype(np.float32),
        "wg0": f["L0_ffn_Wg"], "w1": f["L0_ffn_W1"], "w2": f["L0_ffn_W2"], "w3": f["L0_ffn_W3"],
    }


def kernel(**inputs):
    import concourse.bacc as bacc
    from concourse.bass_utils import run_bass_kernel_spmd

    nc = bacc.Bacc("TRN2", target_bir_lowering=False, num_devices=1)
    arrays, io = {}, {}
    for name, a in layout(inputs).items():
        arrays[f"in_{name}"] = np.ascontiguousarray(a)
        io[name] = nc.dram_tensor(f"in_{name}", a.shape, mybir.dt.from_np(a.dtype), kind="ExternalInput").ap()
    io["out"] = nc.dram_tensor("out", (B, T, D), F32, kind="ExternalOutput").ap()
    build(nc, io)
    r = run_bass_kernel_spmd(nc, [arrays], core_ids=[0])
    return r.results[0]["out"]
```

```python
from contextlib import ExitStack

import numpy as np

import concourse.bass as bass
from concourse import mybir
from concourse.alu_op_type import AluOpType as ALU

ACT = mybir.ActivationFunctionType
F32 = mybir.dt.float32
F32R = mybir.dt.float32r
I32 = mybir.dt.int32
AX = mybir.AxisListType

P = 128
B, T, D = 4, 1024, 128
TB = T // P
NT = B * TB
G4 = 4
EPS = 1e-5
E0, H0 = 8, 512
CAP = int(B * T / E0 * 1.25)
ST = CAP // P
NSLOT = E0 * CAP
NH, DH = 16, 64
HD = NH * DH
HG = 4
NG = NH // HG
E1, MR = 16, 32
NS, MS = 2, 64
MB = E1 * MR // P
TWO_PI = 6.283185307179586
C1 = 6.28125
C2 = float(np.float32(round((TWO_PI - C1) * 2.0**20) / 2.0**20))
C3 = float(TWO_PI - C1 - C2)
ROUND = 12582912.0
PI32 = 3.1415925


class Engine:

    def __init__(self, name, eng, sem):
        self.name, self.eng, self.sem = name, eng, sem
        self.base, self.k, self.per = 0, 0, 0

    def inc(self, ins):
        ins.then_inc(self.sem, 1)
        self.k += 1
        return self


class Sync:

    def __init__(self, nc, ctx):
        self.nc = nc
        mk = lambda n, e: Engine(n, e, ctx.enter_context(nc.semaphore(f"done_{n}")))
        self.pe, self.act = mk("pe", nc.tensor), mk("act", nc.scalar)
        self.dve, self.pool = mk("dve", nc.vector), mk("pool", nc.gpsimd)
        self.all = [self.pe, self.act, self.dve, self.pool]
        self.marks, self.waited = {}, {}
        self.turn = 0

    def mark(self, name, e):
        self.marks[name] = (e, self.turn, e.k, e.base if isinstance(e.base, int) else None)

    def did(self, name, e, ins):
        e.inc(ins)
        self.mark(name, e)

    def value(self, name):
        e, turn, k, base = self.marks[name]
        rolled = not isinstance(e.base, int)
        if turn == self.turn:
            return e, ((1, k) if rolled else (0, e.base + k))
        if rolled and turn == self.turn - 1:
            return e, (1, k - e.per)
        return e, (0, base + k)

    def need(self, waiter, *names, apart=False):
        latest = {}
        for name in names:
            if name in self.marks:
                e, v = self.value(name)
                latest[e.name] = max(latest.get(e.name, (e, v)), (e, v), key=lambda x: x[1])
        waits = []
        for e, v in latest.values():
            key = (id(waiter), e.name)
            turn, done = self.waited.get(key, (-1, (0, 0)))
            if turn == self.turn and done >= v:
                continue
            self.waited[key] = (self.turn, v)
            waits.append((e.sem, e.base + v[1] if v[0] else v[1]))
        if apart and any(not isinstance(value, int) for _, value in waits):
            waits = [(sem, value if isinstance(value, int) else waiter.to_reg(value)) for sem, value in waits]
            waiter.wait_ge(next(e.sem for e in self.all if e.eng is waiter), 1)
        for sem, value in waits:
            waiter.wait_ge(sem, value)

    def need_apart(self, waiter, *names):
        self.need(waiter, *names, apart=True)

    def loop(self, first, last, body):
        def counted(n):
            self.turn += 1
            before = [e.k for e in self.all]
            body(n)
            return [e.k - b for e, b in zip(self.all, before)]
        for e in self.all:
            e.base += e.k
            e.k = 0
        got = counted(first)
        for e, g in zip(self.all, got):
            e.per = g
        start = [e.base + g for e, g in zip(self.all, got)]
        with self.nc.Fori(first + 1, last) as n:
            for e, s in zip(self.all, start):
                e.base, e.k = n * e.per + (s - (first + 1) * e.per), 0
            again = counted(n)
            assert again == got, (got, again)
        for e, s in zip(self.all, start):
            e.base, e.k = s + (last - first - 1) * e.per, 0
        self.turn += 1
        for m, (e, turn, k, base) in list(self.marks.items()):
            if turn == self.turn - 1 and base is None:
                self.marks[m] = (e, turn, k - e.per, e.base)


def rows(ap, count):
    p, w = ap.shape
    return ap.unsqueeze(1).to_broadcast([p, count, w])


class Kernel:

    def __init__(self, nc, ctx, io):
        self.nc, self.ctx, self.io = nc, ctx, io
        self.mem, self.outer, self.scratch = ctx, [], {}
        self.s = Sync(nc, ctx)
        self.pe, self.act, self.dve, self.pool, self.sp = nc.tensor, nc.scalar, nc.vector, nc.gpsimd, nc.sync
        self.psum = ctx.enter_context(nc.psum_tensor("psum", [P, 8, 512], F32))
        self.bank = [self.psum[:, i, :] for i in range(8)]
        self.dma_sems, self.dma_total = {}, {}

    def sb(self, name, shape, dt=F32):
        return self.mem.enter_context(self.nc.sbuf_tensor(f"sb_{name}", shape, dt))

    def phase(self):
        self.outer.append(self.mem)
        self.mem = ExitStack()
        self.scratch = {}

    def end_phase(self):
        for waiter in (self.pe, self.act, self.dve, self.pool, self.sp):
            for e in self.s.all:
                waiter.wait_ge(e.sem, e.base + e.k)
        self.mem.close()
        self.mem = self.outer.pop()
        self.scratch = {}

    def V(self, name, ins):
        self.s.did(name, self.s.dve, ins)

    def S(self, name, ins):
        self.s.did(name, self.s.act, ins)

    def M(self, name, ins):
        self.s.did(name, self.s.pe, ins)

    def GP(self, name, ins):
        self.s.did(name, self.s.pool, ins)

    def load(self, name, out, in_, queue=None):
        sem = self.ctx.enter_context(self.nc.semaphore(f"dma_{name}"))
        self.dma_sems[name] = sem
        self.dma_total[name] = 16
        (queue or self.sp).dma_start(out, in_).then_inc(sem, 16)

    def loaded(self, waiter, *names):
        for name in names:
            waiter.wait_ge(self.dma_sems[name], self.dma_total[name])

    def stats(self, tag, tiles, buf):
        v, need, V = self.dve, self.s.need, self.V
        st, mv, y, h, t = buf
        n = len(tiles)
        for i, x in enumerate(tiles):
            ins = v.bn_stats(st[:, i, :], x)
        V(f"{tag}.st", ins)
        self.s.need_apart(v, f"{tag}.st")
        for i in range(n):
            ins = v.bn_aggr(mv[:, i, :], st[:, i, :])
        V(f"{tag}.mv", ins)
        need(v, f"{tag}.mv")
        V(f"{tag}.v", v.tensor_scalar(t[:, 0:n], mv[:, 0:n, 1], EPS, None, ALU.add))
        V(f"{tag}.h", v.tensor_scalar(h[:, 0:n], mv[:, 0:n, 1], EPS, -0.5, ALU.add, ALU.mult))
        need(v, f"{tag}.v")
        V(f"{tag}.y0", v.tensor_scalar(y[:, 0:n].bitcast(I32), t[:, 0:n].bitcast(I32), -0.5, 1597463007.0,
                                       ALU.mult, ALU.add))
        for _ in range(4):
            need(v, f"{tag}.y0")
            V(f"{tag}.t", v.tensor_tensor(t[:, 0:n], y[:, 0:n], y[:, 0:n], ALU.mult))
            need(v, f"{tag}.t")
            V(f"{tag}.t", v.tensor_tensor(t[:, 0:n], t[:, 0:n], h[:, 0:n], ALU.mult))
            need(v, f"{tag}.t")
            V(f"{tag}.y0", v.scalar_tensor_tensor(y[:, 0:n], t[:, 0:n], 1.5, y[:, 0:n], ALU.add, ALU.mult))
        need(v, f"{tag}.y0")

    def normed(self, name, out, x, i, buf):
        _, mv, y, _, _ = buf
        self.V(name, self.dve.tensor_scalar(out, x, mv[:, i, 0:1], y[:, i:i + 1], ALU.subtract, ALU.mult))

    def stat_buffers(self, tag, n):
        return (self.sb(f"{tag}_st", [P, n, 6]), self.sb(f"{tag}_mv", [P, n, 2]), self.sb(f"{tag}_y", [P, n]),
                self.sb(f"{tag}_h", [P, n]), self.sb(f"{tag}_t", [P, n]))

    def setup(self):
        nc, io, v, s, pe = self.nc, self.io, self.dve, self.s, self.pe
        need, V, S, M = s.need, self.V, self.S, self.M
        sb = self.sb
        self.X = sb("x", [P, NT, D])
        self.cols = sb("cols", [P, io["cols"].shape[1]])
        self.consts = sb("consts", [P, io["consts"].shape[1]])
        self.rowsb = sb("rows", [P, io["rows"].shape[1]])
        self.mT = [sb(f"mt{i}", [P, 6, B]) for i in range(2)]
        self.mB = [sb(f"mb{i}", [P, B, 6, D]) for i in range(2)]
        self.w0 = [sb(f"w0_{k}", [P, NT]) for k in range(2)]
        self.slot = [sb(f"slot{k}", [P, NT], I32) for k in range(2)]
        self.e_w12 = sb("e_w12", [P, 2, 2, H0])
        self.e_w3 = sb("e_w3", [P, 2, H0 // P, D])
        self.phase()
        self.H2 = sb("h2", [P, NT, D])
        self.LG = sb("lg", [P, NT, E0])
        self.phase()
        self.wmod = [sb(f"wmod{i}", [P, 6 * D]) for i in range(2)]
        self.W0 = sb("w0", [P, 4 * D])
        self.WoT = sb("wo0", [P, D])
        self.load("cols", self.cols[:], io["cols"])
        self.load("consts", self.consts[:], io["consts"])
        self.load("wmod0", self.wmod[0][:], io["wmod0"], self.act)
        for b in range(B):
            self.load(f"x{b}", self.X[:, b * TB:(b + 1) * TB, :],
                      io["x"][b].rearrange("(c p) d -> p c d", p=P), self.act if b % 2 else self.sp)
            if b == 0:
                self.load("rows", self.rowsb[:], io["rows"].to_broadcast([P, io["rows"].shape[1]]))
                self.load("w0", self.W0[:], io["w0"], self.act)
        self.load("wo0", self.WoT[:], io["wo0"])
        self.load("wmod1", self.wmod[1][:], io["wmod1"], self.act)
        at = 0
        self.c = {}
        for name, w in CONSTS:
            self.c[name] = self.consts[:, at:at + w]
            at += w
        at = 0
        for name, w in COLS:
            self.c[name] = self.cols[:, at:at + w]
            at += w
        at = 0
        for name, w in ROWS:
            self.c[name] = self.rowsb[:, at:at + w]
            at += w
        self.zero = sb("zero", [P, 10 * D])
        self.GP("zero", self.pool.memset(self.zero[:], 0.0))
        self.disp = nc.dram_tensor("disp", [NSLOT, D], F32).ap()
        self.eout = nc.dram_tensor("eout", [NSLOT + 1, D], F32).ap()
        need(self.sp, "zero")
        sem = self.ctx.enter_context(nc.semaphore("dma_zeroed"))
        self.dma_sems["zeroed"] = sem
        self.dma_total["zeroed"] = 5 * 16
        part = NSLOT // 4
        for i in range(4):
            self.sp.dma_start(self.disp[i * part:(i + 1) * part, :].rearrange("(p a) d -> p (a d)", p=P),
                              self.zero[:]).then_inc(sem, 16)
        self.sp.dma_start(self.eout[NSLOT:NSLOT + 1, :], self.zero[0:1, 0:D]).then_inc(sem, 16)

        self.sc = sb("sc", [P, 2, B])
        self.scB = sb("scb", [P, B, P])
        self.loaded(self.act, "cols")
        S("sc", self.act.activation(self.sc[:], self.c["cT"].rearrange("p (l b) -> p l b", l=2), ACT.Silu))
        for lay in range(2):
            self.modulations(lay)

    def modulations(self, lay):
        v, s, pe, act = self.dve, self.s, self.pe, self.act
        need, V, S, M = s.need, self.V, self.S, self.M
        w, mT, mB = self.wmod[lay], self.mT[lay], self.mB[lay]
        need(v, "sc", "mod.mm")
        V("mod.scB", v.tensor_copy(self.scB[:], self.sc[:, lay, :].unsqueeze(2).to_broadcast([P, B, P])))
        self.loaded(pe, f"wmod{lay}")
        need(pe, "sc", "mod.evT")
        for j in range(6):
            ins = pe.matmul(self.bank[0][:, j * B:(j + 1) * B], w[:, j * D:(j + 1) * D], self.sc[:, lay, :],
                            start=True, stop=True)
        M("mod.T", ins)
        need(act, "mod.T")
        S("mod.evT", act.copy(mT[:], self.bank[0][:, 0:6 * B].rearrange("p (j b) -> p j b", j=6)))
        need(pe, "mod.scB")
        for b in range(B):
            k = 1 + 2 * (b % 2)
            need(pe, f"mod.evB{b % 2}")
            pe.matmul(self.bank[k][:, :], self.scB[:, b, :], w[:, 0:512], start=True, stop=True)
            M("mod.mm", pe.matmul(self.bank[k + 1][:, 0:256], self.scB[:, b, :], w[:, 512:768],
                                  start=True, stop=True))
            need(act, "mod.mm")
            act.copy(mB[:, b, 0:4, :].rearrange("p j d -> p (j d)"), self.bank[k][:, :])
            S(f"mod.evB{b % 2}", act.copy(mB[:, b, 4:6, :].rearrange("p j d -> p (j d)"),
                                          self.bank[k + 1][:, 0:256]))
        need(v, "mod.evT", "mod.evB0", "mod.evB1")
        for j in (1, 4):
            v.tensor_scalar(mT[:, j, :], mT[:, j, :], 1.0, None, ALU.add)
        V("mod.one", v.tensor_scalar(mB[:, :, 4, :], mB[:, :, 4, :], 1.0, None, ALU.add))
        for j in (2, 5):
            g = mB[:, :, j, :]
            t = self.scr(f"gate{j}", [P, B, D])
            V("mod.sg", v.tensor_scalar(t[:], g, 0.0, 2.0, ALU.is_ge, ALU.mult))
            V("mod.ab", v.scalar_tensor_tensor(g, g, -1.0, g, ALU.mult, ALU.max))
            need(v, "mod.ab")
            V("mod.sg", v.tensor_scalar(t[:], t[:], -1.0, None, ALU.add))
            need(v, "mod.sg")
            V("mod.g", v.scalar_tensor_tensor(g, g, 0.25, t[:], ALU.max, ALU.mult))
        s.mark(f"mod{lay}", s.dve)

    def scr(self, name, shape):
        if name not in self.scratch:
            self.scratch[name] = self.sb(name, shape)
        return self.scratch[name]

    def rotation(self):
        v, s, pe, act = self.dve, self.s, self.pe, self.act
        need, V, S, M = s.need, self.V, self.S, self.M
        th = self.sb("th", [P, TB, D])
        cnt = self.sb("cnt", [P, TB, D])
        self.tokT = [self.sb(f"tokt{k}", [P, TB, D]) for k in range(2)]
        self.dimT = [self.sb(f"dimt{k}", [P, T]) for k in range(2)]
        self.loaded(v, "rows")
        self.loaded(v, "consts")
        for c in range(TB):
            ins = v.tensor_scalar(th[:, c, :], self.c["theta"], self.c["pos"][:, c:c + 1], None, ALU.mult)
        V("th", ins)
        for k, (turn, shift) in enumerate(((0.25, TWO_PI / 4), (0.0, 0.0))):
            r = self.tokT[k]
            need(v, "th", "rot.r")
            V("rot.n", v.tensor_scalar(cnt[:], th[:], 1.0 / TWO_PI, turn, ALU.mult, ALU.add))
            need(v, "rot.n")
            V("rot.n", v.tensor_scalar(cnt[:], cnt[:], ROUND, None, ALU.add))
            need(v, "rot.n")
            V("rot.n", v.tensor_scalar(cnt[:], cnt[:], ROUND, None, ALU.subtract))
            need(v, "rot.n")
            V("rot.r", v.scalar_tensor_tensor(r[:], cnt[:], -C1, th[:], ALU.mult, ALU.add))
            for cc in (C2, C3):
                need(v, "rot.r")
                V("rot.r", v.scalar_tensor_tensor(r[:], cnt[:], -cc, r[:], ALU.mult, ALU.add))
            need(v, "rot.r")
            V("rot.r", v.tensor_scalar(r[:], r[:], shift, None, ALU.add))
            need(v, "rot.r")
            V("rot.n", v.tensor_scalar(cnt[:], r[:], 1.0 / TWO_PI, ROUND, ALU.mult, ALU.add))
            need(v, "rot.n")
            V("rot.n", v.tensor_scalar(cnt[:], cnt[:], ROUND, None, ALU.subtract))
            need(v, "rot.n")
            V("rot.r", v.scalar_tensor_tensor(r[:], cnt[:], -TWO_PI, r[:], ALU.mult, ALU.add))
            need(v, "rot.r")
            V("rot.r", v.tensor_scalar(r[:], r[:], -PI32, PI32, ALU.max, ALU.min))
            need(act, "rot.r")
            S(f"tok{k}", act.activation(r[:], r[:], ACT.Sin))
            for half in range(2):
                bk = self.bank[5 + half]
                need(pe, f"tok{k}", f"rot.ev{half}")
                for i in range(4):
                    ins = pe.transpose(bk[:, i * P:(i + 1) * P], r[:, 4 * half + i, :], self.c["ident"])
                M("rot.tr", ins)
                need(v, "rot.tr")
                V(f"rot.ev{half}", v.tensor_copy(self.dimT[k][:, half * 512:(half + 1) * 512], bk[:, :]))
        s.mark("rotation", s.dve)

    def l0_buffers(self):
        sb = self.sb
        self.qT = sb("q_t", [P, NT * P])
        self.uT = sb("u_t", [P, NT * P])
        self.xn = sb("xn", [P, G4, D])
        self.hT = sb("h_t", [P, G4 * P])
        self.kv = sb("kv", [P, G4, 2 * D])
        self.kr = [sb(f"kr{k}", [P, G4, D]) for k in range(2)]
        self.KVa = sb("kva", [P, 2, D])
        self.KVm = sb("kvm", [P, 2, D])
        self.qr = [sb(f"qr{k}", [P, G4 * P]) for k in range(2)]
        self.on = sb("on", [P, G4, D])
        self.oT = sb("o_t", [P, G4 * P])
        self.hm = sb("hm", [P, G4, D])
        self.h2T = sb("h2_t", [P, G4 * P])
        self.wog = sb("wog", [P, D])
        self.gbo = sb("gbo", [P, D])
        self.stA, self.stB, self.stC = (self.stat_buffers(f"s{x}", G4) for x in "abc")
        self.Wg = sb("wg0", [P, E0])
        self.load("wg0", self.Wg[:], self.io["wg0"])

    def l0_keys(self, b, half):
        v, s, pe, act, bank = self.dve, self.s, self.pe, self.act, self.bank
        need, V, S, M = s.need, self.V, self.S, self.M
        n0 = b * TB + half * G4
        tiles = [self.X[:, n0 + i, :] for i in range(G4)]
        self.stats("ln1", tiles, self.stA)
        need(v, "l0.xT")
        for i in range(G4):
            ins_name = "l0.xn"
            self.normed(ins_name, self.xn[:, i, :], tiles[i], i, self.stA)
        need(pe, "l0.xn", "l0.hT")
        for i in range(G4):
            ins = pe.transpose(bank[0][:, i * P:(i + 1) * P], self.xn[:, i, :], self.c["ident"])
        M("l0.xT", ins)
        self.s.need_apart(act, "l0.xT", "l0.kvmm")
        S("l0.hT", act.activation(self.hT[:], bank[0][:, :], ACT.Identity, scale=at1(self.mT[0][:, 1, :], b),
                                  bias=at1(self.mT[0][:, 0, :], b)))
        need(pe, "l0.hT", "l0.q", "l0.u")
        M("l0.qmm", pe.matmul(bank[1][:, :], self.W0[:, 0:D], self.hT[:], start=True, stop=True))
        M("l0.umm", pe.matmul(bank[2][:, :], self.W0[:, 3 * D:4 * D], self.hT[:], start=True, stop=True))
        sl = tokens(n0, G4)
        self.s.need_apart(act, "l0.qmm")
        S("l0.q", act.activation(self.qT[:, sl], bank[1][:, :], ACT.Silu, bias=self.c["bq"]))
        self.s.need_apart(act, "l0.umm")
        S("l0.u", act.activation(self.uT[:, sl], bank[2][:, :], ACT.Identity, bias=self.c["bu"]))
        for j in range(2):
            need(pe, f"l0.kv{j}")
            for i in range(2):
                t = 2 * j + i
                ins = pe.matmul(bank[3 + j][:, i * 256:(i + 1) * 256], self.hT[:, t * P:(t + 1) * P],
                                self.W0[:, D:3 * D], start=True, stop=True)
            M("l0.kvmm", ins)
            need(v, "l0.kvmm", "l0.state", "l0.ks")
            V(f"l0.kv{j}", v.tensor_tensor(self.kv[:, 2 * j:2 * j + 2, :],
                                           bank[3 + j][:, :].rearrange("p (a b) -> p a b", a=2),
                                           rows(self.c["bkv"], 2), ALU.add))
        need(act, "l0.kv1", "l0.kr")
        S("l0.ks", act.activation(self.kv[:, :, 0:D], self.kv[:, :, 0:D], ACT.Silu))
        need(v, "l0.ks", "l0.state")
        for k in range(2):
            V("l0.kr", v.tensor_tensor(self.kr[k][:], self.kv[:, :, 0:D], self.tokT[k][:, 4 * half:4 * half + 4, :],
                                       ALU.mult))
        need(pe, "l0.kr", "l0.kva")
        for k in range(2):
            for i in range(G4):
                ins = pe.matmul(bank[5][:, k * D:(k + 1) * D], self.kr[k][:, i, :], self.kv[:, i, D:2 * D],
                                start=(i == 0), stop=(i == G4 - 1))
        M("l0.state", ins)
        need(v, "l0.state", "l0.kvm")
        both = bank[5][:, 0:2 * D].rearrange("p (k d) -> p k d", k=2)
        if half == 0:
            V("l0.kva", v.tensor_copy(self.KVa[:], both))
        else:
            V("l0.kva", v.tensor_tensor(self.KVa[:], self.KVa[:], both, ALU.add))

    def l0_close_state(self):
        need, v = self.s.need, self.dve
        need(v, "l0.kva", "l0.omm")
        self.V("l0.kvm", v.tensor_tensor(self.KVm[:], self.KVa[:], rows(self.c["headmask"], 2), ALU.mult))

    def l0_out_weights(self, b):
        need, v = self.s.need, self.dve
        g = self.mB[0][:, b, 2, :]
        need(v, "l0.ymm", "l0.x")
        v.tensor_tensor(self.wog[:], self.WoT[:], g, ALU.mult)
        self.V("l0.wog", v.tensor_tensor(self.gbo[:], self.c["bout"], g, ALU.mult))

    def l0_queries(self, b, half):
        v, s, pe, act, bank = self.dve, self.s, self.pe, self.act, self.bank
        need, V, S, M = s.need, self.V, self.S, self.M
        n0 = b * TB + half * G4
        sl = tokens(n0, G4)
        need(v, "l0.q", "l0.omm")
        for k in range(2):
            V("l0.qr", v.tensor_tensor(self.qr[k][:], self.qT[:, sl], self.dimT[k][:, half * 512:half * 512 + 512],
                                       ALU.mult))
        need(pe, "l0.qr", "l0.kvm", "l0.x")
        for i in range(G4):
            for k in range(2):
                ins = pe.matmul(bank[6][:, i * P:(i + 1) * P], self.qr[k][:, i * P:(i + 1) * P], self.KVm[:, k, :],
                                start=(k == 0), stop=(k == 1))
        M("l0.omm", ins)
        need(v, "l0.omm")
        self.stats("ln2", [bank[6][:, i * P:(i + 1) * P] for i in range(G4)], self.stB)
        need(v, "l0.onT")
        for i in range(G4):
            self.normed("l0.on", self.on[:, i, :], bank[6][:, i * P:(i + 1) * P], i, self.stB)
        need(pe, "l0.on", "l0.h2T")
        for i in range(G4):
            ins = pe.transpose(bank[7][:, i * P:(i + 1) * P], self.on[:, i, :], self.c["ident"])
        M("l0.onT", ins)
        need(act, "l0.onT", "l0.ymm")
        S("l0.oT", act.activation(self.oT[:], bank[7][:, :], ACT.Identity, scale=self.c["lnw"], bias=self.c["lnb"]))
        need(v, "l0.oT", "l0.u")
        V("l0.ou", v.tensor_tensor(self.oT[:], self.oT[:], self.uT[:, sl], ALU.mult))
        need(pe, "l0.ou", "l0.wog")
        for i in range(G4):
            ins = pe.matmul(bank[6][:, i * P:(i + 1) * P], self.oT[:, i * P:(i + 1) * P], self.wog[:],
                            start=True, stop=True)
        M("l0.ymm", ins)
        xs = self.X[:, bass.ds(n0, G4), :]
        need(v, "l0.ymm")
        V("l0.xa", v.tensor_tensor(xs, bank[6][:, :].rearrange("p (a b) -> p a b", a=G4), xs, ALU.add))
        need(v, "l0.xa", "l0.wog")
        V("l0.x", v.tensor_tensor(xs, xs, rows(self.gbo[:], G4), ALU.add))
        self.s.need_apart(v, "l0.x", "l0.H2", "l0.h2mm")
        tiles = [self.X[:, n0 + i, :] for i in range(G4)]
        self.stats("ln3", tiles, self.stC)
        for i in range(G4):
            self.normed("l0.hn", self.hm[:, i, :], tiles[i], i, self.stC)
        need(v, "l0.hn")
        V("l0.hc", v.tensor_tensor(self.hm[:], self.hm[:], rows(self.mB[0][:, b, 4, :], G4), ALU.mult))
        need(v, "l0.hc")
        V("l0.h2", v.tensor_tensor(self.hm[:], self.hm[:], rows(self.mB[0][:, b, 3, :], G4), ALU.add))
        need(act, "l0.h2")
        S("l0.H2", act.copy(self.H2[:, bass.ds(n0, G4), :], self.hm[:]))
        need(pe, "l0.h2", "l0.oT")
        for i in range(G4):
            ins = pe.transpose(bank[7][:, i * P:(i + 1) * P], self.hm[:, i, :], self.c["ident"])
        M("l0.h2mm", ins)
        need(act, "l0.h2mm", "l0.lgmm")
        S("l0.h2T", act.copy(self.h2T[:], bank[7][:, :]))
        need(pe, "l0.h2T", "l0.lg")
        for i in range(G4):
            ins = pe.matmul(bank[6][:, i * E0:(i + 1) * E0], self.h2T[:, i * P:(i + 1) * P], self.Wg[:],
                            start=True, stop=True)
        M("l0.lgmm", ins)
        need(v, "l0.lgmm")
        V("l0.lg", v.tensor_tensor(self.LG[:, bass.ds(n0, G4), :],
                                   bank[6][:, 0:G4 * E0].rearrange("p (a b) -> p a b", a=G4),
                                   rows(self.c["bg"], G4), ALU.add))
        s.mark("l0.x", s.dve)

    def layer0_attention(self):
        s = self.s
        self.l0_buffers()
        for b in range(B):
            self.loaded(self.dve, f"x{b}")
        self.loaded(self.pe, "w0", "consts", "wg0", "wo0")
        self.loaded(self.dve, "wo0")
        s.need(self.pe, "rotation")
        s.need(self.act, "mod0", "rotation")

        self.l0_keys(0, 0)
        self.l0_keys(0, 1)
        self.l0_close_state()

        def body(b):
            self.l0_out_weights(b)
            for half in range(2):
                self.l0_keys(b + 1, half)
                self.l0_queries(b, half)
            self.l0_close_state()

        s.loop(0, B - 1, body)
        self.l0_out_weights(B - 1)
        for half in range(2):
            self.l0_queries(B - 1, half)
        self.end_phase()

    def top2(self, tag, lg, oh, n, e, iota, top):
        v, need, V = self.dve, self.s.need, self.V
        wk = self.scr(f"{tag}_wk", [P, n, e])
        rest = self.scr(f"{tag}_rest", [P, n, e])
        idx = self.scr(f"{tag}_idx", [P, n])
        src = lg
        for k in range(2):
            V(f"{tag}.a", v.tensor_reduce(top[k], src, AX.X, ALU.max))
            need(v, f"{tag}.a")
            V(f"{tag}.a", v.tensor_tensor(wk[:], src, top[k].unsqueeze(2).to_broadcast([P, n, e]), ALU.is_equal))
            need(v, f"{tag}.a")
            V(f"{tag}.a", v.scalar_tensor_tensor(wk[:], wk[:], -64.0, rows(iota, n), ALU.mult, ALU.add))
            need(v, f"{tag}.a")
            V(f"{tag}.a", v.tensor_reduce(idx[:], wk[:], AX.X, ALU.min))
            need(v, f"{tag}.a")
            V(f"{tag}.a", v.tensor_scalar(idx[:], idx[:], 64.0, None, ALU.add))
            need(v, f"{tag}.a")
            V(f"{tag}.a", v.tensor_tensor(oh[k], rows(iota, n), idx[:].unsqueeze(2).to_broadcast([P, n, e]),
                                          ALU.is_equal))
            need(v, f"{tag}.a")
            if k == 0:
                V(f"{tag}.a", v.scalar_tensor_tensor(rest[:], oh[0], -3.0e38, lg, ALU.mult, ALU.add))
                need(v, f"{tag}.a")
                src = rest[:]

    def l0_routing(self):
        v, s, pe, act, bank = self.dve, self.s, self.pe, self.act, self.bank
        need, V, S, M, sb = s.need, self.V, self.S, self.M, self.sb
        oh = [sb(f"oh{k}", [P, NT, E0]) for k in range(2)]
        top = [sb(f"top{k}", [P, NT]) for k in range(2)]
        label, seq, pre, wk = (sb(f"rt_{x}", [P, NT, E0]) for x in ("label", "seq", "pre", "wk"))
        sf, sv = sb("rt_sf", [P, NT]), sb("rt_sv", [P, NT])
        need(v, "l0.lg")
        self.top2("t0", self.LG[:], [o[:] for o in oh], NT, E0, self.c["iota8"], [t[:] for t in top])
        V("r0.d", v.tensor_tensor(self.w0[1][:], top[1][:], top[0][:], ALU.subtract))
        V("r0.label", v.tensor_tensor(label[:], oh[0][:], oh[1][:], ALU.add))
        need(act, "r0.d")
        S("r0.e", act.activation(self.w0[1][:], self.w0[1][:], ACT.Exp))
        need(pe, "r0.label")
        flat = label[:].rearrange("p n e -> p (n e)")
        pe.matmul(bank[0][:, 0:NT * E0], self.c["upto"], flat, start=True, stop=True)
        M("r0.cum", pe.matmul(bank[1][:, 0:NT * E0], self.c["ones"], flat, start=True, stop=True))
        need(v, "r0.cum")
        tot = bank[1][:, 0:NT * E0].rearrange("p (n e) -> p n e", e=E0)
        V("r0.a", v.tensor_copy(pre[:], tot))
        need(v, "r0.a")
        a, b = pre, wk
        step = 1
        while step < NT:
            V("r0.a", v.tensor_copy(b[:, 0:step, :], a[:, 0:step, :]))
            V("r0.a", v.tensor_tensor(b[:, step:, :], a[:, step:, :], a[:, 0:NT - step, :], ALU.add))
            need(v, "r0.a")
            a, b = b, a
            step *= 2
        V("r0.a", v.tensor_tensor(seq[:], a[:], tot, ALU.subtract))
        need(v, "r0.a")
        V("r0.seq", v.tensor_tensor(seq[:], seq[:], bank[0][:, 0:NT * E0].rearrange("p (n e) -> p n e", e=E0),
                                    ALU.add))
        need(v, "r0.seq", "r0.e")
        V("r0.w", v.tensor_scalar(self.w0[0][:], self.w0[1][:], 1.0, None, ALU.add))
        need(v, "r0.w")
        V("r0.w", v.reciprocal(self.w0[0][:], self.w0[0][:]))
        need(v, "r0.w")
        V("r0.w", v.tensor_tensor(self.w0[1][:], self.w0[1][:], self.w0[0][:], ALU.mult))
        for k in range(2):
            V("r0.a", v.tensor_tensor(wk[:], seq[:], oh[k][:], ALU.mult))
            need(v, "r0.a")
            V("r0.a", v.tensor_reduce(sv[:], wk[:], AX.X, ALU.add))
            need(v, "r0.a")
            V("r0.a", v.tensor_tensor(wk[:], rows(self.c["iota8"], NT), oh[k][:], ALU.mult))
            need(v, "r0.a")
            V("r0.a", v.tensor_reduce(sf[:], wk[:], AX.X, ALU.add))
            need(v, "r0.a")
            V("r0.a", v.tensor_scalar(sf[:], sf[:], float(CAP), -1.0, ALU.mult, ALU.add))
            need(v, "r0.a")
            V("r0.a", v.tensor_tensor(sf[:], sf[:], sv[:], ALU.add))
            V("r0.b", v.tensor_scalar(sv[:], sv[:], float(CAP), None, ALU.is_le))
            need(v, "r0.a", "r0.b")
            V("r0.a", v.scalar_tensor_tensor(sf[:], sf[:], -float(NSLOT), sv[:], ALU.add, ALU.mult))
            need(v, "r0.a")
            V("r0.a", v.tensor_scalar(sf[:], sf[:], float(NSLOT), None, ALU.add))
            need(v, "r0.a")
            V(f"r0.slot{k}", v.tensor_copy(self.slot[k][:], sf[:]))
        g = self.pool
        need(g, "r0.slot0", "r0.slot1", "l0.H2")
        self.loaded(g, "zeroed")
        sem = self.ctx.enter_context(self.nc.semaphore("dma_dispatched"))
        self.dma_sems["dispatched"], self.dma_total["dispatched"] = sem, 2 * NT * 16
        for n in range(NT):
            for k in range(2):
                g.indirect_dma_start(out=self.disp, out_offset=bass.IndirectOffsetOnAxis(
                    ap=self.slot[k][:, n:n + 1], axis=0), in_=self.H2[:, n, :], in_offset=None,
                    bounds_check=NSLOT - 1, oob_is_err=False).then_inc(sem, 16)

    def l0_experts(self):
        nc, v, s, pe, act, bank, sp = self.nc, self.dve, self.s, self.pe, self.act, self.bank, self.sp
        need, V, S, M, sb, io = s.need, self.V, self.S, self.M, self.sb, self.io
        w12, w3 = self.e_w12, self.e_w3
        self.phase()
        xe = sb("e_x", [P, 2, ST, D])
        xT = sb("e_xt", [P, CAP])
        hs = sb("e_hs", [P, H0 // P, CAP])
        sg = sb("e_sg", [P, CAP])
        y = sb("e_y", [P, ST, D])
        sem = lambda n: self.ctx.enter_context(nc.semaphore(n))
        s_w = [sem(f"dma_expert_w{i}") for i in range(2)]
        s_x = [sem(f"dma_expert_x{i}") for i in range(2)]
        s_y = sem("dma_expert_y")
        HC = CAP // 2
        PAIRS = E0 // 2

        def load_weights(e, i):
            act.dma_start(w12[:, i, 0, :], io["w1"][e]).then_inc(s_w[i], 16)
            act.dma_start(w12[:, i, 1, :], io["w2"][e]).then_inc(s_w[i], 16)
            act.dma_start(w3[:, i, :, :], io["w3"][e].rearrange("(m p) d -> p m d", p=P)).then_inc(s_w[i], 16)

        def load_slots(e, i):
            sp.dma_start(xe[:, i, :, :], self.disp[bass.ds(e * CAP, CAP), :].rearrange("(a p) d -> p a d", p=P)
                         ).then_inc(s_x[i], 16)

        for i in range(2):
            load_weights(i, i)
        self.loaded(sp, "dispatched")
        for i in range(2):
            load_slots(i, i)

        def body(pair, last=False):
            for i in range(2):
                e = 2 * pair + i
                pe.wait_ge(s_x[i], (pair + 1) * 16)
                need(pe, "e.xT")
                for a in range(ST):
                    bk, col = (6, a) if a < 4 else (7, 0)
                    ins = pe.transpose(bank[bk][:, col * P:(col + 1) * P], xe[:, i, a, :], self.c["ident"])
                M("e.tr", ins)
                s.mark(f"e.tr{i}", s.pe)
                need(v, "e.tr", "e.mm")
                v.tensor_copy(xT[:, 0:512], bank[6][:, :])
                V("e.xT", v.tensor_copy(xT[:, 512:CAP], bank[7][:, 0:P]))
                pe.wait_ge(s_w[i], (pair + 1) * 48)
                need(pe, "e.xT")
                for m in range(H0 // P):
                    for half in range(2):
                        need(pe, f"e.h{half}")
                        cols = slice(half * HC, (half + 1) * HC)
                        pe.matmul(bank[2 * half][:, 0:HC], w12[:, i, 0, m * P:(m + 1) * P], xT[:, cols],
                                  start=True, stop=True)
                        M("e.mm", pe.matmul(bank[2 * half + 1][:, 0:HC], w12[:, i, 1, m * P:(m + 1) * P],
                                            xT[:, cols], start=True, stop=True))
                        need(act, "e.mm", f"e.h{half}")
                        S(f"e.sg{half}", act.activation(sg[:, cols], bank[2 * half][:, 0:HC], ACT.Silu))
                        need(v, f"e.sg{half}", "e.down")
                        V(f"e.h{half}", v.tensor_tensor(hs[:, m, cols], bank[2 * half + 1][:, 0:HC], sg[:, cols],
                                                        ALU.mult))
                need(pe, "e.h0", "e.h1")
                for a in range(ST):
                    bk, col = (4, a) if a < 4 else (5, 0)
                    need(pe, f"e.y{min(a, 4) // 4}")
                    for m in range(H0 // P):
                        ins = pe.matmul(bank[bk][:, col * P:(col + 1) * P], hs[:, m, a * P:(a + 1) * P],
                                        w3[:, i, m, :], start=(m == 0), stop=(m == H0 // P - 1))
                M("e.down", ins)
                s.mark(f"e.down{i}", s.pe)
                need(act, "e.down")
                if not isinstance(e, int) or e > 0:
                    act.wait_ge(s_y, e * 16)
                S("e.y0", act.copy(y[:, 0:4, :], bank[4][:, :].rearrange("p (a d) -> p a d", d=D)))
                S("e.y1", act.copy(y[:, 4, :], bank[5][:, 0:P]))
                need(sp, "e.y1")
                sp.dma_start(self.eout[bass.ds(e * CAP, CAP), :].rearrange("(a p) d -> p a d", p=P),
                             y[:]).then_inc(s_y, 16)
                if not last:
                    need(act, f"e.down{i}")
                    load_weights(e + 2, i)
                    need(sp, f"e.tr{i}")
                    load_slots(e + 2, i)

        s.loop(0, PAIRS - 1, body)
        body(PAIRS - 1, last=True)
        self.dma_sems["experts"], self.dma_total["experts"] = s_y, E0 * 16
        s.mark("experts", s.act)
        self.sp.wait_ge(s_y, E0 * 16)
        self.act.wait_ge(s_y, E0 * 16)
        self.end_phase()

    def l1_attention_setup(self):
        sb, io, g = self.sb, self.io, self.pool
        self.phase()
        self.Wq = sb("a_wq", [P, HD])
        self.Wk = sb("a_wk", [P, HD])
        self.Wv = sb("a_wv", [P, HD])
        self.Wo = sb("a_wo", [P, HD // P, D])
        self.csQ = sb("a_csq", [P, 2, T])
        self.G = [sb(f"a_g{k}", [P, NT, D]) for k in range(2)]
        self.state = sb("a_state", [P, NG, 2, 2, 2 * (DH + 1)])
        self.load("wq1", self.Wq[:], io["wq1"], self.act)
        self.load("wk1", self.Wk[:], io["wk1"])
        self.load("wv1", self.Wv[:], io["wv1"], self.act)
        self.load("wo1", self.Wo[:], io["wo1"].rearrange("(m p) d -> p m d", p=P))
        self.load("csq", self.csQ[:].rearrange("p k t -> p (k t)"), io["csq"].to_broadcast([P, 2 * T]), self.act)
        ring = [self.ctx.enter_context(self.nc.semaphore(f"dma_gather{k}")) for k in range(4)]
        self.gathered = self.ctx.enter_context(self.nc.semaphore("gathered_tiles"))
        self.loaded(g, "experts")
        for n in range(NT + len(ring)):
            done = n - len(ring)
            if done >= 0:
                g.wait_ge(ring[done % len(ring)], 32 * (done // len(ring) + 1))
                g.sem_inc(self.gathered, 1)
            if n < NT:
                for k in range(2):
                    g.indirect_dma_start(out=self.G[k][:, n, :], out_offset=None, in_=self.eout,
                                         in_offset=bass.IndirectOffsetOnAxis(ap=self.slot[k][:, n:n + 1], axis=0)
                                         ).then_inc(ring[n % len(ring)], 16)
        each = lambda name, shape, count=NG: [sb(f"a_{name}{i}", shape) for i in range(count)]
        self.Qp = each("qp", [P, 2, P])
        self.Qr = each("qr", [P, 2, 2, P])
        self.Kb = each("kb", [P, HG, DH])
        self.Kr = each("kr", [P, 2, HG, DH])
        self.Va = each("va", [P, HG, DH + 1])
        self.KT = each("kt", [P, 2, P])
        self.Sm = each("sm", [P, 2, 2, P], 2)
        self.den = sb("a_den", [P, HG])
        self.O = sb("a_o", [P, NH, DH])
        self.oT1 = sb("a_ot", [P, HD // P, P])
        self.hT1 = sb("a_ht", [P, P])
        self.xn1 = sb("a_xn", [P, D])
        self.mt1 = sb("a_mt", [P, D])
        self.yt1 = sb("a_yt", [P, D])
        self.st1 = self.stat_buffers("s1", 1)
        v = self.dve
        for va in self.Va:
            v.memset(va[:], 1.0)
        self.V("a.init", v.memset(self.state[:], 0.0))

    def a_mix(self, n):
        v, s = self.dve, self.s
        need, V = s.need, self.V
        x, b = self.X[:, n, :], n // TB
        v.wait_ge(self.gathered, n + 1)
        V("a.m", v.tensor_scalar(self.mt1[:], self.G[0][:, n, :], self.w0[0][:, bass.ds(n, 1)], None, ALU.mult))
        yield
        need(v, "a.m")
        V("a.m", v.scalar_tensor_tensor(self.mt1[:], self.G[1][:, n, :], self.w0[1][:, bass.ds(n, 1)], self.mt1[:],
                                        ALU.mult, ALU.add))
        yield
        need(v, "a.m")
        V("a.m", v.tensor_tensor(self.mt1[:], self.mt1[:], self.mB[0][:, b, 5, :], ALU.mult))
        yield
        need(v, "a.m")
        V("a.m", v.tensor_tensor(x, x, self.mt1[:], ALU.add))
        s.mark("a.mixed", s.dve)

    def a_pre(self, n):
        v, s = self.dve, self.s
        need, V = s.need, self.V
        x = self.X[:, n, :]
        st, mv, y, h, t = self.st1
        s.need_apart(v, "a.mixed")
        V("a.st", v.bn_stats(st[:, 0, :], x))
        yield
        s.need_apart(v, "a.st")
        V("a.mv", v.bn_aggr(mv[:, 0, :], st[:, 0, :]))
        yield
        need(v, "a.mv")
        V("a.v", v.tensor_scalar(t[:], mv[:, :, 1], EPS, None, ALU.add))
        V("a.hh", v.tensor_scalar(h[:], mv[:, :, 1], EPS, -0.5, ALU.add, ALU.mult))
        yield
        need(v, "a.v")
        V("a.y0", v.tensor_scalar(y[:].bitcast(I32), t[:].bitcast(I32), -0.5, 1597463007.0, ALU.mult, ALU.add))
        yield
        for _ in range(3):
            need(v, "a.y0", "a.hh")
            V("a.t", v.scalar_tensor_tensor(t[:], y[:], h[:], y[:], ALU.mult, ALU.mult))
            yield
            need(v, "a.t")
            V("a.y0", v.scalar_tensor_tensor(y[:], t[:], 1.5, y[:], ALU.add, ALU.mult))
            yield
        need(v, "a.y0", "a.xT")
        self.normed("a.xn", self.xn1[:], x, 0, self.st1)

    def a_ready(self, n):
        pe, act, b = self.pe, self.act, n // TB
        self.s.need(pe, "a.xn", "a.Yread", "a.oTc")
        self.M("a.xT", pe.transpose(self.bank[7][:, 0:P], self.xn1[:], self.c["ident"]))
        self.s.need_apart(act, "a.xT", "a.kvmm")
        self.S("a.hT", act.activation(self.hT1[:], self.bank[7][:, 0:P], ACT.Identity,
                                      scale=at1(self.mT[1][:, 1, :], b), bias=at1(self.mT[1][:, 0, :], b)))

    def a_project(self, n, g):
        v, s, pe, act, bank = self.dve, self.s, self.pe, self.act, self.bank
        need, V, S, M = s.need, self.V, self.S, self.M
        w = HG * DH
        need(pe, "a.hT", "a.Qp", "a.KTc")
        for j in range(2):
            ins = pe.matmul(bank[0][:, j * P:(j + 1) * P], self.Wq[:, (2 * g + j) * P:(2 * g + j + 1) * P],
                            self.hT1[:], start=True, stop=True)
        M("a.qmm", ins)
        need(pe, "a.Va")
        pe.matmul(bank[1][:, 0:w], self.hT1[:], self.Wk[:, g * w:(g + 1) * w], start=True, stop=True)
        M("a.kvmm", pe.matmul(bank[1][:, w:2 * w], self.hT1[:], self.Wv[:, g * w:(g + 1) * w],
                              start=True, stop=True))
        need(v, "a.kvmm", f"a.Kr{g}", f"a.KT{g}")
        V("a.Kb", v.tensor_tensor(self.Kb[g][:].rearrange("p h d -> p (h d)"), bank[1][:, 0:w],
                                  self.c["bk1"][:, g * w:(g + 1) * w], ALU.add))
        s.mark(f"a.Kb{g}", s.dve)
        need(v, f"a.U{g}", f"a.I{g}")
        V("a.Va", v.tensor_tensor(self.Va[g][:, :, 0:DH], bank[1][:, w:2 * w].rearrange("p (h d) -> p h d", d=DH),
                                  self.c["bv1"][:, g * w:(g + 1) * w].rearrange("p (h d) -> p h d", d=DH), ALU.add))
        s.mark(f"a.Va{g}", s.dve)
        need(act, "a.qmm", f"a.Qr{g}", f"a.S{g}")
        for j in range(2):
            ins = act.activation(self.Qp[g][:, j, :], bank[0][:, j * P:(j + 1) * P], ACT.Relu,
                                 bias=self.c["bq1"][:, 2 * g + j:2 * g + j + 1])
        S("a.Qp", ins)
        s.mark(f"a.Qp{g}", s.act)
        s.need_apart(act, "a.Kb", f"a.U{g}")
        for k in range(2):
            ins = act.activation(self.Kr[g][:, k, :, :], self.Kb[g][:], ACT.Relu,
                                 scale=self.c[("cos1", "sin1")[k]][:, bass.ds(n, 1)])
        S(f"a.Kr{g}", ins)

    def a_queries(self, n, g):
        v, need = self.dve, self.s.need
        c = n % TB
        need(v, f"a.Qp{g}", f"a.I{g}")
        self.V(f"a.Qr{g}", v.tensor_tensor(self.Qr[g][:], self.Qp[g][:].unsqueeze(1).to_broadcast([P, 2, 2, P]),
                                           self.csQ[:, :, tokens(c, 1)].unsqueeze(2).to_broadcast([P, 2, 2, P]),
                                           ALU.mult))

    def a_keys_turned(self, g):
        pe, act = self.pe, self.act
        need = self.s.need
        need(pe, f"a.Kb{g}", "a.Qp", "a.KTc")
        for j in range(2):
            ins = pe.transpose(self.bank[0][:, (2 + j) * P:(3 + j) * P],
                               self.Kb[g][:, 2 * j:2 * j + 2, :].rearrange("p h d -> p (h d)"), self.c["ident"])
        self.M(f"a.KT{g}", ins)
        need(act, f"a.KT{g}", f"a.S{g}")
        self.S("a.KTc", act.activation(self.KT[g][:].rearrange("p j t -> p (j t)"), self.bank[0][:, 2 * P:],
                                       ACT.Relu))
        self.s.mark(f"a.KTc{g}", self.s.act)

    def a_scores(self, g):
        v, s, pe, bank, i = self.dve, self.s, self.pe, self.bank, g % 2
        need = s.need
        need(pe, f"a.KTc{g}", f"a.Qp{g}", "a.Sm")
        for h in range(HG):
            j, half = h // 2, h % 2
            p = slice(half * DH, (half + 1) * DH)
            ins = pe.matmul(bank[2 + half][:, j * P:(j + 1) * P], self.KT[g][p, j, :], self.Qp[g][p, j, :],
                            start=True, stop=True)
        self.M(f"a.S{g}", ins)
        need(v, f"a.S{g}", f"a.I{(g - 2) % NG}")
        self.V("a.Sm", v.tensor_tensor(self.Sm[i][:], self.psum[:, 2:4, 0:2 * P].rearrange("p x (j t) -> p x j t", j=2),
                                       self.c["cosmask"].unsqueeze(1).unsqueeze(1).to_broadcast([P, 2, 2, P]),
                                       ALU.mult))
        s.mark(f"a.Sm{i}", s.dve)

    def a_update(self, g):
        pe, bank, need = self.pe, self.bank, self.s.need
        need(pe, f"a.Va{g}", f"a.Kr{g}", "a.state")
        w = 2 * (DH + 1)
        for k in range(2):
            for j in range(2):
                ins = pe.matmul(bank[5 + k][:, j * 256:j * 256 + w],
                                self.Kr[g][:, k, 2 * j:2 * j + 2, :].rearrange("p h d -> p (h d)"),
                                self.Va[g][:, 2 * j:2 * j + 2, :].rearrange("p h d -> p (h d)"),
                                start=True, stop=True)
        self.M(f"a.U{g}", ins)

    def a_values(self, n, g):
        v, s, pe, bank, i = self.dve, self.s, self.pe, self.bank, g % 2
        need, V, M = s.need, self.V, self.M
        need(pe, f"a.Sm{i}", f"a.Qr{g}", "a.On", "a.state", "a.init")
        w = 2 * (DH + 1)
        for j in range(2):
            pair = bank[4][:, j * w:(j + 1) * w]
            for k in range(2):
                pe.matmul(pair, self.Qr[g][:, k, j, :],
                          self.state[:, g, k, j, :],
                          start=(k == 0), stop=False)
            for h in (2 * j, 2 * j + 1):
                ins = pe.matmul(bank[4][:, h * 65:(h + 1) * 65], self.Sm[i][:, h % 2, j, :], self.Va[g][:, h, :],
                                start=False, stop=(h % 2 == 1))
        M(f"a.I{g}", ins)
        need(v, f"a.I{g}")
        o4 = bank[4][:, 0:HG * 65].rearrange("p (h d) -> p h d", d=65)
        V("a.den", v.tensor_scalar(self.den[:], o4[:, :, DH], 1e-6, None, ALU.max))
        for half in range(2):
            p = slice(half * DH, (half + 1) * DH)
            cols = slice(half * (DH + 1), (half + 1) * (DH + 1))
            st = self.state[p, g, :, :, cols].rearrange("p k j d -> p (k j) d")
            u = self.psum[p, 5:7, :].rearrange("p k (j x) -> p (k j) x", j=2)[:, :, cols]
            ins = v.scalar_tensor_tensor(st, st, self.c["keep"][p, bass.ds(n, 1)], u, ALU.mult, ALU.add)
            if half == 0:
                V("a.st0", ins)
                need(v, "a.den")
                V("a.den", v.reciprocal(self.den[:], self.den[:]))
        V("a.state", ins)
        need(v, "a.den", f"a.oT{g}")
        V("a.On", v.tensor_tensor(self.O[:, HG * g:HG * (g + 1), :], o4[:, :, 0:DH],
                                  self.den[:].unsqueeze(2).to_broadcast([P, HG, DH]), ALU.mult))
        s.mark(f"a.On{g}", s.dve)

    def a_turned(self, g):
        pe, act, need = self.pe, self.act, self.s.need
        need(pe, f"a.On{g}", "a.oTc", "a.hT", "a.Yread")
        for j in range(2):
            blk = 2 * g + j
            ins = pe.transpose(self.bank[7][:, j * P:(j + 1) * P],
                               self.O[:, 2 * blk:2 * blk + 2, :].rearrange("p h d -> p (h d)"), self.c["ident"])
        self.M(f"a.oT{g}", ins)
        need(act, f"a.oT{g}", "a.Y")
        self.S("a.oTc", act.copy(self.oT1[:, 2 * g:2 * g + 2, :],
                                 self.bank[7][:, 0:2 * P].rearrange("p (j t) -> p j t", j=2)))

    def a_output(self, n):
        v, s, pe, bank = self.dve, self.s, self.pe, self.bank
        need, V, M = s.need, self.V, self.M
        need(pe, "a.oTc", "a.hT", "a.Yread")
        for m in range(HD // P):
            ins = pe.matmul(bank[7][:, 0:D], self.oT1[:, m, :], self.Wo[:, m, :], start=(m == 0),
                            stop=(m == HD // P - 1))
        M("a.Y", ins)
        need(v, "a.Y")
        V("a.Yread", v.tensor_tensor(self.yt1[:], bank[7][:, 0:D], self.c["bo1"], ALU.add))
        need(v, "a.Yread")
        V("a.y", v.tensor_tensor(self.yt1[:], self.yt1[:], self.mB[1][:, n // TB, 2, :], ALU.mult))
        need(v, "a.y")
        x = self.X[:, n, :]
        V("a.x", v.tensor_tensor(x, x, self.yt1[:], ALU.add))

    def a_step(self, n, g, pre=None, first=0, last=NT * NG):
        at = lambda d: (n + (g + d) // NG, (g + d) % NG)
        known = lambda d: first <= g + d < last

        def steps(count):
            for _ in range(count):
                next(pre, None) if pre else None

        if known(2):
            self.a_project(*at(2))
        steps(2)
        if known(0):
            self.a_scores(g)
        if known(1):
            self.a_keys_turned(at(1)[1])
            self.a_queries(*at(1))
        steps(3)
        if known(-1):
            self.a_update(at(-1)[1])
        if g == 2 and known(-3):
            self.a_output(n - 1)
        if g == 1 and pre:
            steps(20)
            self.a_ready(n + 1)
        if known(-1):
            self.a_values(*at(-1))
        steps(3)
        if known(-2):
            self.a_turned(at(-2)[1])

    def l1_attention(self):
        s = self.s
        self.l1_attention_setup()
        self.loaded(self.pe, "wq1", "wk1", "wv1", "wo1")
        self.loaded(self.dve, "csq")
        s.need(self.act, "mod1")

        def body(n, first=-NG, last=3 * NG):
            pre = self.a_pre(n + 1) if last > NG else None
            mix = self.a_mix(n + 2) if last > 2 * NG else None
            for g in range(NG):
                self.a_step(n, g, (pre, pre, None, mix)[g], first, last)

        for _ in self.a_mix(0):
            pass
        for _ in self.a_pre(0):
            pass
        self.a_ready(0)
        for _ in self.a_mix(1):
            pass
        self.a_step(0, -2)
        self.a_step(0, -1)
        body(0, first=0)
        s.loop(1, NT - 2, body)
        body(NT - 2, last=2 * NG)
        body(NT - 1, last=NG)
        self.a_step(NT - 1, NG, first=0, last=NG)
        self.a_step(NT - 1, NG + 1, first=0, last=NG)
        self.a_output(NT - 1)
        self.end_phase()

    def l1_moe(self):
        s = self.s
        io, sb = self.io, self.sb
        self.phase()
        self.Wgu = sb("m_wgu", [P, 2, (MB + 1) * P])
        self.Wd = sb("m_wd", [P, MB + 1, D])
        self.Wr = sb("m_wr", [P, E1])
        self.load("wgu", self.Wgu[:], io["wgu"], self.act)
        self.load("wr", self.Wr[:], io["wr"])
        self.load("wd", self.Wd[:], io["wd"].rearrange("(m p) d -> p m d", p=P))
        self.ex_in = sb("m_ex0", [2 * E1, MB * P])
        self.load("expand", self.ex_in[:], io["expand"], self.act)
        self.ex = sb("m_ex", [2 * E1, MB * P], F32R)
        self.h3T = sb("m_h3t", [P, NT * P])
        self.lg1 = sb("m_lg", [P, NT, E1])
        self.xn3 = sb("m_xn", [P, G4, D])
        self.hl3 = sb("m_hl", [P, G4, P])
        self.st3 = self.stat_buffers("s3", G4)
        self.sg3 = [sb(f"m_sg{k}", [P, G4 * P]) for k in range(2)]
        self.hd3 = [sb(f"m_hd{k}", [P, G4 * P]) for k in range(MB + 1)]
        self.comb = sb("m_comb", [P, NT, 2, E1], F32R)
        self.combT = sb("m_combt", [2 * E1, NT * P], F32R)
        self.yo = sb("m_yo", [P, G4, D])
        self.loaded(self.pe, "wr", "wgu", "wd")
        s.loop(0, NT // G4, self.m_logits)
        self.m_routing()
        self.stored = self.ctx.enter_context(self.nc.semaphore("dma_stored"))
        s.loop(0, NT // G4, self.m_experts)
        self.sp.wait_ge(self.stored, NT // G4 * 16)
        self.end_phase()

    def m_logits(self, gi):
        v, s, pe, act, bank = self.dve, self.s, self.pe, self.act, self.bank
        need, V, S, M = s.need, self.V, self.S, self.M
        b, n0 = gi // (TB // G4), gi * G4
        tiles = [self.X[:, n0 + i, :] for i in range(G4)]
        self.stats("ln5", tiles, self.st3)
        need(v, "m.xT")
        for i in range(G4):
            self.normed("m.xn", self.xn3[:, i, :], tiles[i], i, self.st3)
        need(pe, "m.xn", "m.hT")
        for i in range(G4):
            ins = pe.transpose(bank[0][:, i * P:(i + 1) * P], self.xn3[:, i, :], self.c["ident"])
        M("m.xT", ins)
        self.s.need_apart(act, "m.xT", "m.lgmm")
        flat = self.hl3[:].rearrange("p n t -> p (n t)")
        S("m.hT", act.activation(flat, bank[0][:, :], ACT.Identity, scale=at1(self.mT[1][:, 4, :], b),
                                 bias=at1(self.mT[1][:, 3, :], b)))
        need(self.pool, "m.hT")
        self.GP("m.h3", self.pool.tensor_copy(self.h3T[:, tokens(n0, G4)], flat))
        need(pe, "m.hT", "m.lg")
        for i in range(G4):
            ins = pe.matmul(bank[1][:, i * E1:(i + 1) * E1], self.hl3[:, i, :], self.Wr[:], start=True, stop=True)
        M("m.lgmm", ins)
        need(v, "m.lgmm")
        V("m.lg", v.tensor_copy(self.lg1[:, bass.ds(n0, G4), :],
                                bank[1][:, 0:G4 * E1].rearrange("p (n e) -> p n e", e=E1)))
        need(act, "m.h3")

    def m_routing(self):
        v, s, pe, act, bank = self.dve, self.s, self.pe, self.act, self.bank
        need, V, S, M, sb = s.need, self.V, self.S, self.M, self.sb
        oh = [sb(f"m_oh{k}", [P, NT, E1]) for k in range(2)]
        top = [sb(f"m_top{k}", [P, NT]) for k in range(2)]
        z, w1, w2 = (sb(f"m_{x}", [P, NT]) for x in ("z", "w1", "w2"))
        dl, cm = sb("m_dl", [P, NT, E1]), sb("m_cm", [P, NT, E1])
        self.loaded(v, "expand")
        V("m.ex", v.tensor_copy(self.ex[:], self.ex_in[:]))
        need(v, "m.lg")
        self.top2("t1", self.lg1[:], [o[:] for o in oh], NT, E1, self.c["iota16"], [t[:] for t in top])
        V("m.dl", v.tensor_tensor(dl[:], self.lg1[:], top[0][:].unsqueeze(2).to_broadcast([P, NT, E1]), ALU.subtract))
        V("m.d2", v.tensor_tensor(w2[:], top[1][:], top[0][:], ALU.subtract))
        need(act, "m.d2")
        act.activation(dl[:], dl[:], ACT.Exp)
        S("m.exp", act.activation(w2[:], w2[:], ACT.Exp))
        need(v, "m.exp")
        V("m.z", v.tensor_reduce(z[:], dl[:], AX.X, ALU.add))
        need(v, "m.z")
        V("m.z", v.scalar_tensor_tensor(z[:], z[:], 1e-9, w2[:], ALU.mult, ALU.add))
        need(v, "m.z")
        V("m.z", v.tensor_scalar(z[:], z[:], 1.0, None, ALU.add))
        need(v, "m.z")
        V("m.w1", v.reciprocal(w1[:], z[:]))
        need(v, "m.w1")
        V("m.w2", v.tensor_tensor(w2[:], w2[:], w1[:], ALU.mult))
        need(v, "m.w2")
        for k, w in enumerate((w1, w2)):
            V(f"m.oh{k}", v.tensor_tensor(oh[k][:], oh[k][:], w[:].unsqueeze(2).to_broadcast([P, NT, E1]), ALU.mult))
        need(v, "m.oh1")
        V("m.cm", v.tensor_tensor(cm[:], oh[0][:], oh[1][:], ALU.add))
        need(v, "m.cm")
        V("m.hi", v.tensor_copy(self.comb[:, :, 0, :], cm[:]))
        need(v, "m.hi")
        V("m.lo", v.tensor_tensor(self.comb[:, :, 1, :], cm[:], self.comb[:, :, 0, :].bitcast(F32), ALU.subtract))
        need(pe, "m.lo")
        for q in range(NT // G4):
            bk = bank[2 + q % 2]
            need(pe, f"m.ct{q % 2}")
            for i in range(G4):
                ins = pe.transpose(bk[0:2 * E1, i * P:(i + 1) * P],
                                   self.comb[:, q * G4 + i, :, :].rearrange("p k e -> p (k e)").bitcast(F32),
                                   self.c["ident"])
            M("m.ctT", ins)
            need(act, "m.ctT")
            S(f"m.ct{q % 2}", act.copy(self.combT[:, q * G4 * P:(q + 1) * G4 * P], bk[0:2 * E1, :]))

    def m_experts(self, gi):
        v, s, pe, act, bank = self.dve, self.s, self.pe, self.act, self.bank
        need, V, S, M = s.need, self.V, self.S, self.M
        b, n0 = gi // (TB // G4), gi * G4
        sl = tokens(n0, G4)
        need(pe, "m.h3", "m.ct0", "m.ct1", "m.ex")
        order = [MB] + list(range(MB))
        for j, blk in enumerate(order):
            i = j % 2
            need(pe, f"m.h{i}")
            pe.matmul(bank[2 * i][:, :], self.Wgu[:, 0, blk * P:(blk + 1) * P], self.h3T[:, sl], start=True, stop=True)
            M(f"m.gu{i}", pe.matmul(bank[2 * i + 1][:, :], self.Wgu[:, 1, blk * P:(blk + 1) * P], self.h3T[:, sl],
                                    start=True, stop=True))
            if blk < MB:
                self.s.need_apart(pe, f"m.hc{i}")
                M(f"m.ce{i}", pe.matmul(bank[4 + i][:, :], self.ex[:, blk * P:(blk + 1) * P], self.combT[:, sl],
                                        start=True, stop=True))
            need(act, f"m.gu{i}", f"m.h{i}")
            S(f"m.sg{i}", act.activation(self.sg3[i][:], bank[2 * i][:, :], ACT.Silu))
            hd = self.hd3[blk]
            need(v, f"m.sg{i}", "m.down")
            V(f"m.h{i}", v.tensor_tensor(hd[:], bank[2 * i + 1][:, :], self.sg3[i][:], ALU.mult))
            if blk < MB:
                need(v, f"m.h{i}", f"m.ce{i}")
                V(f"m.hc{i}", v.tensor_tensor(hd[:], bank[4 + i][:, :], hd[:], ALU.mult))
        need(pe, "m.hc0", "m.hc1", "m.y")
        for i in range(G4):
            for j, blk in enumerate(order):
                ins = pe.matmul(bank[6][:, i * P:(i + 1) * P], self.hd3[blk][:, i * P:(i + 1) * P], self.Wd[:, blk, :],
                                start=(j == 0), stop=(j == MB))
        M("m.down", ins)
        need(v, "m.down", "m.x")
        V("m.y", v.tensor_tensor(self.yo[:], bank[6][:, :].rearrange("p (n d) -> p n d", d=D),
                                 rows(self.mB[1][:, b, 5, :], G4), ALU.mult))
        need(v, "m.y")
        x = self.X[:, bass.ds(n0, G4), :]
        V("m.x", v.tensor_tensor(x, x, self.yo[:], ALU.add))
        need(self.sp, "m.x")
        self.sp.dma_start(self.io["out"].rearrange("b (c p) d -> p (b c) d", p=P)[:, bass.ds(n0, G4), :],
                          x).then_inc(self.stored, 16)

    def build(self):
        self.setup()
        self.rotation()
        self.layer0_attention()
        self.l0_routing()
        self.l0_experts()
        self.end_phase()
        self.l1_attention()
        self.l1_moe()


def build(nc, io):
    with ExitStack() as ctx:
        Kernel(nc, ctx, io).build()


def at1(ap, b):
    return ap[:, bass.ds(b, 1)]


def tokens(n0, count):
    return bass.ds(n0 * P, count * P)


CONSTS = [("ident", P), ("headmask", P), ("upto", P), ("ones", P), ("pos", TB), ("iota8", E0), ("iota16", E1),
          ("cos1", NT), ("sin1", NT), ("keep", NT), ("cosmask", P)]
COLS = [("cT", 2 * B), ("bq", 1), ("bu", 1), ("lnw", 1), ("lnb", 1), ("bq1", NH // 2)]
ROWS = [("theta", D), ("bkv", 2 * D), ("bout", D), ("bg", E0), ("bk1", HD), ("bv1", HD), ("bo1", D)]


def layout(i):
    f = {k: np.asarray(a) for k, a in i.items()}
    j = np.arange(P)
    angle = np.float32(np.pi / (2.0 * T)) * np.arange(T, dtype=np.float32)
    cs, sn = np.cos(angle).astype(np.float32), np.sin(angle).astype(np.float32)
    consts = np.concatenate([
        np.eye(P), (j[:, None] // 8 == j[None, :] // 8), (j[:, None] <= j[None, :]), np.ones((P, P)),
        j[:, None] + P * np.arange(TB)[None, :],
        np.broadcast_to(np.arange(E0)[None, :], (P, E0)), np.broadcast_to(np.arange(E1)[None, :], (P, E1)),
        np.tile(cs.reshape(TB, P).T, (1, B)), np.tile(sn.reshape(TB, P).T, (1, B)),
        np.broadcast_to((np.arange(NT) % TB != 0)[None, :], (P, NT)),
        np.where(j[:, None] <= j[None, :], np.cos(np.pi / (2.0 * T) * (j[None, :] - j[:, None])), 0.0),
    ], axis=1).astype(np.float32)
    bqkvu = f["L0_attn_bqkvu"]
    cols = np.concatenate([
        f["L0_c"].T, f["L1_c"].T, bqkvu[0:D, None], bqkvu[3 * D:, None], f["L0_attn_ln_w"][:, None],
        f["L0_attn_ln_b"][:, None], f["L1_attn_bq"].reshape(NH // 2, P).T,
    ], axis=1)
    rws = np.concatenate([f["L0_attn_theta"].reshape(-1), bqkvu[D:3 * D], f["L0_attn_bout"], f["L0_ffn_bg"],
                          f["L1_attn_bk"], f["L1_attn_bv"], f["L1_attn_bo"]])[None, :]
    return {
        "x": f["L0_attn_x"], "cols": cols, "consts": consts, "rows": rws,
        "wmod0": f["L0_wmod"], "wmod1": f["L1_wmod"], "w0": f["L0_attn_Wqkvu"].T, "wo0": f["L0_attn_Wout"].T,
        "csq": np.concatenate([np.where(np.arange(T) < P, 0, w) for w in (cs, sn)])[None, :].astype(np.float32),
        "wq1": f["L1_attn_Wq"], "wk1": f["L1_attn_Wk"], "wv1": f["L1_attn_Wv"],
        "wo1": f["L1_attn_Wo"],
        "wgu": np.stack([np.concatenate([f[f"L1_ffn_w{k}_r"].transpose(1, 0, 2).reshape(D, E1 * MR),
                                         f[f"L1_ffn_w{k}_s"].transpose(1, 0, 2).reshape(D, NS * MS)], axis=1)
                         for k in "gu"], axis=1),
        "wd": np.concatenate([f["L1_ffn_wd_r"].reshape(E1 * MR, D), f["L1_ffn_wd_s"].reshape(NS * MS, D)]),
        "wr": f["L1_ffn_router_w"],
        "expand": (np.arange(2 * E1)[:, None] % E1 == np.arange(E1 * MR)[None, :] // MR).astype(np.float32),
        "wg0": f["L0_ffn_Wg"], "w1": f["L0_ffn_W1"], "w2": f["L0_ffn_W2"], "w3": f["L0_ffn_W3"],
    }


def kernel(**inputs):
    import concourse.bacc as bacc
    from concourse.bass_utils import run_bass_kernel_spmd

    nc = bacc.Bacc("TRN2", target_bir_lowering=False, num_devices=1)
    arrays, io = {}, {}
    for name, a in layout(inputs).items():
        arrays[f"in_{name}"] = np.ascontiguousarray(a)
        io[name] = nc.dram_tensor(f"in_{name}", a.shape, mybir.dt.from_np(a.dtype), kind="ExternalInput").ap()
    io["out"] = nc.dram_tensor("out", (B, T, D), F32, kind="ExternalOutput").ap()
    build(nc, io)
    r = run_bass_kernel_spmd(nc, [arrays], core_ids=[0])
    return r.results[0]["out"]
```

```python
from contextlib import ExitStack

import numpy as np

import concourse.bass as bass
from concourse import mybir
from concourse.alu_op_type import AluOpType as ALU

ACT = mybir.ActivationFunctionType
F32 = mybir.dt.float32
F32R = mybir.dt.float32r
I32 = mybir.dt.int32
AX = mybir.AxisListType

P = 128
B, T, D = 4, 1024, 128
TB = T // P
NT = B * TB
G4 = 4
EPS = 1e-5
E0, H0 = 8, 512
CAP = int(B * T / E0 * 1.25)
ST = CAP // P
NSLOT = E0 * CAP
NH, DH = 16, 64
HD = NH * DH
HG = 4
NG = NH // HG
E1, MR = 16, 32
NS, MS = 2, 64
MB = E1 * MR // P
TWO_PI = 6.283185307179586
C1 = 6.28125
C2 = float(np.float32(round((TWO_PI - C1) * 2.0**20) / 2.0**20))
C3 = float(TWO_PI - C1 - C2)
ROUND = 12582912.0
PI32 = 3.1415925


TPE, ACTE, DVE = "tensor", "scalar", "vector"


class Engine:

    def __init__(self, name, eng, sem):
        self.name, self.eng, self.sem = name, eng, sem
        self.base, self.k, self.per = 0, 0, 0

    def inc(self, ins):
        ins.then_inc(self.sem, 1)
        self.k += 1
        return self


class Sync:

    def __init__(self, nc, ctx):
        self.nc = nc
        mk = lambda n, e: Engine(n, e, ctx.enter_context(nc.semaphore(f"done_{n}")))
        self.pe, self.act = mk("pe", nc.tensor), mk("act", nc.scalar)
        self.dve, self.pool = mk("dve", nc.vector), mk("pool", nc.gpsimd)
        self.all = [self.pe, self.act, self.dve, self.pool]
        self.marks, self.waited = {}, {}
        self.turn = 0

    def mark(self, name, e):
        self.marks[name] = (e, self.turn, e.k, e.base if isinstance(e.base, int) else None)

    def did(self, name, e, ins):
        e.inc(ins)
        self.mark(name, e)

    def alias(self, new, old):
        if old in self.marks:
            self.marks[new] = self.marks[old]

    def value(self, name):
        e, turn, k, base = self.marks[name]
        rolled = not isinstance(e.base, int)
        if turn == self.turn:
            return e, ((1, k) if rolled else (0, e.base + k))
        if rolled and turn == self.turn - 1:
            return e, (1, k - e.per)
        return e, (0, base + k)

    def need(self, waiter, *names, apart=False):
        latest = {}
        for name in names:
            if name in self.marks:
                e, v = self.value(name)
                latest[e.name] = max(latest.get(e.name, (e, v)), (e, v), key=lambda x: x[1])
        waits = []
        for e, v in latest.values():
            key = (id(waiter), e.name)
            turn, done = self.waited.get(key, (-1, (0, 0)))
            if turn == self.turn and done >= v:
                continue
            self.waited[key] = (self.turn, v)
            waits.append((e.sem, e.base + v[1] if v[0] else v[1]))
        if apart and any(not isinstance(value, int) for _, value in waits):
            waits = [(sem, value if isinstance(value, int) else waiter.to_reg(value)) for sem, value in waits]
            waiter.wait_ge(next(e.sem for e in self.all if e.eng is waiter), 1)
        for sem, value in waits:
            waiter.wait_ge(sem, value)

    def need_apart(self, waiter, *names):
        self.need(waiter, *names, apart=True)

    def loop(self, first, last, body):
        def counted(n):
            self.turn += 1
            before = [e.k for e in self.all]
            body(n)
            return [e.k - b for e, b in zip(self.all, before)]
        for e in self.all:
            e.base += e.k
            e.k = 0
        got = counted(first)
        for e, g in zip(self.all, got):
            e.per = g
        start = [e.base + g for e, g in zip(self.all, got)]
        with self.nc.Fori(first + 1, last) as n:
            for e, s in zip(self.all, start):
                e.base, e.k = n * e.per + (s - (first + 1) * e.per), 0
            again = counted(n)
            assert again == got, (got, again)
        for e, s in zip(self.all, start):
            e.base, e.k = s + (last - first - 1) * e.per, 0
        self.turn += 1
        for m, (e, turn, k, base) in list(self.marks.items()):
            if turn == self.turn - 1 and base is None:
                self.marks[m] = (e, turn, k - e.per, e.base)


def rows(ap, count):
    p, w = ap.shape
    return ap.unsqueeze(1).to_broadcast([p, count, w])


class Kernel:

    def __init__(self, nc, ctx, io):
        self.nc, self.ctx, self.io = nc, ctx, io
        self.mem, self.outer, self.scratch = ctx, [], {}
        self.s = Sync(nc, ctx)
        self.pe, self.act, self.dve, self.pool, self.sp = nc.tensor, nc.scalar, nc.vector, nc.gpsimd, nc.sync
        self.psum = ctx.enter_context(nc.psum_tensor("psum", [P, 8, 512], F32))
        self.bank = [self.psum[:, i, :] for i in range(8)]
        self.dma_sems, self.dma_total = {}, {}

    def sb(self, name, shape, dt=F32):
        return self.mem.enter_context(self.nc.sbuf_tensor(f"sb_{name}", shape, dt))

    def phase(self):
        self.outer.append(self.mem)
        self.mem = ExitStack()
        self.scratch = {}

    def end_phase(self):
        for waiter in (self.pe, self.act, self.dve, self.pool, self.sp):
            for e in self.s.all:
                waiter.wait_ge(e.sem, e.base + e.k)
        self.mem.close()
        self.mem = self.outer.pop()
        self.scratch = {}

    def V(self, name, ins):
        self.s.did(name, self.s.dve, ins)

    def S(self, name, ins):
        self.s.did(name, self.s.act, ins)

    def M(self, name, ins):
        self.s.did(name, self.s.pe, ins)

    def GP(self, name, ins):
        self.s.did(name, self.s.pool, ins)

    def load(self, name, out, in_, queue=None):
        sem = self.ctx.enter_context(self.nc.semaphore(f"dma_{name}"))
        self.dma_sems[name] = sem
        self.dma_total[name] = 16
        (queue or self.sp).dma_start(out, in_).then_inc(sem, 16)

    def loaded(self, waiter, *names):
        for name in names:
            waiter.wait_ge(self.dma_sems[name], self.dma_total[name])

    def stats(self, tag, tiles, buf):
        v, need, V = self.dve, self.s.need, self.V
        st, mv, y, h, t, nm = buf
        n = len(tiles)
        for i, x in enumerate(tiles):
            ins = v.bn_stats(st[:, i, :], x)
        V(f"{tag}.st", ins)
        yield DVE, 0.2 * n
        self.s.need_apart(v, f"{tag}.st")
        for i in range(n):
            ins = v.bn_aggr(mv[:, i, :], st[:, i, :])
        V(f"{tag}.mv", ins)
        yield DVE, 0.07 * n
        need(v, f"{tag}.mv")
        V(f"{tag}.v", v.tensor_scalar(t[:, 0:n], mv[:, 0:n, 1], EPS, None, ALU.add))
        V(f"{tag}.h", v.tensor_scalar(h[:, 0:n], mv[:, 0:n, 1], EPS, -0.5, ALU.add, ALU.mult))
        yield DVE, 0.15
        need(v, f"{tag}.v")
        V(f"{tag}.y", v.tensor_scalar(y[:, 0:n].bitcast(I32), t[:, 0:n].bitcast(I32), -0.5, 1597463007.0,
                                      ALU.mult, ALU.add))
        yield DVE, 0.07
        for _ in range(3):
            need(v, f"{tag}.y")
            V(f"{tag}.t", v.tensor_tensor(t[:, 0:n], y[:, 0:n], y[:, 0:n], ALU.mult))
            yield DVE, 0.07
            need(v, f"{tag}.t")
            V(f"{tag}.t", v.tensor_tensor(t[:, 0:n], t[:, 0:n], h[:, 0:n], ALU.mult))
            yield DVE, 0.07
            need(v, f"{tag}.t")
            V(f"{tag}.y", v.scalar_tensor_tensor(y[:, 0:n], t[:, 0:n], 1.5, y[:, 0:n], ALU.add, ALU.mult))
            yield DVE, 0.07
        need(v, f"{tag}.y")
        V(f"{tag}.nm", v.scalar_tensor_tensor(nm[:, 0:n], mv[:, 0:n, 0], -1.0, y[:, 0:n], ALU.mult, ALU.mult))
        yield DVE, 0.07

    def normed(self, name, tag, outs, tiles, buf, *free):
        _, _, y, _, _, nm = buf
        self.s.need_apart(self.act, f"{tag}.nm", *free)
        for i, (out, x) in enumerate(zip(outs, tiles)):
            ins = self.act.activation(out, x, ACT.Identity, scale=y[:, i:i + 1], bias=nm[:, i:i + 1])
        self.S(name, ins)

    def stat_buffers(self, tag, n):
        return (self.sb(f"{tag}_st", [P, n, 6]), self.sb(f"{tag}_mv", [P, n, 2]), self.sb(f"{tag}_y", [P, n]),
                self.sb(f"{tag}_h", [P, n]), self.sb(f"{tag}_t", [P, n]), self.sb(f"{tag}_nm", [P, n]))

    def setup(self):
        nc, io, v, s, pe = self.nc, self.io, self.dve, self.s, self.pe
        need, V, S, M = s.need, self.V, self.S, self.M
        sb = self.sb
        self.X = sb("x", [P, NT, D])
        self.cols = sb("cols", [P, io["cols"].shape[1]])
        self.consts = sb("consts", [P, io["consts"].shape[1]])
        self.rowsb = sb("rows", [P, io["rows"].shape[1]])
        self.mT = [sb(f"mt{i}", [P, 6, B]) for i in range(2)]
        self.mB = [sb(f"mb{i}", [P, B, 6, D]) for i in range(2)]
        self.w0 = [sb(f"w0_{k}", [P, NT]) for k in range(2)]
        self.slot = [sb(f"slot{k}", [P, NT], I32) for k in range(2)]
        self.Wkv = [sb(f"wkv{k}", [P, NG, 2 * HG * DH], F32R) for k in range(2)]
        self.Wgus = [sb(f"wgus{k}", [P, 2, (MB + 1) * P], F32R) for k in range(2)]
        self.phase()
        self.wmod = [sb(f"wmod{i}", [P, 6 * D]) for i in range(2)]
        self.sc = sb("sc", [P, 2, B])
        self.scB = sb("scb", [P, B, P])
        self.H2 = sb("h2", [P, NT, D])
        self.LG = sb("lg", [P, NT, E0])
        self.l0_route_buffers()
        self.phase()
        self.W0 = sb("w0", [P, 4 * D])
        self.WoT = sb("wo0", [P, D])
        x = lambda b: io["x"][b].rearrange("(c p) d -> p c d", p=P)
        X = lambda b: self.X[:, b * TB:(b + 1) * TB, :]
        early = sum(w for _, w in ROWS[:EARLY_ROWS])
        row = lambda a, b: io["rows"][:, a:b].to_broadcast([P, b - a])
        self.load("cols", self.cols[:], io["cols"], self.act)
        self.load("rows", self.rowsb[:, 0:early], row(0, early))
        self.load("consts", self.consts[:], io["consts"])
        self.load("wmod0", self.wmod[0][:], io["wmod0"], self.act)
        self.load("x0", X(0), x(0))
        self.load("w0", self.W0[:], io["w0"], self.act)
        self.loaded(self.sp, "wmod0", "x0")
        self.load("x1", X(1), x(1))
        self.load("x2", X(2), x(2))
        self.load("wo0", self.WoT[:], io["wo0"])
        self.load("x3", X(3), x(3))
        self.load("wmod1", self.wmod[1][:], io["wmod1"])
        self.load("rows1", self.rowsb[:, early:], row(early, io["rows"].shape[1]))
        at = 0
        self.c = {}
        for name, w in CONSTS:
            self.c[name] = self.consts[:, at:at + w]
            at += w
        at = 0
        for name, w in COLS:
            self.c[name] = self.cols[:, at:at + w]
            at += w
        at = 0
        for name, w in ROWS:
            self.c[name] = self.rowsb[:, at:at + w]
            at += w
        self.zero = sb("zero", [P, 10 * D])
        self.GP("zero", self.pool.memset(self.zero[:], 0.0))
        self.disp = nc.dram_tensor("disp", [NSLOT, D], F32).ap()
        self.eout = nc.dram_tensor("eout", [NSLOT + 1, D], F32).ap()
        need(self.sp, "zero")
        sem = self.ctx.enter_context(nc.semaphore("dma_zeroed"))
        self.dma_sems["zeroed"] = sem
        self.dma_total["zeroed"] = 5 * 16
        part = NSLOT // 4
        for i in range(4):
            self.sp.dma_start(self.disp[i * part:(i + 1) * part, :].rearrange("(p a) d -> p (a d)", p=P),
                              self.zero[:]).then_inc(sem, 16)
        self.sp.dma_start(self.eout[NSLOT:NSLOT + 1, :], self.zero[0:1, 0:D]).then_inc(sem, 16)

        self.loaded(self.act, "cols")
        S("sc", self.act.activation(self.sc[:], self.c["cT"].rearrange("p (l b) -> p l b", l=2), ACT.Silu))

    def modulations(self, lay):
        v, s, pe, act = self.dve, self.s, self.pe, self.act
        need, V, S, M = s.need, self.V, self.S, self.M
        w, mT, mB = self.wmod[lay], self.mT[lay], self.mB[lay]
        need(v, "sc", "mod.mm")
        V("mod.scB", v.tensor_copy(self.scB[:], self.sc[:, lay, :].unsqueeze(2).to_broadcast([P, B, P])))
        yield DVE, 0.4
        self.loaded(pe, f"wmod{lay}")
        need(pe, "sc", "mod.evT", "l0.kv1")
        for j in range(6):
            ins = pe.matmul(self.bank[0][:, j * B:(j + 1) * B], w[:, j * D:(j + 1) * D], self.sc[:, lay, :],
                            start=True, stop=True)
        M("mod.T", ins)
        need(act, "mod.T")
        S("mod.evT", act.copy(mT[:], self.bank[0][:, 0:6 * B].rearrange("p (j b) -> p j b", j=6)))
        yield TPE, 1.3
        need(pe, "mod.scB")
        for b in range(B):
            first, second = self.bank[1 + 2 * (b % 2)], self.bank[(2, 0)[b % 2]]
            need(pe, f"mod.evB{b % 2}", "mod.evT", "l0.q", "l0.u", "l0.kv0")
            pe.matmul(first, self.scB[:, b, :], w[:, 0:512], start=True, stop=True)
            M("mod.mm", pe.matmul(second[:, 0:256], self.scB[:, b, :], w[:, 512:768], start=True, stop=True))
            need(act, "mod.mm")
            act.copy(mB[:, b, 0:4, :].rearrange("p j d -> p (j d)"), first)
            S(f"mod.evB{b % 2}", act.copy(mB[:, b, 4:6, :].rearrange("p j d -> p (j d)"), second[:, 0:256]))
            yield TPE, 1.1
        need(v, "mod.evT", "mod.evB0", "mod.evB1")
        for j in (1, 4):
            v.tensor_scalar(mT[:, j, :], mT[:, j, :], 1.0, None, ALU.add)
        V("mod.one", v.tensor_scalar(mB[:, :, 4, :], mB[:, :, 4, :], 1.0, None, ALU.add))
        for j in (2, 5):
            g = mB[:, :, j, :]
            t = self.scr(f"gate{j}", [P, B, D])
            V("mod.sg", v.tensor_scalar(t[:], g, 0.0, 2.0, ALU.is_ge, ALU.mult))
            V("mod.ab", v.scalar_tensor_tensor(g, g, -1.0, g, ALU.mult, ALU.max))
            need(v, "mod.ab")
            V("mod.sg", v.tensor_scalar(t[:], t[:], -1.0, None, ALU.add))
            need(v, "mod.sg")
            V("mod.g", v.scalar_tensor_tensor(g, g, 0.25, t[:], ALU.max, ALU.mult))
            yield DVE, 2.3
        s.mark(f"mod{lay}", s.dve)

    def scr(self, name, shape):
        if name not in self.scratch:
            self.scratch[name] = self.sb(name, shape)
        return self.scratch[name]

    def rotation(self):
        v, s, pe, act = self.dve, self.s, self.pe, self.act
        need, V, S, M = s.need, self.V, self.S, self.M
        th = self.sb("th", [P, TB, D])
        cnt = self.sb("cnt", [P, TB, D])
        self.tokT = [self.sb(f"tokt{k}", [P, TB, D]) for k in range(2)]
        self.dimT = [self.sb(f"dimt{k}", [P, T]) for k in range(2)]
        self.loaded(v, "rows")
        self.loaded(v, "consts")
        for c in range(TB):
            ins = v.tensor_scalar(th[:, c, :], self.c["theta"], self.c["pos"][:, c:c + 1], None, ALU.mult)
        V("rot", ins)
        yield DVE, 1.6
        r = self.tokT[1]

        def step(out, make):
            need(v, "rot")
            V("rot", make(out))

        def turns(src):
            step(cnt, lambda o: v.tensor_scalar(o[:], src[:], 1.0 / TWO_PI, ROUND, ALU.mult, ALU.add))
            step(cnt, lambda o: v.tensor_scalar(o[:], cnt[:], ROUND, None, ALU.subtract))

        turns(th)
        yield DVE, 1.3
        src = th
        for part in (C1, C2, C3):
            step(r, lambda o, part=part, src=src: v.scalar_tensor_tensor(o[:], cnt[:], -part, src[:],
                                                                         ALU.mult, ALU.add))
            yield DVE, 1.1
            src = r
        turns(r)
        yield DVE, 1.3
        step(r, lambda o: v.scalar_tensor_tensor(o[:], cnt[:], -TWO_PI, r[:], ALU.mult, ALU.add))
        yield DVE, 1.1
        step(r, lambda o: v.tensor_scalar(o[:], r[:], -PI32, PI32, ALU.max, ALU.min))
        yield DVE, 0.6
        step(self.tokT[0], lambda o: v.scalar_tensor_tensor(o[:], r[:], -1.0, r[:], ALU.mult, ALU.max))
        yield DVE, 1.1
        need(act, "rot")
        S("tok0", act.activation(self.tokT[0][:], self.tokT[0][:], ACT.Sin, scale=-1.0, bias=self.c["quarter"]))
        S("tok1", act.activation(r[:], r[:], ACT.Sin))
        yield ACTE, 4.5
        for k in range(2):
            for half in range(2):
                bk = self.bank[5 + half]
                if k == half == 0:
                    self.loaded(pe, "consts")
                need(pe, f"tok{k}", f"rot.ev{half}")
                for i in range(4):
                    ins = pe.transpose(bk[:, i * P:(i + 1) * P], self.tokT[k][:, 4 * half + i, :], self.c["ident"])
                M("rot.tr", ins)
                need(act, "rot.tr")
                S(f"rot.ev{half}", act.copy(self.dimT[k][:, half * 512:(half + 1) * 512], bk))
            yield TPE, 1.5
        s.mark("rotation", s.act)

    def l0_buffers(self):
        sb = self.sb
        self.qT = sb("q_t", [P, NT * P])
        self.uT = sb("u_t", [P, NT * P])
        self.xn = sb("xn", [P, G4, D])
        self.hT = sb("h_t", [P, G4 * P])
        self.kv = sb("kv", [P, G4, 2 * D])
        self.ks = sb("ks", [P, G4, D])
        self.kr = [sb(f"kr{k}", [P, G4, D]) for k in range(2)]
        self.KVa = sb("kva", [P, 2, D])
        self.KVm = sb("kvm", [P, 2, D])
        self.qr = [sb(f"qr{k}", [P, G4 * P]) for k in range(2)]
        self.on = sb("on", [P, G4, D])
        self.oT = sb("o_t", [P, G4 * P])
        self.hm = sb("hm", [P, G4, D])
        self.h2T = sb("h2_t", [P, G4 * P])
        self.wog = sb("wog", [P, D])
        self.gbo = sb("gbo", [P, D])
        self.stA = self.stat_buffers("sa", NT)
        self.stB, self.stC = (self.stat_buffers(f"s{x}", G4) for x in "bc")
        self.Wg = sb("wg0", [P, E0])
        self.load("wg0", self.Wg[:], self.io["wg0"])

    def l0_stats(self, b):
        tiles = [self.X[:, b * TB + i, :] for i in range(TB)]
        at = slice(b * TB, (b + 1) * TB)
        self.loaded(self.dve, f"x{b}")
        yield from self.stats("ln1", tiles, [a[:, at] for a in self.stA])
        self.s.mark(f"ln1.{b}", self.s.dve)

    def l0_normed(self, b, half):
        n0 = b * TB + half * G4
        _, _, y, _, _, nm = self.stA
        self.s.need_apart(self.act, f"ln1.{b}", "l0.xT")
        for i in range(G4):
            ins = self.act.activation(self.xn[:, i, :], self.X[:, n0 + i, :], ACT.Identity,
                                      scale=y[:, bass.ds(n0 + i, 1)], bias=nm[:, bass.ds(n0 + i, 1)])
        self.S("l0.xn", ins)

    def after(self, *names):
        while not all(n in self.s.marks for n in names):
            yield f"waits for {names}", 0.5

    def l0_keys(self, b, half, first=False):
        v, s, pe, act, bank = self.dve, self.s, self.pe, self.act, self.bank
        need, V, S, M = s.need, self.V, self.S, self.M
        n0 = b * TB + half * G4
        sl = tokens(n0, G4)
        if first:
            yield from self.after("ln1.0", "mod0")
            self.loaded(pe, "w0")
            need(pe, "mod0")
            need(act, "mod0")
        self.l0_normed(b, half)
        yield ACTE, 1.6
        need(pe, "l0.xn", "l0.kv1")
        for i in range(G4):
            ins = pe.transpose(bank[0][:, i * P:(i + 1) * P], self.xn[:, i, :], self.c["ident"])
        M("l0.xT", ins)
        yield TPE, 0.45
        s.need_apart(act, "l0.xT", "l0.kvmm")
        S("l0.hT", act.activation(self.hT[:], bank[0], ACT.Identity, scale=at1(self.mT[0][:, 1, :], b),
                                  bias=at1(self.mT[0][:, 0, :], b)))
        yield ACTE, 0.7
        for j, bk in ((0, bank[3]), (1, bank[0])):
            need(pe, "l0.hT", f"l0.kv{j}")
            for i in range(2):
                t = 2 * j + i
                ins = pe.matmul(bk[:, i * 256:(i + 1) * 256], self.hT[:, t * P:(t + 1) * P],
                                self.W0[:, D:3 * D], start=True, stop=True)
            M("l0.kvmm", ins)
            yield TPE, 0.9
            need(v, "l0.kvmm", "l0.state", "l0.kr")
            V(f"l0.kv{j}", v.tensor_tensor(self.kv[:, 2 * j:2 * j + 2, :], bk.rearrange("p (a b) -> p a b", a=2),
                                           rows(self.c["bkv"], 2), ALU.add))
            yield DVE, 0.6
        need(pe, "l0.hT", "l0.q")
        M("l0.qmm", pe.matmul(bank[1], self.W0[:, 0:D], self.hT[:], start=True, stop=True))
        need(pe, "l0.u")
        M("l0.umm", pe.matmul(bank[2], self.W0[:, 3 * D:4 * D], self.hT[:], start=True, stop=True))
        s.mark("l0.kvmm", s.pe)
        yield TPE, 1.7
        if first:
            yield from self.after("rotation")
            need(pe, "rotation")
        need(act, "l0.kv1", "l0.state")
        S("l0.ks", act.activation(self.ks[:], self.kv[:, :, 0:D], ACT.Silu))
        yield ACTE, 0.6
        for k in range(2):
            need(v, "l0.ks", "l0.state", "tok0", "tok1")
            V("l0.kr", v.tensor_tensor(self.kr[k][:], self.ks[:], self.tokT[k][:, 4 * half:4 * half + 4, :],
                                       ALU.mult))
            yield DVE, 0.6
        s.need_apart(act, "l0.qmm")
        S("l0.q", act.activation(self.qT[:, sl], bank[1], ACT.Silu, bias=self.c["bq"]))
        yield ACTE, 0.6
        s.need_apart(act, "l0.umm")
        S("l0.u", act.activation(self.uT[:, sl], bank[2], ACT.Identity, bias=self.c["bu"]))
        yield ACTE, 0.6
        need(pe, "l0.kr", "l0.kva", "r0.cp")
        for k in range(2):
            for i in range(G4):
                ins = pe.matmul(bank[5][:, k * D:(k + 1) * D], self.kr[k][:, i, :], self.kv[:, i, D:2 * D],
                                start=(i == 0), stop=(i == G4 - 1))
        M("l0.state", ins)
        yield TPE, 1.7
        need(v, "l0.state", "l0.kvm", "r0.cum")
        both = bank[5][:, 0:2 * D].rearrange("p (k d) -> p k d", k=2)
        if half == 0:
            V("l0.kva", v.tensor_copy(self.KVa[:], both))
        else:
            V("l0.kva", v.tensor_tensor(self.KVa[:], self.KVa[:], both, ALU.add))

    def l0_close_state(self):
        need, v = self.s.need, self.dve
        need(v, "l0.kva", "l0.omm")
        self.V("l0.kvm", v.tensor_tensor(self.KVm[:], self.KVa[:], rows(self.c["headmask"], 2), ALU.mult))

    def l0_out_weights(self, b):
        need, v = self.s.need, self.dve
        g = self.mB[0][:, b, 2, :]
        need(v, "l0.ymm", "l0.x")
        v.tensor_tensor(self.wog[:], self.WoT[:], g, ALU.mult)
        self.V("l0.wog", v.tensor_tensor(self.gbo[:], self.c["bout"], g, ALU.mult))

    def l0_queries(self, b, half):
        v, s, pe, act, bank = self.dve, self.s, self.pe, self.act, self.bank
        need, V, S, M = s.need, self.V, self.S, self.M
        n0 = b * TB + half * G4
        sl = tokens(n0, G4)
        for k in range(2):
            need(v, "l0.q.before", "l0.omm")
            V("l0.qr", v.tensor_tensor(self.qr[k][:], self.qT[:, sl], self.dimT[k][:, half * 512:half * 512 + 512],
                                       ALU.mult))
            yield DVE, 0.6
        need(pe, "l0.qr", "l0.kvm", "l0.on")
        for i in range(G4):
            for k in range(2):
                ins = pe.matmul(bank[6][:, i * P:(i + 1) * P], self.qr[k][:, i * P:(i + 1) * P], self.KVm[:, k, :],
                                start=(k == 0), stop=(k == 1))
        M("l0.omm", ins)
        yield TPE, 1.7
        need(v, "l0.omm")
        outs = [bank[6][:, i * P:(i + 1) * P] for i in range(G4)]
        yield from self.stats("ln2", outs, self.stB)
        self.normed("l0.on", "ln2", [self.on[:, i, :] for i in range(G4)], outs, self.stB, "l0.onT")

    def l0_output(self, b, half):
        v, s, pe, act, bank = self.dve, self.s, self.pe, self.act, self.bank
        need, V, S, M = s.need, self.V, self.S, self.M
        n0 = b * TB + half * G4
        sl = tokens(n0, G4)
        need(pe, "l0.on.before", "l0.xa")
        for i in range(G4):
            ins = pe.transpose(bank[7][:, i * P:(i + 1) * P], self.on[:, i, :], self.c["ident"])
        M("l0.onT", ins)
        yield TPE, 0.45
        need(act, "l0.onT", "l0.ymm")
        S("l0.oT", act.activation(self.oT[:], bank[7], ACT.Identity, scale=self.c["lnw"], bias=self.c["lnb"]))
        yield ACTE, 0.6
        need(v, "l0.oT", "l0.u.before")
        V("l0.ou", v.tensor_tensor(self.oT[:], self.oT[:], self.uT[:, sl], ALU.mult))
        yield DVE, 0.6
        need(pe, "l0.ou", "l0.wog", "l0.oT")
        for i in range(G4):
            ins = pe.matmul(bank[7][:, i * P:(i + 1) * P], self.oT[:, i * P:(i + 1) * P], self.wog[:],
                            start=True, stop=True)
        M("l0.ymm", ins)
        yield TPE, 0.9
        xs = self.X[:, bass.ds(n0, G4), :]
        need(v, "l0.ymm")
        V("l0.xa", v.tensor_tensor(xs, bank[7].rearrange("p (a b) -> p a b", a=G4), xs, ALU.add))
        yield DVE, 0.6
        need(v, "l0.xa", "l0.wog")
        V("l0.x", v.tensor_tensor(xs, xs, rows(self.gbo[:], G4), ALU.add))

    def l0_moe_input(self, b, half):
        v, s, pe, act, bank = self.dve, self.s, self.pe, self.act, self.bank
        need, V, S, M = s.need, self.V, self.S, self.M
        n0 = b * TB + half * G4
        tiles = [self.X[:, n0 + i, :] for i in range(G4)]
        s.need_apart(v, "l0.x.before")
        yield from self.stats("ln3", tiles, self.stC)
        self.normed("l0.hn", "ln3", [self.hm[:, i, :] for i in range(G4)], tiles, self.stC, "l0.H2", "l0.h2mm")
        yield ACTE, 1.6
        need(v, "l0.hn")
        V("l0.hc", v.tensor_tensor(self.hm[:], self.hm[:], rows(self.mB[0][:, b, 4, :], G4), ALU.mult))
        yield DVE, 0.6
        need(v, "l0.hc")
        V("l0.h2", v.tensor_tensor(self.hm[:], self.hm[:], rows(self.mB[0][:, b, 3, :], G4), ALU.add))
        yield DVE, 0.6
        need(pe, "l0.h2", "l0.lg")
        for i in range(G4):
            ins = pe.transpose(bank[4][:, i * P:(i + 1) * P], self.hm[:, i, :], self.c["ident"])
        M("l0.h2mm", ins)
        yield TPE, 0.45
        need(act, "l0.h2mm", "l0.lgmm")
        S("l0.h2T", act.copy(self.h2T[:], bank[4]))
        S("l0.H2", act.copy(self.H2[:, bass.ds(n0, G4), :], self.hm[:]))
        yield ACTE, 1.2
        need(pe, "l0.h2T")
        for i in range(G4):
            ins = pe.matmul(bank[4][:, i * E0:(i + 1) * E0], self.h2T[:, i * P:(i + 1) * P], self.Wg[:],
                            start=True, stop=True)
        M("l0.lgmm", ins)
        yield TPE, 0.9
        need(v, "l0.lgmm")
        V("l0.lg", v.tensor_tensor(self.LG[:, bass.ds(n0, G4), :],
                                   bank[4][:, 0:G4 * E0].rearrange("p (a b) -> p a b", a=G4),
                                   rows(self.c["bg"], G4), ALU.add))

    def together(self, *streams):
        streams = [x for x in streams if x is not None]
        for name in ("q", "u", "x", "on", "lg"):
            self.s.alias(f"l0.{name}.before", f"l0.{name}")
        ready, free = {x: 0.0 for x in streams}, {}
        while ready:
            x = min(ready, key=ready.get)
            issued = next(x, None)
            if issued is None:
                del ready[x]
            else:
                engine, took = issued
                if engine == TPE:
                    took *= 2
                free[engine] = max(ready[x], free.get(engine, 0.0)) + took
                ready[x] = free[engine] + 0.1

    def layer0_attention(self):
        s = self.s
        self.l0_buffers()

        def body(b, first=False, last=False):
            if not first:
                before = [self.l0_output(b - 1, 1), self.l0_moe_input(b - 1, 0)]
            self.together(self.l0_queries(b, 0), *([] if first else before),
                          None if last else self.l0_keys(b + 1, 0),
                          self.l0_route(b - 2) if not isinstance(b, int) or b > 1 else None,
                          self.l0_stats(2) if first else None)
            self.l0_out_weights(b)
            self.together(self.l0_queries(b, 1), self.l0_output(b, 0), self.l0_stats(3) if first else None,
                          None if first else self.l0_moe_input(b - 1, 1),
                          None if last else self.l0_keys(b + 1, 1))
            if not last:
                self.l0_close_state()

        self.together(self.modulations(0), self.rotation(), self.l0_stats(0), self.l0_keys(0, 0, first=True))
        self.together(self.l0_keys(0, 1), self.l0_stats(1))
        self.loaded(self.pe, "wg0")
        self.loaded(self.dve, "wo0")
        self.l0_close_state()
        for b in range(B):
            body(b, first=b == 0, last=b == B - 1)
            if b > 1:
                self.l0_dispatch(b - 2)
        self.together(self.l0_output(B - 1, 1), self.l0_moe_input(B - 1, 0), self.l0_route(B - 2))
        self.l0_dispatch(B - 2)
        self.together(self.l0_moe_input(B - 1, 1))
        self.together(self.l0_route(B - 1), self.modulations(1))
        self.l0_dispatch(B - 1)
        self.end_phase()

    def top2(self, tag, lg, oh, n, e, iota, top):
        v, need, V = self.dve, self.s.need, self.V
        wk = self.scr(f"{tag}_wk", [P, n, e])
        rest = self.scr(f"{tag}_rest", [P, n, e])
        idx = self.scr(f"{tag}_idx", [P, n])
        src = lg
        took = (DVE, 0.1 + n * e / 960)
        for k in range(2):
            V(f"{tag}.a", v.tensor_reduce(top[k], src, AX.X, ALU.max))
            yield took
            need(v, f"{tag}.a")
            V(f"{tag}.a", v.tensor_tensor(wk[:], src, top[k].unsqueeze(2).to_broadcast([P, n, e]), ALU.is_equal))
            yield took
            need(v, f"{tag}.a")
            V(f"{tag}.a", v.scalar_tensor_tensor(wk[:], wk[:], -64.0, rows(iota, n), ALU.mult, ALU.add))
            yield took
            need(v, f"{tag}.a")
            V(f"{tag}.a", v.tensor_reduce(idx[:], wk[:], AX.X, ALU.min))
            yield took
            need(v, f"{tag}.a")
            V(f"{tag}.a", v.tensor_scalar(idx[:], idx[:], 64.0, None, ALU.add))
            yield DVE, 0.1
            need(v, f"{tag}.a")
            V(f"{tag}.a", v.tensor_tensor(oh[k], rows(iota, n), idx[:].unsqueeze(2).to_broadcast([P, n, e]),
                                          ALU.is_equal))
            yield took
            need(v, f"{tag}.a")
            if k == 0:
                V(f"{tag}.a", v.scalar_tensor_tensor(rest[:], oh[0], -3.0e38, lg, ALU.mult, ALU.add))
                yield took
                need(v, f"{tag}.a")
                src = rest[:]

    def l0_route_buffers(self):
        sb = self.sb
        self.top = [sb(f"top{k}", [P, NT]) for k in range(2)]
        self.oh = [sb(f"oh{k}", [P, TB, E0]) for k in range(2)]
        self.label, self.seq, self.pre, self.rwk = (sb(f"rt_{x}", [P, TB, E0]) for x in ("label", "seq", "pre", "wk"))
        self.cum = sb("rt_cum", [P, 2, TB, E0])
        self.queued = sb("rt_queued", [P, E0])
        self.sf, self.sv = sb("rt_sf", [P, TB]), sb("rt_sv", [P, TB])
        self.V("r0.queued", self.dve.memset(self.queued[:], 0.0))

    def l0_route(self, b):
        v, s, pe, bank = self.dve, self.s, self.pe, self.bank
        need, V, M = s.need, self.V, self.M
        bt = slice(b * TB, (b + 1) * TB)
        oh, label, seq, wk, sf, sv, cum = self.oh, self.label, self.seq, self.rwk, self.sf, self.sv, self.cum
        small = (DVE, 0.15)
        need(v, "l0.lg.before")
        yield from self.top2("t0", self.LG[:, bt, :], [o[:] for o in oh], TB, E0, self.c["iota8"],
                             [t[:, bt] for t in self.top])
        V("r0.label", v.tensor_tensor(label[:], oh[0][:], oh[1][:], ALU.add))
        yield small
        need(pe, "r0.label", "l0.kva")
        flat = label[:].rearrange("p n e -> p (n e)")
        at, w = 2 * D, TB * E0
        pe.matmul(bank[5][:, at:at + w], self.c["upto"], flat, start=True, stop=True)
        M("r0.cum", pe.matmul(bank[5][:, at + w:at + 2 * w], self.c["ones"], flat, start=True, stop=True))
        need(v, "r0.cum")
        V("r0.cp", v.tensor_copy(cum[:].rearrange("p k n e -> p (k n e)"), bank[5][:, at:at + 2 * w]))
        yield DVE, 0.8
        need(v, "r0.cp")
        tot = cum[:, 1, :, :]
        a, to = tot, [self.pre[:], wk[:]]
        step = 1
        while step < TB:
            o = to[0]
            V("r0.a", v.tensor_copy(o[:, 0:step, :], a[:, 0:step, :]))
            V("r0.a", v.tensor_tensor(o[:, step:, :], a[:, step:, :], a[:, 0:TB - step, :], ALU.add))
            yield small
            need(v, "r0.a")
            a, to = o, to[::-1]
            step *= 2
        V("r0.a", v.tensor_tensor(seq[:], a, tot, ALU.subtract))
        yield small
        need(v, "r0.a")
        V("r0.a", v.tensor_tensor(seq[:], seq[:], cum[:, 0, :, :], ALU.add))
        yield small
        need(v, "r0.a", "r0.queued")
        V("r0.seq", v.tensor_tensor(seq[:], seq[:], rows(self.queued[:], TB), ALU.add))
        yield small
        need(v, "r0.seq")
        V("r0.queued", v.tensor_tensor(self.queued[:], self.queued[:], a[:, TB - 1, :], ALU.add))
        yield small
        need(v, "r0.seq", "r0.queued")
        for k in range(2):
            V("r0.a", v.tensor_tensor(wk[:], seq[:], oh[k][:], ALU.mult))
            V("r0.b", v.tensor_tensor(self.pre[:], rows(self.c["iota8"], TB), oh[k][:], ALU.mult))
            yield small
            need(v, "r0.a", "r0.b")
            V("r0.a", v.tensor_reduce(sv[:], wk[:], AX.X, ALU.add))
            V("r0.b", v.tensor_reduce(sf[:], self.pre[:], AX.X, ALU.add))
            yield small
            need(v, "r0.a", "r0.b")
            V("r0.a", v.tensor_scalar(sf[:], sf[:], float(CAP), -1.0, ALU.mult, ALU.add))
            yield small
            need(v, "r0.a")
            V("r0.a", v.tensor_tensor(sf[:], sf[:], sv[:], ALU.add))
            yield small
            V("r0.b", v.tensor_scalar(sv[:], sv[:], float(CAP), None, ALU.is_le))
            yield small
            need(v, "r0.a", "r0.b")
            V("r0.a", v.scalar_tensor_tensor(sf[:], sf[:], -float(NSLOT), sv[:], ALU.add, ALU.mult))
            yield small
            need(v, "r0.a")
            V("r0.a", v.tensor_scalar(sf[:], sf[:], float(NSLOT), None, ALU.add))
            yield small
            need(v, "r0.a")
            V(f"r0.slot{k}", v.tensor_copy(self.slot[k][:, bt], sf[:]))
            yield small

    def l0_dispatch(self, b):
        g = self.pool
        self.s.need(g, "r0.slot0", "r0.slot1", "l0.H2")
        if b == 0:
            self.loaded(g, "zeroed")
            self.dma_sems["dispatched"] = self.ctx.enter_context(self.nc.semaphore("dma_dispatched"))
            self.dma_total["dispatched"] = 2 * NT * 16
        for n in range(b * TB, (b + 1) * TB):
            for k in range(2):
                g.indirect_dma_start(out=self.disp, out_offset=bass.IndirectOffsetOnAxis(
                    ap=self.slot[k][:, n:n + 1], axis=0), in_=self.H2[:, n, :], in_offset=None,
                    bounds_check=NSLOT - 1, oob_is_err=False).then_inc(self.dma_sems["dispatched"], 16)

    def l0_weights(self):
        v, s, act = self.dve, self.s, self.act
        need, V, S = s.need, self.V, self.S
        V("r0.d", v.tensor_tensor(self.w0[1][:], self.top[1][:], self.top[0][:], ALU.subtract))
        need(act, "r0.d")
        S("r0.e", act.activation(self.w0[1][:], self.w0[1][:], ACT.Exp))
        need(v, "r0.e")
        V("r0.w", v.tensor_scalar(self.w0[0][:], self.w0[1][:], 1.0, None, ALU.add))
        need(v, "r0.w")
        V("r0.w", v.reciprocal(self.w0[0][:], self.w0[0][:]))
        need(v, "r0.w")
        V("r0.w", v.tensor_tensor(self.w0[1][:], self.w0[1][:], self.w0[0][:], ALU.mult))

    def split_layer1_weights(self):
        v, act, s = self.dve, self.act, self.s
        for name, parts, n in (("wkv1", self.Wkv, NG), ("wgu", self.Wgus, 2)):
            raw = self.sb(f"raw_{name}", list(parts[0].shape))
            self.load(name, raw[:], self.io[name])
            self.loaded(act, name)
            for i in range(n):
                self.S("wh", act.copy(parts[0][:, i, :], raw[:, i, :]))
                s.need(v, "wh")
                self.V("ws", v.tensor_tensor(parts[1][:, i, :], raw[:, i, :], parts[0][:, i, :].bitcast(F32),
                                             ALU.subtract))

    def l0_experts(self):
        nc, v, s, pe, act, bank, sp = self.nc, self.dve, self.s, self.pe, self.act, self.bank, self.sp
        need, V, S, M, sb, io = s.need, self.V, self.S, self.M, self.sb, self.io
        self.phase()
        w12 = sb("e_w12", [P, 2, 2, H0])
        w3 = sb("e_w3", [P, 2, H0 // P, D])
        NB = H0 // P
        xe = sb("e_x", [P, 2, ST, D])
        xT = sb("e_xt", [P, 2, 2, CAP], F32R)
        ws = sb("e_ws", [P, 2, 2, 2, H0], F32R)
        hs = sb("e_hs", [P, NB, CAP])
        sg = sb("e_sg", [P, CAP])
        y = sb("e_y", [P, ST, D])
        sem = lambda n: self.ctx.enter_context(nc.semaphore(n))
        s_w = [sem(f"dma_expert_w{i}") for i in range(2)]
        s_w3 = [sem(f"dma_expert_w3_{i}") for i in range(2)]
        s_x = [sem(f"dma_expert_x{i}") for i in range(2)]
        s_y = sem("dma_expert_y")
        HC = CAP // 2
        PAIRS = E0 // 2

        def load_weights(e, i):
            sp.dma_start(w12[:, i, 0, :], io["w1"][e]).then_inc(s_w[i], 16)
            sp.dma_start(w12[:, i, 1, :], io["w2"][e]).then_inc(s_w[i], 16)

        def load_w3(e, i):
            sp.dma_start(w3[:, i, :, :], io["w3"][e].rearrange("(m p) d -> p m d", p=P)).then_inc(s_w3[i], 16)

        def load_slots(e, i):
            sp.dma_start(xe[:, i, :, :], self.disp[bass.ds(e * CAP, CAP), :].rearrange("(a p) d -> p a d", p=P)
                         ).then_inc(s_x[i], 16)

        def split_weights(m, use, i):
            cols = slice(m * P, (m + 1) * P)
            act.wait_ge(s_w[i], use * 32)
            need(act, f"e.mm{i}")
            S("e.wh", act.copy(ws[:, i, 0, :, cols], w12[:, i, :, cols]))
            need(v, "e.wh")
            V(f"e.ws{i}", v.tensor_tensor(ws[:, i, 1, :, cols], w12[:, i, :, cols],
                                          ws[:, i, 0, :, cols].bitcast(F32), ALU.subtract))

        def turn_slots(use, i):
            pe.wait_ge(s_x[i], use * 16)
            need(pe, "e.xT")
            for a in range(ST):
                bk, col = (6, a) if a < 4 else (7, 0)
                ins = pe.transpose(bank[bk][:, col * P:(col + 1) * P], xe[:, i, a, :], self.c["ident"])
            M("e.tr", ins)
            s.mark(f"e.tr{i}", s.pe)
            need(v, "e.tr", f"e.mm{i}")
            both = self.psum[:, 6:8, :].rearrange("p k x -> p (k x)")[:, 0:CAP]
            V("e.xh", v.tensor_copy(xT[:, i, 0, :], both))
            need(v, "e.xh")
            V("e.xT", v.tensor_tensor(xT[:, i, 1, :], both, xT[:, i, 0, :].bitcast(F32), ALU.subtract))
            s.mark(f"e.xT{i}", s.dve)

        def product(out, w, i, m, cols):
            for k, (wp, xp) in enumerate(((0, 0), (0, 1), (1, 0))):
                ins = pe.matmul(out, ws[:, i, wp, w, m * P:(m + 1) * P], xT[:, i, xp, cols],
                                start=(k == 0), stop=(k == 2))
            return ins

        for i in range(2):
            load_weights(i, i)
            load_w3(i, i)
        self.split_layer1_weights()
        self.loaded(sp, "dispatched")
        load_slots(0, 0)
        load_slots(1, 1)
        for m in range(NB):
            split_weights(m, 1, 0)
        turn_slots(1, 0)

        def body(pair, last=False):
            for i in range(2):
                e = 2 * pair + i
                more = not (last and i == 1)
                if not last:
                    need(sp, f"e.ws{i}", f"e.tr{i}")
                    load_weights(e + 2, i)
                    load_slots(e + 2, i)
                for m in range(NB):
                    for half in range(2):
                        need(pe, f"e.h{half}", f"e.xT{i}", f"e.ws{i}")
                        cols = slice(half * HC, (half + 1) * HC)
                        M("e.gate", product(bank[2 * half][:, 0:HC], 0, i, m, cols))
                        M(f"e.mm{i}", product(bank[2 * half + 1][:, 0:HC], 1, i, m, cols))
                        need(act, "e.gate", f"e.h{half}")
                        S(f"e.sg{half}", act.activation(sg[:, cols], bank[2 * half][:, 0:HC], ACT.Silu))
                        need(v, f"e.sg{half}", f"e.mm{i}", "e.down")
                        V(f"e.h{half}", v.tensor_tensor(hs[:, m, cols], bank[2 * half + 1][:, 0:HC], sg[:, cols],
                                                        ALU.mult))
                    if more:
                        split_weights(m, pair + 1 + i, 1 - i)
                if more:
                    turn_slots(pair + 1 + i, 1 - i)
                need(pe, "e.h0", "e.h1")
                pe.wait_ge(s_w3[i], (pair + 1) * 16)
                for a in range(ST):
                    bk, col = (4, a) if a < 4 else (5, 0)
                    need(pe, f"e.y{min(a, 4) // 4}")
                    for m in range(NB):
                        ins = pe.matmul(bank[bk][:, col * P:(col + 1) * P], hs[:, m, a * P:(a + 1) * P],
                                        w3[:, i, m, :], start=(m == 0), stop=(m == NB - 1))
                M("e.down", ins)
                need(act, "e.down")
                if not isinstance(e, int) or e > 0:
                    act.wait_ge(s_y, e * 16)
                S("e.y0", act.copy(y[:, 0:4, :], bank[4].rearrange("p (a d) -> p a d", d=D)))
                S("e.y1", act.copy(y[:, 4, :], bank[5][:, 0:P]))
                if not last:
                    need(sp, "e.down")
                    load_w3(e + 2, i)
                need(sp, "e.y1")
                sp.dma_start(self.eout[bass.ds(e * CAP, CAP), :].rearrange("(a p) d -> p a d", p=P),
                             y[:]).then_inc(s_y, 16)

        s.loop(0, PAIRS - 1, body)
        body(PAIRS - 1, last=True)
        self.dma_sems["experts"], self.dma_total["experts"] = s_y, E0 * 16
        s.mark("experts", s.act)
        for e in (self.sp, self.act, self.dve, self.pe, self.pool):
            e.wait_ge(s_y, E0 * 16)
        self.end_phase()

    def l1_attention_setup(self):
        sb, io, g = self.sb, self.io, self.pool
        self.phase()
        self.l1_moe_setup()
        self.phase()
        self.Wq = sb("a_wq", [P, HD])
        self.Wo = sb("a_wo", [P, HD // P, D])
        self.csQ = sb("a_csq", [P, 2, T])
        self.G = [sb(f"a_g{k}", [P, NT, D]) for k in range(2)]
        self.state = sb("a_state", [P, NG, 2, 2, 2 * (DH + 1)])
        self.load("wq1", self.Wq[:], io["wq1"], self.act)
        self.load("wo1", self.Wo[:], io["wo1"].rearrange("(m p) d -> p m d", p=P))
        self.load("csq", self.csQ[:].rearrange("p k t -> p (k t)"), io["csq"].to_broadcast([P, 2 * T]), self.act)
        ring = [self.ctx.enter_context(self.nc.semaphore(f"dma_gather{k}")) for k in range(4)]
        self.gathered = self.ctx.enter_context(self.nc.semaphore("gathered_tiles"))
        self.loaded(g, "experts")
        done = 0
        for n in range(NT):
            for k in range(2):
                g.indirect_dma_start(out=self.G[k][:, n, :], out_offset=None, in_=self.eout,
                                     in_offset=bass.IndirectOffsetOnAxis(ap=self.slot[k][:, n:n + 1], axis=0)
                                     ).then_inc(ring[n % len(ring)], 16)
            while done < (n if n < 3 else NT if n == NT - 1 else n + 2 - len(ring)):
                g.wait_ge(ring[done % len(ring)], 32 * (done // len(ring) + 1))
                g.sem_inc(self.gathered, 1)
                done += 1
        each = lambda name, shape, count=NG: [sb(f"a_{name}{i}", shape) for i in range(count)]
        self.Qp = each("qp", [P, 2, P])
        self.Qr = each("qr", [P, 2, 2, P])
        self.Kb = each("kb", [P, HG, DH])
        self.Kr = each("kr", [P, 2, HG, DH])
        self.Va = each("va", [P, HG, DH + 1])
        self.KT = each("kt", [P, 2, P])
        self.Sm = each("sm", [P, 2, 2, P], 2)
        self.den = sb("a_den", [P, HG])
        self.O = sb("a_o", [P, NH, DH])
        self.oT1 = sb("a_ot", [P, HD // P, P])
        self.hT1 = sb("a_ht", [P, P])
        self.hs1 = sb("a_hs", [P, 2, P], F32R)
        self.xn1 = sb("a_xn", [P, 2, D])
        self.h3 = sb("a_h3", [P, P])
        self.mt1 = sb("a_mt", [P, D])
        self.yt1 = sb("a_yt", [P, D])
        self.st1 = self.stat_buffers("s1", 2)
        v = self.dve
        for va in self.Va:
            v.memset(va[:], 1.0)
        self.V("a.init", v.memset(self.state[:], 0.0))

    def a_mix(self, n):
        v, s = self.dve, self.s
        need, V = s.need, self.V
        x, b = self.X[:, n, :], n // TB
        v.wait_ge(self.gathered, n + 1)
        V("a.m", v.tensor_scalar(self.mt1[:], self.G[0][:, n, :], self.w0[0][:, bass.ds(n, 1)], None, ALU.mult))
        yield
        need(v, "a.m")
        V("a.m", v.scalar_tensor_tensor(self.mt1[:], self.G[1][:, n, :], self.w0[1][:, bass.ds(n, 1)], self.mt1[:],
                                        ALU.mult, ALU.add))
        yield
        need(v, "a.m")
        V("a.m", v.tensor_tensor(self.mt1[:], self.mt1[:], self.mB[0][:, b, 5, :], ALU.mult))
        yield
        need(v, "a.m")
        V("a.m", v.tensor_tensor(x, x, self.mt1[:], ALU.add))
        s.mark("a.mixed", s.dve)

    def a_stats(self, tiles):
        v, s = self.dve, self.s
        need, V = s.need, self.V
        st, mv, y, h, t, _ = self.st1
        at = slice(min(tiles), max(tiles) + 1)
        s.need_apart(v, "a.mixed", "a.x")
        for i, n in tiles.items():
            ins = v.bn_stats(st[:, i, :], self.X[:, n, :])
        V("a.st", ins)
        yield
        s.need_apart(v, "a.st")
        for i in tiles:
            ins = v.bn_aggr(mv[:, i, :], st[:, i, :])
        V("a.mv", ins)
        yield
        need(v, "a.mv")
        V("a.v", v.tensor_scalar(t[:, at], mv[:, at, 1], EPS, None, ALU.add))
        V("a.hh", v.tensor_scalar(h[:, at], mv[:, at, 1], EPS, -0.5, ALU.add, ALU.mult))
        yield
        need(v, "a.v")
        V("a.y0", v.tensor_scalar(y[:, at].bitcast(I32), t[:, at].bitcast(I32), -0.5, 1597463007.0,
                                  ALU.mult, ALU.add))
        yield

    def a_norms(self, tiles):
        v, need, V = self.dve, self.s.need, self.V
        _, mv, y, h, t, _ = self.st1
        at = slice(min(tiles), max(tiles) + 1)
        for _ in range(3):
            need(v, "a.y0", "a.hh")
            V("a.t", v.tensor_tensor(t[:, at], y[:, at], y[:, at], ALU.mult))
            yield
            need(v, "a.t")
            V("a.t", v.tensor_tensor(t[:, at], t[:, at], h[:, at], ALU.mult))
            yield
            need(v, "a.t")
            V("a.y0", v.scalar_tensor_tensor(y[:, at], t[:, at], 1.5, y[:, at], ALU.add, ALU.mult))
            yield
        need(v, "a.y0", "a.xT")
        for i, n in tiles.items():
            ins = v.tensor_scalar(self.xn1[:, i, :], self.X[:, n, :], mv[:, i, 0:1], y[:, i:i + 1],
                                  ALU.subtract, ALU.mult)
        V("a.xn", ins)

    BANK7 = ("a.Yread", "a.oTc", "a.hT", "a.h3", "a.lg")

    def a_ready(self, tiles):
        pe, act, s = self.pe, self.act, self.s
        s.need(pe, "a.xn", *self.BANK7)
        for i in tiles:
            ins = pe.transpose(self.bank[7][:, i * P:(i + 1) * P], self.xn1[:, i, :], self.c["ident"])
        self.M("a.xT", ins)
        if 0 in tiles:
            b = tiles[0] // TB
            s.need_apart(act, "a.xT", "a.kvmm")
            for out in (self.hT1[:], self.hs1[:, 0, :]):
                ins = act.activation(out, self.bank[7][:, 0:P], ACT.Identity,
                                     scale=at1(self.mT[1][:, 1, :], b), bias=at1(self.mT[1][:, 0, :], b))
            self.S("a.hT", ins)
            s.need(self.dve, "a.hT")
            self.V("a.hl", self.dve.tensor_tensor(self.hs1[:, 1, :], self.hT1[:], self.hs1[:, 0, :].bitcast(F32),
                                                  ALU.subtract))
        if 1 in tiles:
            n = tiles[1]
            b = n // TB
            s.need_apart(act, "a.xT", "a.lgmm")
            for out in (self.h3[:], self.h3T[:, tokens(n, 1)]):
                ins = act.activation(out, self.bank[7][:, P:2 * P], ACT.Identity,
                                     scale=at1(self.mT[1][:, 4, :], b), bias=at1(self.mT[1][:, 3, :], b))
            self.S("a.h3", ins)

    def a_logits(self, n):
        pe, v, need = self.pe, self.dve, self.s.need
        need(pe, *self.BANK7)
        self.M("a.lgmm", pe.matmul(self.bank[7][:, 2 * P:2 * P + E1], self.h3[:], self.Wr[:], start=True, stop=True))
        need(v, "a.lgmm")
        self.V("a.lg", v.tensor_copy(self.lg1[:, n, :], self.bank[7][:, 2 * P:2 * P + E1]))

    def a_project(self, n, g):
        v, s, pe, act, bank = self.dve, self.s, self.pe, self.act, self.bank
        need, V, S, M = s.need, self.V, self.S, self.M
        w = HG * DH
        need(pe, "a.hT", "a.Qp", "a.KTc")
        for j in range(2):
            ins = pe.matmul(bank[0][:, j * P:(j + 1) * P], self.Wq[:, (2 * g + j) * P:(2 * g + j + 1) * P],
                            self.hT1[:], start=True, stop=True)
        M("a.qmm", ins)
        need(pe, "a.hl", "a.Va")
        high, low = (x[:, g, :] for x in self.Wkv)
        for k, (part, ws) in enumerate(((0, high), (1, high), (0, low))):
            ins = pe.matmul(bank[1], self.hs1[:, part, :], ws, start=(k == 0), stop=(k == 2))
        M("a.kvmm", ins)
        need(v, "a.kvmm", f"a.Kr{g}", f"a.KT{g}")
        V("a.Kb", v.tensor_tensor(self.Kb[g][:].rearrange("p h d -> p (h d)"), bank[1][:, 0:w],
                                  self.c["bk1"][:, g * w:(g + 1) * w], ALU.add))
        s.mark(f"a.Kb{g}", s.dve)
        need(v, f"a.U{g}", f"a.I{g}")
        V("a.Va", v.tensor_tensor(self.Va[g][:, :, 0:DH], bank[1][:, w:2 * w].rearrange("p (h d) -> p h d", d=DH),
                                  self.c["bv1"][:, g * w:(g + 1) * w].rearrange("p (h d) -> p h d", d=DH), ALU.add))
        s.mark(f"a.Va{g}", s.dve)
        need(act, "a.qmm", f"a.Qr{g}", f"a.S{g}")
        for j in range(2):
            ins = act.activation(self.Qp[g][:, j, :], bank[0][:, j * P:(j + 1) * P], ACT.Relu,
                                 bias=self.c["bq1"][:, 2 * g + j:2 * g + j + 1])
        S("a.Qp", ins)
        s.mark(f"a.Qp{g}", s.act)
        s.need_apart(act, "a.Kb", f"a.U{g}")
        for k in range(2):
            ins = act.activation(self.Kr[g][:, k, :, :], self.Kb[g][:], ACT.Relu,
                                 scale=self.c[("cos1", "sin1")[k]][:, bass.ds(n, 1)])
        S(f"a.Kr{g}", ins)

    def a_queries(self, n, g):
        v, need = self.dve, self.s.need
        c = n % TB
        need(v, f"a.Qp{g}", f"a.I{g}")
        self.V(f"a.Qr{g}", v.tensor_tensor(self.Qr[g][:], self.Qp[g][:].unsqueeze(1).to_broadcast([P, 2, 2, P]),
                                           self.csQ[:, :, tokens(c, 1)].unsqueeze(2).to_broadcast([P, 2, 2, P]),
                                           ALU.mult))

    def a_keys_turned(self, g):
        pe, act = self.pe, self.act
        need = self.s.need
        need(pe, f"a.Kb{g}", "a.Qp", "a.KTc")
        for j in range(2):
            ins = pe.transpose(self.bank[0][:, (2 + j) * P:(3 + j) * P],
                               self.Kb[g][:, 2 * j:2 * j + 2, :].rearrange("p h d -> p (h d)"), self.c["ident"])
        self.M(f"a.KT{g}", ins)
        need(act, f"a.KT{g}", f"a.S{g}")
        self.S("a.KTc", act.activation(self.KT[g][:].rearrange("p j t -> p (j t)"), self.bank[0][:, 2 * P:],
                                       ACT.Relu))
        self.s.mark(f"a.KTc{g}", self.s.act)

    def a_scores(self, g):
        v, s, pe, bank, i = self.dve, self.s, self.pe, self.bank, g % 2
        need = s.need
        need(pe, f"a.KTc{g}", f"a.Qp{g}", "a.Sm")
        for h in range(HG):
            j, half = h // 2, h % 2
            p = slice(half * DH, (half + 1) * DH)
            ins = pe.matmul(bank[2 + half][:, j * P:(j + 1) * P], self.KT[g][p, j, :], self.Qp[g][p, j, :],
                            start=True, stop=True)
        self.M(f"a.S{g}", ins)
        need(v, f"a.S{g}", f"a.I{(g - 2) % NG}")
        self.V("a.Sm", v.tensor_tensor(self.Sm[i][:], self.psum[:, 2:4, 0:2 * P].rearrange("p x (j t) -> p x j t", j=2),
                                       self.c["cosmask"].unsqueeze(1).unsqueeze(1).to_broadcast([P, 2, 2, P]),
                                       ALU.mult))
        s.mark(f"a.Sm{i}", s.dve)

    def a_update(self, g):
        pe, bank, need = self.pe, self.bank, self.s.need
        need(pe, f"a.Va{g}", f"a.Kr{g}", "a.state")
        w = 2 * (DH + 1)
        for k in range(2):
            for j in range(2):
                ins = pe.matmul(bank[5 + k][:, j * 256:j * 256 + w],
                                self.Kr[g][:, k, 2 * j:2 * j + 2, :].rearrange("p h d -> p (h d)"),
                                self.Va[g][:, 2 * j:2 * j + 2, :].rearrange("p h d -> p (h d)"),
                                start=True, stop=True)
        self.M(f"a.U{g}", ins)

    def a_values(self, n, g):
        v, s, pe, bank, i = self.dve, self.s, self.pe, self.bank, g % 2
        need, V, M = s.need, self.V, self.M
        need(pe, f"a.Sm{i}", f"a.Qr{g}", "a.On", "a.state", "a.init")
        w = 2 * (DH + 1)
        for j in range(2):
            pair = bank[4][:, j * w:(j + 1) * w]
            for k in range(2):
                pe.matmul(pair, self.Qr[g][:, k, j, :],
                          self.state[:, g, k, j, :],
                          start=(k == 0), stop=False)
            for h in (2 * j, 2 * j + 1):
                ins = pe.matmul(bank[4][:, h * 65:(h + 1) * 65], self.Sm[i][:, h % 2, j, :], self.Va[g][:, h, :],
                                start=False, stop=(h % 2 == 1))
        M(f"a.I{g}", ins)
        need(v, f"a.I{g}")
        o4 = bank[4][:, 0:HG * 65].rearrange("p (h d) -> p h d", d=65)
        V("a.den", v.tensor_scalar(self.den[:], o4[:, :, DH], 1e-6, None, ALU.max))
        for half in range(2):
            p = slice(half * DH, (half + 1) * DH)
            cols = slice(half * (DH + 1), (half + 1) * (DH + 1))
            st = self.state[p, g, :, :, cols].rearrange("p k j d -> p (k j) d")
            u = self.psum[p, 5:7, :].rearrange("p k (j x) -> p (k j) x", j=2)[:, :, cols]
            ins = v.scalar_tensor_tensor(st, st, self.c["keep"][p, bass.ds(n, 1)], u, ALU.mult, ALU.add)
            if half == 0:
                V("a.st0", ins)
                need(v, "a.den")
                V("a.den", v.reciprocal(self.den[:], self.den[:]))
        V("a.state", ins)
        need(v, "a.den", f"a.oT{g}")
        V("a.On", v.tensor_tensor(self.O[:, HG * g:HG * (g + 1), :], o4[:, :, 0:DH],
                                  self.den[:].unsqueeze(2).to_broadcast([P, HG, DH]), ALU.mult))
        s.mark(f"a.On{g}", s.dve)

    def a_turned(self, g):
        pe, act, need = self.pe, self.act, self.s.need
        need(pe, f"a.On{g}", *self.BANK7)
        for j in range(2):
            blk = 2 * g + j
            ins = pe.transpose(self.bank[7][:, j * P:(j + 1) * P],
                               self.O[:, 2 * blk:2 * blk + 2, :].rearrange("p h d -> p (h d)"), self.c["ident"])
        self.M(f"a.oT{g}", ins)
        need(act, f"a.oT{g}", "a.Y")
        self.S("a.oTc", act.copy(self.oT1[:, 2 * g:2 * g + 2, :],
                                 self.bank[7][:, 0:2 * P].rearrange("p (j t) -> p j t", j=2)))

    def a_output(self, n):
        v, s, pe, bank = self.dve, self.s, self.pe, self.bank
        need, V, M = s.need, self.V, self.M
        need(pe, *self.BANK7)
        for m in range(HD // P):
            ins = pe.matmul(bank[7][:, 0:D], self.oT1[:, m, :], self.Wo[:, m, :], start=(m == 0),
                            stop=(m == HD // P - 1))
        M("a.Y", ins)
        need(v, "a.Y")
        V("a.Yread", v.tensor_tensor(self.yt1[:], bank[7][:, 0:D], self.c["bo1"], ALU.add))
        need(v, "a.Yread")
        V("a.y", v.tensor_tensor(self.yt1[:], self.yt1[:], self.mB[1][:, n // TB, 2, :], ALU.mult))
        need(v, "a.y")
        x = self.X[:, n, :]
        V("a.x", v.tensor_tensor(x, x, self.yt1[:], ALU.add))

    def a_step(self, n, g, pre=None, first=0, last=NT * NG, norms=None):
        at = lambda d: (n + (g + d) // NG, (g + d) % NG)
        known = lambda d: first <= g + d < last

        def steps(count):
            for _ in range(count):
                next(pre, None) if pre else None

        if known(2):
            self.a_project(*at(2))
        steps(3)
        if known(0):
            self.a_scores(g)
        if known(1):
            self.a_keys_turned(at(1)[1])
            self.a_queries(*at(1))
        steps(5)
        if g == 1 and norms:
            steps(30)
            self.a_ready(norms)
        if known(-1):
            self.a_update(at(-1)[1])
        if g == 3 and norms and 1 in norms:
            self.a_logits(norms[1])
        if g == 2 and known(-3):
            self.a_output(n - 1)
        if known(-1):
            self.a_values(*at(-1))
        steps(3 if g < 2 else 30)
        if known(-2):
            self.a_turned(at(-2)[1])

    def l1_attention(self):
        s = self.s
        self.l1_attention_setup()
        self.loaded(self.pe, "wq1", "wo1")
        self.loaded(self.dve, "csq", "rows1")
        s.need(self.act, "mod1")

        def body(n, first=-2 * NG, last=3 * NG):
            norms = {}
            if last > NG:
                norms[0] = n + 1
            if first < -NG:
                norms[1] = n - 2
            chain = self.a_norms(norms) if norms else None
            mix, then = None, {}
            if last > 2 * NG:
                mix = self.a_mix(n + 2)
                then[0] = n + 2
            if first < 0:
                then[1] = n - 1
            stats = self.a_stats(then)
            for g in range(NG):
                self.a_step(n, g, (chain, chain, mix, stats)[g], first, last, norms)

        def run(stream):
            for _ in stream:
                pass

        run(self.a_mix(0))
        run(self.a_stats({0: 0}))
        run(self.a_norms({0: 0}))
        self.a_ready({0: 0})
        run(self.a_mix(1))
        run(self.a_stats({0: 1}))
        self.a_step(0, -2)
        self.a_step(0, -1)
        body(0, first=0)
        body(1, first=-NG)
        s.loop(2, NT - 2, body)
        body(NT - 2, last=2 * NG)
        body(NT - 1, last=NG)
        run(self.a_norms({1: NT - 2}))
        self.a_step(NT - 1, NG, first=0, last=NG)
        self.a_ready({1: NT - 2})
        self.a_step(NT - 1, NG + 1, first=0, last=NG)
        self.a_logits(NT - 2)
        self.a_output(NT - 1)
        run(self.a_stats({1: NT - 1}))
        run(self.a_norms({1: NT - 1}))
        self.a_ready({1: NT - 1})
        self.a_logits(NT - 1)
        self.end_phase()

    def l1_moe_setup(self):
        io, sb = self.io, self.sb
        self.Wd = sb("m_wd", [P, MB + 1, D])
        self.Wr = sb("m_wr", [P, E1])
        self.load("wr", self.Wr[:], io["wr"])
        self.load("wd", self.Wd[:], io["wd"].rearrange("(m p) d -> p m d", p=P))
        self.ex_in = sb("m_ex0", [2 * E1, MB * P])
        self.load("expand", self.ex_in[:], io["expand"])
        self.h3T = sb("m_h3t", [P, NT * P])
        self.lg1 = sb("m_lg", [P, NT, E1])

    def l1_moe(self):
        s, sb = self.s, self.sb
        self.ex = sb("m_ex", [2 * E1, MB * P], F32R)
        each = lambda name, shape, dt=F32: [sb(f"m_{name}{i}", shape, dt) for i in range(2)]
        self.sg3 = each("sg", [P, G4 * P])
        self.hs3 = each("hs", [P, 2, G4 * P], F32R)
        self.hd3 = each("hd", [P, MB + 1, G4 * P])
        self.comb = sb("m_comb", [P, NT, 2, E1], F32R)
        self.combT = sb("m_combt", [2 * E1, NT * P], F32R)
        self.yo = sb("m_yo", [P, G4, D])
        self.stored = self.ctx.enter_context(self.nc.semaphore("dma_stored"))
        self.m_split(0, 0)
        self.loaded(self.pe, "wd")
        groups = NT // G4

        def body(pair, last=False):
            for i in (1, 0):
                gi = 2 * pair + (1 if i else 2)
                if last and i == 0:
                    self.m_down(gi - 1, 1)
                else:
                    self.m_experts(gi, i, gi - 1, gi + 1 if not last else None)

        self.together(self.m_routing(), self.m_first_hidden())
        self.m_first_weighted()
        s.loop(0, groups // 2 - 1, body)
        body(groups // 2 - 1, last=True)
        self.sp.wait_ge(self.stored, groups * 16)
        self.end_phase()

    def m_routing(self):
        v, s, pe, act, bank = self.dve, self.s, self.pe, self.act, self.bank
        need, V, S, M, sb = s.need, self.V, self.S, self.M, self.sb
        oh = [sb(f"m_oh{k}", [P, NT, E1]) for k in range(2)]
        top = [sb(f"m_top{k}", [P, NT]) for k in range(2)]
        z, w1, w2 = (sb(f"m_{x}", [P, NT]) for x in ("z", "w1", "w2"))
        dl, cm = sb("m_dl", [P, NT, E1]), sb("m_cm", [P, NT, E1])
        self.loaded(v, "expand")
        V("m.ex", v.tensor_copy(self.ex[:], self.ex_in[:]))
        need(v, "a.lg")
        yield DVE, 0.4
        yield from self.top2("t1", self.lg1[:], [o[:] for o in oh], NT, E1, self.c["iota16"], [t[:] for t in top])
        V("m.dl", v.tensor_tensor(dl[:], self.lg1[:], top[0][:].unsqueeze(2).to_broadcast([P, NT, E1]), ALU.subtract))
        V("m.d2", v.tensor_tensor(w2[:], top[1][:], top[0][:], ALU.subtract))
        yield DVE, 0.7
        need(act, "m.d2")
        act.activation(dl[:], dl[:], ACT.Exp)
        S("m.exp", act.activation(w2[:], w2[:], ACT.Exp))
        yield ACTE, 2.0
        need(v, "m.exp")
        V("m.z", v.tensor_reduce(z[:], dl[:], AX.X, ALU.add))
        need(v, "m.z")
        yield DVE, 1.5
        V("m.z", v.scalar_tensor_tensor(z[:], z[:], 1e-9, w2[:], ALU.mult, ALU.add))
        need(v, "m.z")
        V("m.z", v.tensor_scalar(z[:], z[:], 1.0, None, ALU.add))
        need(v, "m.z")
        V("m.w1", v.reciprocal(w1[:], z[:]))
        need(v, "m.w1")
        V("m.w2", v.tensor_tensor(w2[:], w2[:], w1[:], ALU.mult))
        need(v, "m.w2")
        for k, w in enumerate((w1, w2)):
            V(f"m.oh{k}", v.tensor_tensor(oh[k][:], oh[k][:], w[:].unsqueeze(2).to_broadcast([P, NT, E1]), ALU.mult))
        yield DVE, 2.2
        need(v, "m.oh1")
        V("m.cm", v.tensor_tensor(cm[:], oh[0][:], oh[1][:], ALU.add))
        need(v, "m.cm")
        V("m.hi", v.tensor_copy(self.comb[:, :, 0, :], cm[:]))
        need(v, "m.hi")
        V("m.lo", v.tensor_tensor(self.comb[:, :, 1, :], cm[:], self.comb[:, :, 0, :].bitcast(F32), ALU.subtract))

    def m_turn(self, q):
        pe, act, need = self.pe, self.act, self.s.need
        bk = self.bank[6 + q % 2]
        need(pe, "m.lo", f"m.ct{q % 2}")
        for i in range(G4):
            ins = pe.transpose(bk[0:2 * E1, i * P:(i + 1) * P],
                               self.comb[:, q * G4 + i, :, :].rearrange("p k e -> p (k e)").bitcast(F32),
                               self.c["ident"])
        self.M("m.ctT", ins)
        need(act, "m.ctT")
        self.S(f"m.ct{q % 2}", act.copy(self.combT[:, q * G4 * P:(q + 1) * G4 * P], bk[0:2 * E1, :]))

    def m_first_hidden(self):
        for j, blk in enumerate([MB] + list(range(MB))):
            self.m_gate_up(0, j, blk)
            yield TPE, 1.3
            self.m_hidden(0, j, blk)
            yield DVE, 0.6

    def m_first_weighted(self):
        self.m_turn(0)
        for blk in range(MB):
            k = (blk + 1) % 2
            self.m_spread(0, k, blk)
            self.m_weight(0, k, blk)
            for q in range(1 + 2 * blk, min(3 + 2 * blk, NT // G4)):
                self.m_turn(q)
        self.m_split(1, 1)

    def m_gate_up(self, i, j, blk):
        pe, s, bank, hs, k = self.pe, self.s, self.bank, self.hs3[i], j % 2
        s.need(pe, f"m.hl{i}", f"m.h{k}")
        for w, name in enumerate(("m.gate", f"m.gu{i}")):
            for n, (wp, xp) in enumerate(((0, 0), (0, 1), (1, 0))):
                ins = pe.matmul(bank[2 * k + w], self.Wgus[wp][:, w, blk * P:(blk + 1) * P], hs[:, xp, :],
                                start=(n == 0), stop=(n == 2))
            self.M(name, ins)
        s.mark("m.up", s.pe)

    def m_spread(self, gi, k, blk):
        self.s.need_apart(self.pe, f"m.hc{k}", "m.ct0", "m.ct1", "m.ex")
        self.M("m.ce", self.pe.matmul(self.bank[4 + k], self.ex[:, blk * P:(blk + 1) * P],
                                      self.combT[:, tokens(gi * G4, G4)], start=True, stop=True))

    def m_hidden(self, i, j, blk):
        v, act, s, bank, k = self.dve, self.act, self.s, self.bank, j % 2
        s.need(act, "m.gate", f"m.h{k}")
        self.S(f"m.sg{k}", act.activation(self.sg3[k][:], bank[2 * k], ACT.Silu))
        s.need(v, f"m.sg{k}", "m.up", f"m.down{i}")
        self.V(f"m.h{k}", v.tensor_tensor(self.hd3[i][:, blk, :], bank[2 * k + 1], self.sg3[k][:], ALU.mult))

    def m_weight(self, i, k, blk):
        v, s, hd = self.dve, self.s, self.hd3[i][:, blk, :]
        s.need(v, f"m.h{k}", "m.ce")
        self.V(f"m.hc{k}", v.tensor_tensor(hd, self.bank[4 + k], hd, ALU.mult))
        s.mark(f"m.hd{i}", s.dve)

    def m_split(self, gi, i):
        v, s, act = self.dve, self.s, self.act
        sl = tokens(gi * G4, G4)
        s.need(act, f"m.gu{i}")
        self.S("m.hh", act.copy(self.hs3[i][:, 0, :], self.h3T[:, sl]))
        s.need(v, "m.hh")
        self.V(f"m.hl{i}", v.tensor_tensor(self.hs3[i][:, 1, :], self.h3T[:, sl],
                                           self.hs3[i][:, 0, :].bitcast(F32), ALU.subtract))

    def m_experts(self, gi, i, before, after):
        for j, blk in enumerate([MB] + list(range(MB))):
            k = j % 2
            self.m_gate_up(i, j, blk)
            if blk < MB:
                self.m_spread(gi, k, blk)
            self.m_hidden(i, j, blk)
            if blk < MB:
                self.m_weight(i, k, blk)
            if j == 1 and before is not None:
                self.m_down(before, 1 - i)
            if j == 2 and after is not None:
                self.m_split(after, 1 - i)

    def m_down(self, gi, i):
        v, s, pe, bank = self.dve, self.s, self.pe, self.bank
        need, V, M = s.need, self.V, self.M
        b, n0 = gi // (TB // G4), gi * G4
        need(pe, f"m.hd{i}", "m.y", "m.ct0")
        for t in range(G4):
            for blk in range(MB + 1):
                ins = pe.matmul(bank[6][:, t * P:(t + 1) * P], self.hd3[i][:, blk, t * P:(t + 1) * P],
                                self.Wd[:, blk, :], start=(blk == 0), stop=(blk == MB))
        M(f"m.down{i}", ins)
        need(v, f"m.down{i}", "m.x")
        V("m.y", v.tensor_tensor(self.yo[:], bank[6].rearrange("p (n d) -> p n d", d=D),
                                 rows(self.mB[1][:, b, 5, :], G4), ALU.mult))
        need(v, "m.y")
        x = self.X[:, bass.ds(n0, G4), :]
        V("m.x", v.tensor_tensor(x, x, self.yo[:], ALU.add))
        need(self.sp, "m.x")
        self.sp.dma_start(self.io["out"].rearrange("b (c p) d -> p (b c) d", p=P)[:, bass.ds(n0, G4), :],
                          x).then_inc(self.stored, 16)

    def build(self):
        self.setup()
        self.layer0_attention()
        self.l0_weights()
        self.l0_experts()
        self.end_phase()
        self.l1_attention()
        self.l1_moe()


def build(nc, io):
    with ExitStack() as ctx:
        Kernel(nc, ctx, io).build()


def at1(ap, b):
    return ap[:, bass.ds(b, 1)]


def tokens(n0, count):
    return bass.ds(n0 * P, count * P)


CONSTS = [("ident", P), ("headmask", P), ("upto", P), ("ones", P), ("pos", TB), ("iota8", E0), ("iota16", E1),
          ("cos1", NT), ("sin1", NT), ("keep", NT), ("cosmask", P), ("quarter", 1)]
COLS = [("cT", 2 * B), ("bq", 1), ("bu", 1), ("lnw", 1), ("lnb", 1), ("bq1", NH // 2)]
EARLY_ROWS = 4
ROWS = [("theta", D), ("bkv", 2 * D), ("bout", D), ("bg", E0), ("bk1", HD), ("bv1", HD), ("bo1", D)]


def layout(i):
    f = {k: np.asarray(a) for k, a in i.items()}
    j = np.arange(P)
    angle = np.float32(np.pi / (2.0 * T)) * np.arange(T, dtype=np.float32)
    cs, sn = np.cos(angle).astype(np.float32), np.sin(angle).astype(np.float32)
    consts = np.concatenate([
        np.eye(P), (j[:, None] // 8 == j[None, :] // 8), (j[:, None] <= j[None, :]), np.ones((P, P)),
        j[:, None] + P * np.arange(TB)[None, :],
        np.broadcast_to(np.arange(E0)[None, :], (P, E0)), np.broadcast_to(np.arange(E1)[None, :], (P, E1)),
        np.tile(cs.reshape(TB, P).T, (1, B)), np.tile(sn.reshape(TB, P).T, (1, B)),
        np.broadcast_to((np.arange(NT) % TB != 0)[None, :], (P, NT)),
        np.where(j[:, None] <= j[None, :], np.cos(np.pi / (2.0 * T) * (j[None, :] - j[:, None])), 0.0),
        np.full((P, 1), np.pi / 2),
    ], axis=1).astype(np.float32)
    bqkvu = f["L0_attn_bqkvu"]
    cols = np.concatenate([
        f["L0_c"].T, f["L1_c"].T, bqkvu[0:D, None], bqkvu[3 * D:, None], f["L0_attn_ln_w"][:, None],
        f["L0_attn_ln_b"][:, None], f["L1_attn_bq"].reshape(NH // 2, P).T,
    ], axis=1)
    rws = np.concatenate([f["L0_attn_theta"].reshape(-1), bqkvu[D:3 * D], f["L0_attn_bout"], f["L0_ffn_bg"],
                          f["L1_attn_bk"], f["L1_attn_bv"], f["L1_attn_bo"]])[None, :]
    return {
        "x": f["L0_attn_x"], "cols": cols, "consts": consts, "rows": rws,
        "wmod0": f["L0_wmod"], "wmod1": f["L1_wmod"], "w0": f["L0_attn_Wqkvu"].T, "wo0": f["L0_attn_Wout"].T,
        "csq": np.concatenate([np.where(np.arange(T) < P, 0, w) for w in (cs, sn)])[None, :].astype(np.float32),
        "wq1": f["L1_attn_Wq"], 
        "wkv1": np.concatenate([f["L1_attn_Wk"].reshape(D, NG, HG * DH), f["L1_attn_Wv"].reshape(D, NG, HG * DH)],
                               axis=2),
        "wo1": f["L1_attn_Wo"],
        "wgu": np.stack([np.concatenate([f[f"L1_ffn_w{k}_r"].transpose(1, 0, 2).reshape(D, E1 * MR),
                                         f[f"L1_ffn_w{k}_s"].transpose(1, 0, 2).reshape(D, NS * MS)], axis=1)
                         for k in "gu"], axis=1),
        "wd": np.concatenate([f["L1_ffn_wd_r"].reshape(E1 * MR, D), f["L1_ffn_wd_s"].reshape(NS * MS, D)]),
        "wr": f["L1_ffn_router_w"],
        "expand": (np.arange(2 * E1)[:, None] % E1 == np.arange(E1 * MR)[None, :] // MR).astype(np.float32),
        "wg0": f["L0_ffn_Wg"], "w1": f["L0_ffn_W1"], "w2": f["L0_ffn_W2"], "w3": f["L0_ffn_W3"],
    }


def kernel(**inputs):
    import concourse.bacc as bacc
    from concourse.bass_utils import run_bass_kernel_spmd

    nc = bacc.Bacc("TRN2", target_bir_lowering=False, num_devices=1)
    arrays, io = {}, {}
    for name, a in layout(inputs).items():
        arrays[f"in_{name}"] = np.ascontiguousarray(a)
        io[name] = nc.dram_tensor(f"in_{name}", a.shape, mybir.dt.from_np(a.dtype), kind="ExternalInput").ap()
    io["out"] = nc.dram_tensor("out", (B, T, D), F32, kind="ExternalOutput").ap()
    build(nc, io)
    r = run_bass_kernel_spmd(nc, [arrays], core_ids=[0])
    return r.results[0]["out"]
```
